# Optimizing a Trainium2 kernel written in Bass

```python
import numpy as np
import jax
import jax.numpy as jnp

def _softmax(x, axis=-1):
    return jax.nn.softmax(x, axis=axis)

def _gelu(x):
    return jax.nn.gelu(x, approximate=True)

def _silu(x):
    return jax.nn.silu(x)

def _sigmoid(x):
    return jax.nn.sigmoid(x)

def _layernorm(x, axis=-1, eps=1e-05):
    m = jnp.mean(x, axis=axis, keepdims=True)
    v = jnp.var(x, axis=axis, keepdims=True)
    return (x - m) / jnp.sqrt(v + eps)

def _scatter_add(tgt, idx, src, axis=0):
    return tgt.at[idx].add(src)

def _segment_sum(src, seg, n):
    return jax.ops.segment_sum(src, seg, n)
kernel_name = 'mk_macaron_d2_jaxref_r8_78617c'

def setup_inputs(seed: int=0):
    np.random.seed(seed)
    _w = jnp.asarray

    def _L0_attn_setup():
        import jax, jax.numpy as jnp
        import numpy as np
        D_MODEL = 128
        NHEAD = 16
        HEAD_DIM = D_MODEL // NHEAD
        MAX_POS = 256

        def _rope_tables(seq_len, dim):
            inv_freq = 1.0 / 10000.0 ** (jnp.arange(0, dim, 2, dtype=jnp.float32) / dim)
            t = jnp.arange(seq_len, dtype=jnp.float32)[:, None]
            freqs = t * inv_freq[None, :]
            emb = jnp.concatenate([freqs, freqs], axis=-1)
            return (jnp.cos(emb), jnp.sin(emb))

        def _rotate_half(x):
            x1, x2 = jnp.split(x, 2, axis=-1)
            return jnp.concatenate([-x2, x1], axis=-1)

        def _apply_rope(x, cos, sin):
            c = cos[None, :, None, :]
            s = sin[None, :, None, :]
            return x * c + _rotate_half(x) * s
        key = jax.random.key(seed)
        ks = jax.random.split(key, 9)
        B, L, D = (4, 256, D_MODEL)
        lim = 1.0 / np.sqrt(D)

        def lin(k):
            kw, kb = jax.random.split(k)
            W = jax.random.uniform(kw, (D, D), jnp.float32, -lim, lim)
            b = jax.random.uniform(kb, (D,), jnp.float32, -lim, lim)
            return (W, b)
        Wq, bq = lin(ks[0])
        Wk, bk = lin(ks[1])
        Wv, bv = lin(ks[2])
        Wo, bo = lin(ks[3])
        x = jax.random.normal(ks[4], (B, L, D), jnp.float32)
        return {'x': x, 'Wq': Wq, 'bq': bq, 'Wk': Wk, 'bk': bk, 'Wv': Wv, 'bv': bv, 'Wo': Wo, 'bo': bo}
    _L0_attn_in = _L0_attn_setup()

    def _L0_ffn_setup():
        import jax, jax.numpy as jnp
        import numpy as np
        E = 8
        K = 2
        D = 128
        P = 512
        key = jax.random.key(seed)
        ks = jax.random.split(key, 8)
        s = lambda fan_in: 1.0 / np.sqrt(fan_in)
        x = jax.random.normal(ks[0], (2, 256, D), dtype=jnp.float32)
        W1 = jax.random.normal(ks[1], (E, D, P), dtype=jnp.float32) * s(D)
        b1 = jax.random.normal(ks[2], (E, P), dtype=jnp.float32) * 0.01
        W2 = jax.random.normal(ks[3], (E, P, D), dtype=jnp.float32) * s(P)
        b2 = jax.random.normal(ks[4], (E, D), dtype=jnp.float32) * 0.01
        Wr = jax.random.normal(ks[5], (D, E), dtype=jnp.float32) * s(D)
        br = jax.random.normal(ks[6], (E,), dtype=jnp.float32) * 0.01
        return {'x': x, 'W1': W1, 'b1': b1, 'W2': W2, 'b2': b2, 'Wr': Wr, 'br': br}
    _L0_ffn_in = _L0_ffn_setup()

    def _L1_attn_setup():
        import jax, jax.numpy as jnp
        import numpy as np
        B, N, D = (2, 1024, 128)
        H = 16
        HD = D // H
        EPS = 1e-06

        def _feature_map(a):
            return jax.nn.elu(a) + 1.0
        key = jax.random.key(seed)
        ks = jax.random.split(key, 5)
        scale = 1.0 / np.sqrt(D)
        return {'x': jax.random.normal(ks[0], (B, N, D), dtype=jnp.float32), 'Wq': jax.random.normal(ks[1], (D, D), dtype=jnp.float32) * scale, 'Wk': jax.random.normal(ks[2], (D, D), dtype=jnp.float32) * scale, 'Wv': jax.random.normal(ks[3], (D, D), dtype=jnp.float32) * scale, 'Wo': jax.random.normal(ks[4], (D, D), dtype=jnp.float32) * scale}
    _L1_attn_in = _L1_attn_setup()

    def _L1_ffn_setup():
        import math
        import jax, jax.numpy as jnp
        import numpy as np
        NUM_EXPERTS = 16
        TOP_K = 2
        CAPACITY_FACTOR = 1.25
        key = jax.random.key(seed)
        k1, k2, k3, k4 = jax.random.split(key, 4)
        d, dff, E = (128, 512, NUM_EXPERTS)
        x = jax.random.normal(k1, (4, 256, d), dtype=jnp.float32)
        router_w = jax.random.normal(k2, (E, d), dtype=jnp.float32) * d ** (-0.5)
        router_b = jnp.zeros((E,), dtype=jnp.float32)
        w1 = jax.random.normal(k3, (E, d, dff), dtype=jnp.float32) * 0.02
        b1 = jnp.zeros((E, dff), dtype=jnp.float32)
        w2 = jax.random.normal(k4, (E, dff, d), dtype=jnp.float32) * 0.02
        b2 = jnp.zeros((E, d), dtype=jnp.float32)
        return {'x': x, 'router_w': router_w, 'router_b': router_b, 'w1': w1, 'b1': b1, 'w2': w2, 'b2': b2}
    _L1_ffn_in = _L1_ffn_setup()
    _d = {'L0_attn_x': _L0_attn_in['x'], 'L0_attn_Wq': _L0_attn_in['Wq'], 'L0_attn_bq': _L0_attn_in['bq'], 'L0_attn_Wk': _L0_attn_in['Wk'], 'L0_attn_bk': _L0_attn_in['bk'], 'L0_attn_Wv': _L0_attn_in['Wv'], 'L0_attn_bv': _L0_attn_in['bv'], 'L0_attn_Wo': _L0_attn_in['Wo'], 'L0_attn_bo': _L0_attn_in['bo'], 'L0_ffn_W1': _L0_ffn_in['W1'], 'L0_ffn_b1': _L0_ffn_in['b1'], 'L0_ffn_W2': _L0_ffn_in['W2'], 'L0_ffn_b2': _L0_ffn_in['b2'], 'L0_ffn_Wr': _L0_ffn_in['Wr'], 'L0_ffn_br': _L0_ffn_in['br'], 'L1_attn_Wq': _L1_attn_in['Wq'], 'L1_attn_Wk': _L1_attn_in['Wk'], 'L1_attn_Wv': _L1_attn_in['Wv'], 'L1_attn_Wo': _L1_attn_in['Wo'], 'L1_ffn_router_w': _L1_ffn_in['router_w'], 'L1_ffn_router_b': _L1_ffn_in['router_b'], 'L1_ffn_w1': _L1_ffn_in['w1'], 'L1_ffn_b1': _L1_ffn_in['b1'], 'L1_ffn_w2': _L1_ffn_in['w2'], 'L1_ffn_b2': _L1_ffn_in['b2']}
    _x0 = _d['L0_attn_x']
    _d['L0_attn_x'] = jax.random.normal(jax.random.fold_in(jax.random.key(seed), 1), (8, 512, 128), dtype=_x0.dtype)
    del _x0
    return _d

def reference(L0_attn_x, L0_attn_Wq, L0_attn_bq, L0_attn_Wk, L0_attn_bk, L0_attn_Wv, L0_attn_bv, L0_attn_Wo, L0_attn_bo, L0_ffn_W1, L0_ffn_b1, L0_ffn_W2, L0_ffn_b2, L0_ffn_Wr, L0_ffn_br, L1_attn_Wq, L1_attn_Wk, L1_attn_Wv, L1_attn_Wo, L1_ffn_router_w, L1_ffn_router_b, L1_ffn_w1, L1_ffn_b1, L1_ffn_w2, L1_ffn_b2):

    def _L0_attn_ref(x, Wq, bq, Wk, bk, Wv, bv, Wo, bo):
        import jax, jax.numpy as jnp
        import numpy as np
        D_MODEL = 128
        NHEAD = 16
        HEAD_DIM = D_MODEL // NHEAD
        MAX_POS = 256

        def _rope_tables(seq_len, dim):
            inv_freq = 1.0 / 10000.0 ** (jnp.arange(0, dim, 2, dtype=jnp.float32) / dim)
            t = jnp.arange(seq_len, dtype=jnp.float32)[:, None]
            freqs = t * inv_freq[None, :]
            emb = jnp.concatenate([freqs, freqs], axis=-1)
            return (jnp.cos(emb), jnp.sin(emb))

        def _rotate_half(x):
            x1, x2 = jnp.split(x, 2, axis=-1)
            return jnp.concatenate([-x2, x1], axis=-1)

        def _apply_rope(x, cos, sin):
            c = cos[None, :, None, :]
            s = sin[None, :, None, :]
            return x * c + _rotate_half(x) * s
        B, L, D = x.shape
        H, hd = (NHEAD, HEAD_DIM)
        q = (x @ Wq.T + bq).reshape(B, L, H, hd)
        k = (x @ Wk.T + bk).reshape(B, L, H, hd)
        v = (x @ Wv.T + bv).reshape(B, L, H, hd)
        cos, sin = _rope_tables(L, hd)
        q = _apply_rope(q, cos, sin)
        k = _apply_rope(k, cos, sin)
        scores = jnp.einsum('bqhd,bkhd->bhqk', q, k) / np.sqrt(hd).astype(np.float32)
        attn = jax.nn.softmax(scores, axis=-1)
        out = jnp.einsum('bhqk,bkhd->bqhd', attn, v).reshape(B, L, D)
        return out @ Wo.T + bo

    def _L0_ffn_ref(x, W1, b1, W2, b2, Wr, br):
        import jax, jax.numpy as jnp
        import numpy as np
        E = 8
        K = 2
        D = 128
        P = 512
        B, S, _ = x.shape
        xf = x.reshape(B * S, D)
        scores = xf @ Wr + br
        _, top_idx = jax.lax.top_k(scores, K)
        mask = jax.nn.one_hot(top_idx, E, dtype=scores.dtype).sum(-2) > 0
        router_weights = jax.nn.softmax(jnp.where(mask, scores, -jnp.inf), axis=-1)
        h = jax.nn.gelu(jnp.einsum('td,edp->etp', xf, W1) + b1[:, None, :])
        y = jnp.einsum('etp,epd->etd', h, W2) + b2[:, None, :]
        out = jnp.einsum('te,etd->td', router_weights, y)
        return out.reshape(B, S, D)

    def _L1_attn_ref(x, Wq, Wk, Wv, Wo):
        import jax, jax.numpy as jnp
        import numpy as np
        B, N, D = (2, 1024, 128)
        H = 16
        HD = D // H
        EPS = 1e-06

        def _feature_map(a):
            return jax.nn.elu(a) + 1.0
        b, n, d = x.shape
        q = _feature_map((x @ Wq.T).reshape(b, n, H, HD))
        k = _feature_map((x @ Wk.T).reshape(b, n, H, HD))
        v = (x @ Wv.T).reshape(b, n, H, HD)
        kv = jnp.einsum('bnhd,bnhm->bhdm', k, v)
        k_sum = k.sum(axis=1)
        numerator = jnp.einsum('bnhd,bhdm->bnhm', q, kv)
        denominator = jnp.einsum('bnhd,bhd->bnh', q, k_sum)[..., None]
        out = numerator / (denominator + EPS)
        out = out.reshape(b, n, d)
        return out @ Wo.T

    def _L1_ffn_ref(x, router_w, router_b, w1, b1, w2, b2):
        import math
        import jax, jax.numpy as jnp
        import numpy as np
        NUM_EXPERTS = 16
        TOP_K = 2
        CAPACITY_FACTOR = 1.25
        E, k = (NUM_EXPERTS, TOP_K)
        B, S, d = x.shape
        tokens = B * S
        capacity = max(1, int(math.ceil(CAPACITY_FACTOR * tokens * k / E)))
        x2d = x.reshape(tokens, d)
        logits = x2d @ router_w.T + router_b
        vals, idx = jax.lax.top_k(logits, k)
        gates = jax.nn.softmax(vals, axis=-1)
        flat_e = idx.reshape(-1)
        oh = (flat_e[:, None] == jnp.arange(E)[None, :]).astype(jnp.int32)
        pos = jnp.take_along_axis(jnp.cumsum(oh, axis=0) - 1, flat_e[:, None], axis=1)[:, 0]
        kept = pos < capacity
        kept2 = kept.reshape(tokens, k)
        denom = jnp.sum(gates * kept2, axis=-1, keepdims=True)
        gates = jnp.where(kept2, gates / (denom + 1e-09), 0.0)
        slot = flat_e * capacity + pos
        slot_safe = jnp.where(kept, slot, E * capacity)
        x_rep = jnp.repeat(x2d, k, axis=0)
        buf = jnp.zeros((E * capacity + 1, d), x.dtype).at[slot_safe].set(x_rep)
        packed = buf[:E * capacity].reshape(E, capacity, d)
        h = jax.nn.gelu(jnp.einsum('ecd,edf->ecf', packed, w1) + b1[:, None, :], approximate=False)
        expert_out = jnp.einsum('ecf,efd->ecd', h, w2) + b2[:, None, :]
        eflat = expert_out.reshape(E * capacity, d)
        gathered = eflat[jnp.clip(slot, 0, E * capacity - 1)]
        w = (gates.reshape(-1) * kept.astype(x.dtype))[:, None]
        out = (gathered * w).reshape(tokens, k, d).sum(axis=1)
        return out.reshape(B, S, d)
    x = L0_attn_x
    x = x + 0.5 * _L0_ffn_ref(_layernorm(x, axis=-1), L0_ffn_W1, L0_ffn_b1, L0_ffn_W2, L0_ffn_b2, L0_ffn_Wr, L0_ffn_br)
    x = x + _L0_attn_ref(_layernorm(x, axis=-1), L0_attn_Wq, L0_attn_bq, L0_attn_Wk, L0_attn_bk, L0_attn_Wv, L0_attn_bv, L0_attn_Wo, L0_attn_bo)
    x = x + 0.5 * _L0_ffn_ref(_layernorm(x, axis=-1), L0_ffn_W1, L0_ffn_b1, L0_ffn_W2, L0_ffn_b2, L0_ffn_Wr, L0_ffn_br)
    x = x + 0.5 * _L1_ffn_ref(_layernorm(x, axis=-1), L1_ffn_router_w, L1_ffn_router_b, L1_ffn_w1, L1_ffn_b1, L1_ffn_w2, L1_ffn_b2)
    x = x + _L1_attn_ref(_layernorm(x, axis=-1), L1_attn_Wq, L1_attn_Wk, L1_attn_Wv, L1_attn_Wo)
    x = x + 0.5 * _L1_ffn_ref(_layernorm(x, axis=-1), L1_ffn_router_w, L1_ffn_router_b, L1_ffn_w1, L1_ffn_b1, L1_ffn_w2, L1_ffn_b2)
    return x

_drawn_inputs = setup_inputs


def setup_inputs(seed=0):
    import zlib

    import numpy as np

    out = dict(_drawn_inputs(seed))
    spreads = {'L1_ffn_router_b': (0.0, 0.325), 'L1_ffn_b1': (0.0, 0.464), 'L1_ffn_b2': (0.0, 0.1)}
    factors = {'L0_attn_Wq': 4.126,
     'L0_attn_bq': 8.0,
     'L0_attn_Wk': 4.085,
     'L0_attn_bk': 8.0,
     'L0_ffn_b1': 6.25,
     'L0_ffn_b2': 4.767,
     'L1_attn_Wq': 3.844}
    for name, (base, spread) in spreads.items():
        noise = np.random.default_rng([zlib.crc32(name.encode()), seed]).standard_normal(out[name].shape)
        drawn = base * np.exp(spread * noise) if base else spread * noise
        out[name] = jnp.asarray(drawn.astype(out[name].dtype))
    for name, factor in factors.items():
        out[name] = (out[name] * factor).astype(out[name].dtype)
    return out
```

```python
from contextlib import ExitStack

import concourse.bass as bass
import numpy as np
from concourse import mybir

ALU = mybir.AluOpType
ACT = mybir.ActivationFunctionType
F32 = mybir.dt.float32
BF16 = mybir.dt.bfloat16
I32 = mybir.dt.int32
U32 = mybir.dt.uint32
AX_X = mybir.AxisListType.X

P = 128
D = 128
BATCHES, SEQ = 8, 512
TOKENS = BATCHES * SEQ
NT = TOKENS // P
GT = SEQ // P
NG = NT // GT
HEADS = 16
HD = D // HEADS
DFF = 512
FC = DFF // P
LN_EPS = 1e-5

CAPACITY = -(-5 * TOKENS * 2 // (4 * 16))
E0, S0 = 8, 2
E1, S1 = 16, CAPACITY // P
MOE = [dict(E=E0, S=S0, tiles=TOKENS * 2 // (S0 * P) + E0 - 1), dict(E=E1, S=S1, tiles=E1)]
assert CAPACITY == S1 * P
SLOTS = max(m["tiles"] * m["S"] * P for m in MOE)
PAIRS = 2 * TOKENS
ROW = D + 1
TAG = 65536.0
NEG = -3.0e38
WROW = FC * P + FC * D + FC + D

FFN0, ATTN, FFN1, LINATTN = range(4)
SUBLAYERS = [FFN0, ATTN, FFN0, FFN1, LINATTN, FFN1]

PARTS = 3
QK_ROWS = PARTS * PARTS * HD
STACK = 96
M_ROW = QK_ROWS

RING = 4
PAIR = 2


def constant_layout():
    at, out = 0, {}
    for name, n in [("ident", P), ("before", P), ("ones", P), ("tokid", NT), ("eoff", NT * E1),
                    ("keep", E1 * NT), ("jtab", E0 * 16), ("tiletab", MOE[0]["tiles"] * E0),
                    ("trash", SLOTS // P), ("blockmask", D), ("headmask", HEADS),
                    ("rope_c", SEQ), ("rope_s", SEQ)]:
        out[name] = (at, n)
        at += n
    return out, at


def constants():
    lay, n = constant_layout()
    c = np.zeros((P, n), np.float32)

    def put(name, v):
        a, w = lay[name]
        c[:, a:a + w] = np.broadcast_to(v, (P, w))

    p = np.arange(P)
    put("ident", np.eye(P))
    put("before", p[:, None] < p[None, :])
    put("ones", 1.0)
    put("tokid", np.arange(NT)[None, :] * P + p[:, None])
    put("eoff", np.tile(np.arange(E1) - 64.0, NT)[None, :])
    put("keep", np.tile(np.arange(NT) != 0, E1)[None, :])
    put("jtab", np.tile(np.arange(16) * S0 * P, E0)[None, :])
    put("tiletab", np.repeat(np.arange(MOE[0]["tiles"]), E0)[None, :])
    put("trash", PAIRS + np.arange(SLOTS // P)[None, :] * P + p[:, None])
    put("blockmask", (p[:, None] // HD) == (p[None, :] // HD))
    put("headmask", (p[:, None] // HD) == np.arange(HEADS)[None, :])
    inv = (1.0 / 10000.0 ** (np.arange(0, HD, 2) / HD)).astype(np.float32)
    ang = (np.arange(SEQ, dtype=np.float32)[:, None] * inv[None, :]).astype(np.float32).astype(np.float64)
    dim = p % HD
    ang = ang[:, dim % (HD // 2)].T
    put("rope_c", np.cos(ang))
    put("rope_s", np.sin(ang) * np.where(dim < HD // 2, -1.0, 1.0)[:, None])
    return c


WEIGHTS = [("wq", D), ("wqr", D), ("wk", D), ("wkr", D), ("wv", D), ("wo", D),
           ("lq", D), ("lkv", 2 * D), ("lo", D), ("r0", E0), ("r1", E1),
           ("bq", 1), ("bqr", 1), ("bk", 1), ("bkr", 1), ("bv", D), ("bo", D),
           ("rb0", GT * E0), ("rb1", GT * E1)]


def weight_layout():
    at, out = 0, {}
    for name, n in WEIGHTS:
        out[name] = (at, n)
        at += n
    return out, at


def build(nc, x_in, cst_in, w_in, ex0_in, ex1_in, out):
    CL, CN = constant_layout()
    WL, WN = weight_layout()
    ex_in = [ex0_in, ex1_in]

    ctx = ExitStack()
    with ctx:
        def sb(name, shape, dt=F32):
            return ctx.enter_context(nc.sbuf_tensor(name, shape, dt))

        def sem(name):
            return ctx.enter_context(nc.semaphore(name))

        X = sb("X", [P, NT, D])
        CST = sb("CST", [P, CN])
        WT = sb("WT", [P, WN])
        BST = sb("BST", [P, NT, 6])
        LN = sb("LN", [P, 12, NT])
        MEAN, RSTD = LN[:, 0, :], LN[:, 1, :]
        XS = sb("XS", [P, 2, GT, D])
        XT = sb("XT", [P, 2, SEQ])
        PS = ctx.enter_context(nc.psum_tensor("PS", [P, 8 * 512], F32))

        def bank(n, a=0, b=512):
            return PS[:, 512 * n + a:512 * n + b]

        def cst(name):
            a, n = CL[name]
            return CST[:, a:a + n]

        def wt(name):
            a, n = WL[name]
            return WT[:, a:a + n]

        ident = cst("ident")

        ARENA = 162 * 256
        arena = sb("arena", [P, ARENA])

        class Carver:
            def __init__(self):
                self.at = 0

            def __call__(self, shape, dt=F32, rows=P):
                n = int(np.prod(shape)) * (2 if dt == BF16 else 4)
                assert n % 4 == 0
                n //= 4
                assert self.at + n <= ARENA, (self.at, n)
                v = arena[0:rows, self.at:self.at + n]
                self.at += n
                if dt != F32:
                    v = v.bitcast(dt)
                names = "abcde"[:len(shape)]
                if len(shape) > 1:
                    v = v.rearrange(f"p ({' '.join(names)}) -> p {' '.join(names)}",
                                    **{k: s for k, s in zip(names[:-1], shape[:-1])})
                return v

        cv = Carver()
        XR = cv([2, NT, ROW])
        LG = cv([NT, E1])
        RT = [cv([NT, E1]) for _ in range(6)]
        MB = cv([NT, E1], BF16)
        R1 = cv([20, NT])
        SLOT = cv([2, NT], U32)
        GATE = cv([2, NT])
        RE = cv([8, E0])
        ETF = cv([MOE[0]["tiles"]])
        ET = cv([MOE[0]["tiles"]], I32)
        TT = cv([MOE[0]["tiles"], E0])
        JT = cv([E0, 16])
        WE = cv([RING, WROW])
        XP = cv([RING, S1, ROW])
        XPT = cv([PAIR, S1 * P])
        HT = cv([PAIR, FC, S1 * P])
        YS = cv([RING, S1, D])
        IDF = cv([RING, 3, S1])
        ID = cv([RING, S1], U32)
        YC = cv([2, 2, GT, D])
        cv = Carver()
        QS = cv([2, HEADS, SEQ], BF16)
        KS = cv([2, HEADS, SEQ], BF16)
        PT = cv([2, 4, GT, SEQ])
        at_main = cv.at
        VA = cv([NT, HEADS, HD + 1])
        VB = cv([2, GT, HEADS, HD + 1])
        MX = cv([2, HEADS, GT])
        NMB = cv([4 * GT], BF16)
        NMF = cv([2, 4 * GT])
        NMT = cv([P], BF16)
        OT = cv([SEQ])
        RD = cv([GT, 4])
        AO = cv([GT, D])
        AT = cv([SEQ])
        cv.at = 0
        QF = cv([2, 2, SEQ])
        QT = cv([2, SEQ])
        QR = cv([2, 2, SEQ])
        QP = cv([2, PARTS, 2, SEQ], BF16)
        assert cv.at <= at_main
        cv = Carver()
        LQM = cv([2, SEQ])
        LQE = cv([2, SEQ])
        LQF = cv([2, SEQ])
        LKM = cv([2, GT, D])
        LKE = cv([2, GT, D])
        LKF = cv([2, GT, D])
        LV = cv([2, GT, D + 1])
        BD = cv([2, D + HEADS])
        LRD = cv([2, GT, HEADS])
        LDN = cv([2, GT, HEADS])
        LAO = cv([2, GT, D])
        LAT = cv([2, SEQ])
        cv = Carver()
        ZERO = cv([4 * ROW * 10])
        ones_bf = sb("ones_bf", [P, P], BF16)
        before_bf = sb("before_bf", [P, P], BF16)

        BUF = nc.dram_tensor("dispatched", (SLOTS + PAIRS, ROW), F32).ap()
        YK = nc.dram_tensor("expert_out", (PAIRS + SLOTS, D), F32).ap()
        QKD = nc.dram_tensor("qk_parts", (BATCHES, 2, PARTS, P, SEQ), BF16).ap()
        ZD = nc.dram_tensor("zero_rows", (2, 4 * SEQ), BF16).ap()

        s_x, s_cst, s_wt = sem("x_loaded"), sem("cst_loaded"), sem("weights_loaded")
        s_zero, s_cleared = sem("zeros_made"), sem("scratch_cleared")
        s_dve, s_pool_chain = sem("dve_step"), sem("pool_step")
        s_var, s_sd = sem("variance_ready"), sem("deviation_ready")
        s_xs, s_tr, s_xt = sem("xs_ready"), sem("xs_transposed"), sem("xt_ready")
        s_row0, s_row1 = sem("rows0_copied"), sem("rows1_copied")
        s_lg, s_lgc = sem("logits_done"), sem("logits_copied")
        s_gap, s_ex = sem("score_gap_ready"), sem("gap_exp_ready")
        s_mask, s_rank = sem("chosen_ready"), sem("ranks_done")
        s_slot, s_disp = sem("slots_ready"), sem("rows_dispatched")
        s_xp = [sem(f"tile_rows_in{r}") for r in range(RING)]
        s_we = [sem(f"expert_in{r}") for r in range(RING)]
        s_xpt, s_xpc = sem("tile_transposed"), sem("tile_copied")
        s_h, s_g = sem("hidden_done"), sem("gelu_done")
        s_y, s_yc = sem("y_done"), sem("y_copied")
        s_yo = [sem(f"y_scattered{r}") for r in range(RING)]
        s_yin = [sem(f"y_gathered{u}") for u in range(2)]
        s_comb = sem("group_combined")
        s_final, s_out = sem("x_final"), sem("out_stored")
        s_proj, s_rope, s_rot = sem("projected"), sem("rope_read"), sem("qk_roped")
        s_hi, s_r1, s_mid, s_lo = sem("hi_part"), sem("rest1"), sem("mid_part"), sem("lo_part")
        s_qd = [sem(f"qk_parts_stored{u}") for u in range(2)]
        s_va, s_fill = sem("v_copied"), sem("stack_filled")
        s_vb = sem("v_batch_copied")
        s_st = [[sem(f"stack_in{u}{g}") for g in range(4)] for u in range(2)]
        s_nmi = [sem(f"max_rows_in{g}") for g in range(4)]
        s_e, s_exp = sem("scores_done"), sem("exp_done")
        s_m, s_mr = sem("max_scores_done"), sem("max_done")
        s_nmf, s_nmp, s_nmt = sem("negmax_ready"), sem("negmax_transposed"), sem("negmax_copied")
        s_av, s_ot = sem("av_done"), sem("av_copied")
        s_tp, s_td = sem("av_transposed"), sem("av_normalised")
        s_ap, s_at, s_op, s_od = sem("ao_transposed"), sem("at_copied"), sem("wo_done"), sem("residual_done")
        s_lq, s_lqm, s_lqe, s_lqf = sem("lin_q_done"), sem("lin_q_min"), sem("lin_q_exp"), sem("lin_q_ready")
        s_lk, s_lkm, s_lke, s_lkf = sem("lin_kv_done"), sem("lin_k_min"), sem("lin_k_exp"), sem("lin_k_ready")
        s_lv, s_kv, s_bd = sem("lin_v_ready"), sem("kv_done"), sem("kv_masked")
        s_ln, s_lao, s_la, s_lat = sem("lin_num_done"), sem("lin_out_ready"), sem("lin_out_t"), sem("lin_at_copied")
        s_lo2, s_lres = sem("lin_wo_done"), sem("lin_residual_done")

        block = ctx.enter_context(nc.Block())

        def ffn_of(L):
            return sum(k in (FFN0, FFN1) for k in SUBLAYERS[:L])

        FFNS = [k for k in SUBLAYERS if k in (FFN0, FFN1)]

        def moe_of(f):
            return MOE[0 if FFNS[f] == FFN0 else 1]

        TILES0 = [sum(moe_of(j)["tiles"] for j in range(f)) for f in range(len(FFNS) + 1)]

        def rounds(f, r):
            return len(range(r, moe_of(f)["tiles"], RING))

        def rounds0(f, r):
            return sum(rounds(j, r) for j in range(f))

        def scattered0(f, r):
            return sum(rounds(j, r) * moe_of(j)["S"] * 16 for j in range(f))

        class Chain:

            def __init__(self, eng, s):
                self.eng, self.s, self.n, self.base = eng, s, 0, 0

            def __call__(self, ins):
                ins.then_inc(self.s, 1)
                self.n += 1
                self.eng.wait_ge(self.s, self.base + self.n)

            def loop(self, i, k, first=0):
                self.start, self.k = self.n, k
                self.base, self.n = i * k + (self.start - first * k), 0

            def ended(self, count):
                assert self.n == self.k, (self.n, self.k)
                self.base, self.n = 0, self.start + count * self.k

        @block.sync
        def _(sp):
            sp.dma_start(X[:, :, :], x_in.rearrange("(t p) d -> p t d", p=P)).then_inc(s_x, 16)
            sp.dma_start(CST[:, :], cst_in).then_inc(s_cst, 16)
            sp.dma_start(WT[:, :], w_in).then_inc(s_wt, 16)
            sp.wait_ge(s_zero, 1)
            nclear = 0
            for a in range(0, SLOTS, P * 40):
                sp.dma_start(BUF[a:a + P * 40, :].rearrange("(p r) c -> p (r c)", p=P),
                             ZERO[:, :]).then_inc(s_cleared, 16)
                nclear += 1
            for a in range(0, PAIRS, P * 32):
                sp.dma_start(YK[a:a + P * 32, :].rearrange("(p r) c -> p (r c)", p=P),
                             ZERO[:, 0:32 * D]).then_inc(s_cleared, 16)
                nclear += 1
            sp.dma_start(ZD.rearrange("a b -> (a b)").rearrange("(a b) -> a b", a=8),
                         ZERO[0:8, 0:256].bitcast(BF16)).then_inc(s_cleared, 16)
            nclear += 1
            assert nclear * 16 == CLEARED

            def moe(L):
                f = ffn_of(L)
                m, T0 = moe_of(f), TILES0[ffn_of(L)]
                S, tiles, ex = m["S"], m["tiles"], ex_in[SUBLAYERS[L] == FFN1]
                sp.wait_ge(s_disp, 16 * 2 * NT * (f + 1))
                if S == S0:
                    sp.wait_ge(s_slot, 2 * f + 1)

                def load(i, c):
                    tau, r = i * RING + c, c % RING
                    if not (isinstance(i, int) and i == 0 and c < RING):
                        sp.wait_ge(s_yc, T0 + tau - (RING - 1))
                    sp.dma_start(XP[:, r, 0:S, :], BUF[bass.ds(tau * (S * P), S * P), :]
                                 .rearrange("(j p) c -> p j c", p=P)).then_inc(s_xp[r], 16)
                    if S == S0:
                        e = sp.value_load(ET[0:1, bass.ds(tau, 1)], min_val=0, max_val=E0 - 1)
                    else:
                        e = tau
                    sp.dma_start(WE[:, r, :], ex[bass.ds(e, 1)].rearrange("o p n -> p (o n)"))\
                      .then_inc(s_we[r], 16)

                for c in range(RING):
                    load(0, c)
                whole = tiles // RING - 1
                with sp.Fori(0, whole) as i:
                    for c in range(RING):
                        load(i, RING + c)
                for c in range(RING * (whole + 1), tiles):
                    load(0, c)
                for r in range(RING):
                    sp.wait_ge(s_yo[r], scattered0(f + 1, r))
                src = YK[0:PAIRS, :].rearrange("(k t p) c -> p k t c", k=2, p=P)

                def fetch(i, u):
                    if not (isinstance(i, int) and i == 0):
                        sp.wait_ge(s_comb, i * 2 + (f * NG + u - 1))
                    for k in range(2):
                        sp.dma_start(YC[:, u, k], src[:, k, bass.ds(i * (2 * GT) + u * GT, GT), :])\
                          .then_inc(s_yin[u], 16)

                fetch(0, 0)
                fetch(0, 1)
                with sp.Fori(1, NG // 2) as i:
                    fetch(i, 0)
                    fetch(i, 1)

            def attention(L):
                with sp.Fori(0, NG // 2) as i:
                    for u in range(2):
                        sp.wait_ge(s_lo, i * 2 + u + 1)
                        for w in range(2):
                            sp.dma_start(QKD[bass.ds(i * 2 + u, 1), w].rearrange("o a r t -> r (o a) t"),
                                         QP[:, u, :, w, :]).then_inc(s_qd[u], 16)
                sp.wait_ge(s_qd[0], 32 * NG // 2)
                sp.wait_ge(s_qd[1], 32 * NG // 2)

                def load(b, par, g):
                    hs = slice(4 * g, 4 * g + 4)
                    for a in range(PARTS):
                        src = QKD[bass.ds(b, 1)].rearrange("o w a (h d) t -> (o w) a d h t", d=HD)
                        for c in range(PARTS):
                            r = 24 * a + 8 * c
                            sp.dma_start(QS[r:r + 8, par, hs, :], src[0, a, :, hs, :])\
                              .then_inc(s_st[par][g], 16)
                            sp.dma_start(KS[r:r + 8, par, hs, :], src[1, c, :, hs, :])\
                              .then_inc(s_st[par][g], 16)
                    sp.dma_start(QS[M_ROW:M_ROW + 2, par, hs, :],
                                 ZD.rearrange("a (h t) -> a h t", h=4)).then_inc(s_st[par][g], 16)

                sp.wait_ge(s_fill, 2)
                for b in range(2):
                    for g in range(4):
                        load(b, b, g)

                def iteration(i, par, lo, hi):
                    for g in range(4):
                        gg = g - 1 if g else 3
                        has = (i >= 0 if g == 0 else i + 1 < NG) if lo else True
                        if has and not (lo and g == 0 and i >= NG):
                            bb = i if g == 0 else i + 1
                            pp = par if g == 0 else 1 - par
                            sp.wait_ge(s_nmt, bb * 4 + gg + 1)
                            for k in range(2):
                                sp.dma_start(
                                    QS[M_ROW + k:M_ROW + k + 1, pp, 4 * gg:4 * gg + 4, :]
                                    .rearrange("o h (a t) -> o (h a) t", t=P),
                                    NMT[16 * k:16 * k + 16, :]).then_inc(s_nmi[gg], 16)
                        if (not lo) or (0 <= i and i + 2 < NG):
                            sp.wait_ge(s_e, i * 32 + 8 * g + 8)
                            load(i + 2, par, g)

                iteration(-1, 1, True, True)
                iteration(0, 0, True, True)
                with sp.Fori(0, (LOOP_HI - 3) // 2) as i:
                    iteration(i * 2 + 1, 1, False, False)
                    iteration(i * 2 + 2, 0, False, False)
                for i in range(LOOP_HI - 2, NG + 1):
                    iteration(i, i % 2, True, True)

            for L, kind in enumerate(SUBLAYERS):
                if kind in (FFN0, FFN1):
                    moe(L)
                elif kind == ATTN:
                    attention(L)
            sp.wait_ge(s_final, NG)
            sp.dma_start(out.rearrange("(t p) d -> p t d", p=P), X[:, :, :]).then_inc(s_out, 16)
            sp.wait_ge(s_out, 16)

        @block.gpsimd
        def _(pool):
            nc.gpsimd.memset(ZERO[:, :], 0.0).then_inc(s_zero, 1)

            def moe(L):
                f = ffn_of(L)
                m, T0 = moe_of(f), TILES0[ffn_of(L)]
                S, tiles = m["S"], m["tiles"]
                if f == 0:
                    pool.wait_ge(s_cleared, CLEARED)
                with pool.Fori(0, NG // 2) as i:
                    for u in range(2):
                        pool.wait_ge(s_xs, i * 2 + (NG * L + u + 1))
                        pool.tensor_copy(XR[:, 1, bass.ds(i * 2 * GT + u * GT, GT), 0:D], XS[:, u])\
                            .then_inc(s_row1, 1)
                pool.wait_ge(s_row0, NG * (f + 1))
                pool.wait_ge(s_row1, NG * (f + 1))
                pool.wait_ge(s_slot, 2 * f + 2)
                for t in range(NT):
                    for k in range(2):
                        pool.indirect_dma_start(BUF, bass.IndirectOffsetOnAxis(ap=SLOT[:, k, t:t + 1], axis=0),
                                                XR[:, k, t, :], None).then_inc(s_disp, 16)

                def scatter(i, c):
                    tau, r = i * RING + c, c % RING
                    pool.wait_ge(s_yc, T0 + tau + 1)
                    pool.nop(nofuse=True)
                    for s in range(S):
                        pool.indirect_dma_start(YK, bass.IndirectOffsetOnAxis(ap=ID[:, r, s:s + 1], axis=0),
                                                YS[:, r, s, :], None).then_inc(s_yo[r], 16)

                whole = tiles // RING
                with pool.Fori(0, whole) as i:
                    for c in range(RING):
                        scatter(i, c)
                for c in range(RING * whole, tiles):
                    scatter(0, c)

            def attention(L):
                with pool.Fori(0, NG // 2) as i:
                    for u in range(2):
                        pool.wait_ge(s_hi, i * 2 + u + 1)
                        pool.tensor_tensor(QR[:, u], QF[:, u], QP[:, u, 0], ALU.subtract).then_inc(s_r1, 1)
                        pool.wait_ge(s_mid, i * 2 + u + 1)
                        pool.tensor_tensor(QP[:, u, 2], QR[:, u], QP[:, u, 1], ALU.subtract).then_inc(s_lo, 1)
                pool.wait_ge(s_qd[0], 32 * NG // 2)
                pool.wait_ge(s_qd[1], 32 * NG // 2)
                pool.memset(QS[64:STACK], 0.0).then_inc(s_fill, 1)
                pool.memset(KS[64:STACK], 1.0).then_inc(s_fill, 1)
                pool.wait_ge(s_fill, 2)

                def values(i, par, wait):
                    if wait:
                        pool.wait_ge(s_av, i * 4)
                    pool.tensor_copy(VB[:, 1 - par], VA[:, bass.ds(i * GT + GT, GT)]).then_inc(s_vb, 1)

                pool.wait_ge(s_va, NG)
                values(-1, 1, False)
                values(0, 0, False)
                with pool.Fori(0, (LOOP_HI - 1) // 2) as i:
                    values(i * 2 + 1, 1, True)
                    values(i * 2 + 2, 0, True)

            for L, kind in enumerate(SUBLAYERS):
                if kind in (FFN0, FFN1):
                    moe(L)
                elif kind == ATTN:
                    attention(L)

        @block.scalar
        def _(act):
            def deviation(L):
                act.wait_ge(s_var, L + 1)
                act.activation(LN[:, 7, :], LN[:, 6, :], ACT.Sqrt).then_inc(s_sd, 1)

            def transposed_group(L, i, u):
                act.wait_ge(s_tr, i * 2 + (NG * L + u + 1))
                act.activation(XT[:, u, :], bank(u), ACT.Copy).then_inc(s_xt, 1)

            def moe(L):
                f = ffn_of(L)
                m, T0 = moe_of(f), TILES0[ffn_of(L)]
                S, tiles = m["S"], m["tiles"]
                func = ACT.Gelu_apprx_tanh if SUBLAYERS[L] == FFN0 else ACT.Gelu
                deviation(L)
                with act.Fori(0, NG // 2) as i:
                    for u in range(2):
                        transposed_group(L, i, u)
                        act.activation(XR[:, 0, bass.ds(i * 2 * GT + u * GT, GT), 0:D], XS[:, u], ACT.Copy)\
                           .then_inc(s_row0, 1)
                act.wait_ge(s_gap, f + 1)
                act.activation(R1[:, 5, :], R1[:, 4, :], ACT.Exp).then_inc(s_ex, 1)

                def gelus(i, c):
                    tau, r = i * RING + c, c % RING
                    for q in range(FC):
                        act.wait_ge(s_h, tau * FC + (T0 * FC + q + 1))
                        if q == 0 and not (isinstance(i, int) and i == 0 and c < PAIR):
                            act.wait_ge(s_y, T0 + tau - (PAIR - 1))
                        act.activation(HT[:, c % PAIR, q, 0:S * P], PS[:, 1024 * (q % 2):1024 * (q % 2) + S * P],
                                       func, bias=WE[:, r, 2 * DFF + q:2 * DFF + q + 1]).then_inc(s_g, 1)

                for c in range(RING):
                    gelus(0, c)
                whole = tiles // RING - 1
                with act.Fori(0, whole) as i:
                    for c in range(RING):
                        gelus(i, RING + c)
                for c in range(RING * (whole + 1), tiles):
                    gelus(0, c)

            def attention(L):
                deviation(L)

                def split(i, u):
                    transposed_group(L, i, u)
                    act.wait_ge(s_rot, i * 2 + (u + 1))
                    if not (isinstance(i, int) and i == 0):
                        act.wait_ge(s_qd[u], i * 32)
                    act.activation(QP[:, u, 0], QF[:, u], ACT.Copy).then_inc(s_hi, 1)
                    act.wait_ge(s_r1, i * 2 + (u + 1))
                    act.activation(QP[:, u, 1], QR[:, u], ACT.Copy).then_inc(s_mid, 1)

                split(0, 0)
                split(0, 1)
                with act.Fori(1, NG // 2) as i:
                    split(i, 0)
                    split(i, 1)

                def iteration(i, par, peeled):
                    has_m = not peeled or i + 1 < NG
                    has_e = not peeled or 0 <= i < NG
                    for s in range(HEADS):
                        g, j = s // 4, s % 4
                        if has_e:
                            exp(i, par, s, 0)
                        if j == 0 and (not peeled or 0 <= 4 * i + g - 2 < 4 * NG):
                            G = i * 4 + (g - 2)
                            act.wait_ge(s_av, G + 1)
                            if not (peeled and 4 * i + g - 2 == 0):
                                act.wait_ge(s_tp, G)
                            act.activation(OT[:, :], bank(6), ACT.Copy).then_inc(s_ot, 1)
                        if j == 3:
                            b, gg = (i, 3) if g == 0 else (i + 1, g - 1)
                            if not peeled or (0 <= b < NG):
                                act.wait_ge(s_nmp, b * 4 + gg + 1)
                                if not (peeled and b == 0 and gg == 0):
                                    bb, g2 = (b, gg - 1) if gg else (b - 1, 3)
                                    act.wait_ge(s_nmi[g2], bb * 32 + 32)
                                act.activation(NMT[0:32, :], bank(7, 0, P)[0:32, :], ACT.Copy).then_inc(s_nmt, 1)
                        if s == 8 and (not peeled or 0 <= i - 1 < NG):
                            act.wait_ge(s_ap, i)
                            act.activation(AT[:, :], bank(7), ACT.Copy).then_inc(s_at, 1)
                        if has_e:
                            exp(i, par, s, 1)

                def exp(i, par, s, w):
                    g, j = s // 4, s % 4
                    act.wait_ge(s_e, i * 32 + (2 * s + w + 1))
                    if w == 0 and j == 0 and not (isinstance(i, int) and 4 * i + g < 2):
                        act.wait_ge(s_av, i * 4 + g - 1)
                    act.activation(PT[:, g % 2, j, 2 * w:2 * w + 2, :],
                                   PS[:, 1024 * w:1024 * w + 1024].rearrange("p (a b) -> p a b", a=2),
                                   ACT.Exp, scale=float(1.0 / np.sqrt(HD))).then_inc(s_exp, 1)

                iteration(-1, 1, True)
                iteration(0, 0, True)
                with act.Fori(0, (LOOP_HI - 1) // 2) as i:
                    iteration(i * 2 + 1, 1, False)
                    iteration(i * 2 + 2, 0, False)
                for i in range(LOOP_HI, NG + 1):
                    iteration(i, i % 2, True)

            def linear(L):
                deviation(L)

                def front(i, u):
                    transposed_group(L, i, u)
                    n = i * 2 + (u + 1)
                    act.wait_ge(s_lqm, n)
                    act.activation(LQE[:, u], LQM[:, u], ACT.Exp).then_inc(s_lqe, 1)
                    act.wait_ge(s_lk, n)
                    if not (isinstance(i, int) and i == 0):
                        act.wait_ge(s_kv, n - 2)
                    act.activation(LV[:, u, :, 0:D],
                                   PS[:, 1024:2048].rearrange("p (a b) -> p a b", a=GT)[:, :, D:2 * D],
                                   ACT.Copy).then_inc(s_lv, 1)
                    act.wait_ge(s_lkm, n)
                    act.activation(LKE[:, u], LKM[:, u], ACT.Exp).then_inc(s_lke, 1)

                def back(i, u):
                    n = i * 2 + (u + 1)
                    act.wait_ge(s_la, n)
                    act.activation(LAT[:, u], bank(7), ACT.Copy).then_inc(s_lat, 1)

                front(0, 0)
                front(0, 1)
                back(0, 0)
                with act.Fori(0, NG // 2 - 1) as i:
                    front(i + 1, 0)
                    back(i, 1)
                    front(i + 1, 1)
                    back(i + 1, 0)
                back(NG // 2 - 1, 1)

            for L, kind in enumerate(SUBLAYERS):
                if kind in (FFN0, FFN1):
                    moe(L)
                elif kind == ATTN:
                    attention(L)
                else:
                    linear(L)

        @block.tensor
        def _(pe):
            pe.wait_ge(s_cst, 16)
            pe.wait_ge(s_wt, 16)

            def transpose_group(L, i, u):
                pe.wait_ge(s_xs, i * 2 + (NG * L + u + 1))
                for j in range(GT):
                    mm = pe.transpose(bank(u, P * j, P * j + P), XS[:, u, j, :], ident)
                mm.then_inc(s_tr, 1)

            def moe(L):
                f = ffn_of(L)
                m, T0 = moe_of(f), TILES0[ffn_of(L)]
                E, S, tiles = m["E"], m["S"], m["tiles"]
                wr = wt("r0" if SUBLAYERS[L] == FFN0 else "r1")
                N = S * P

                def logits(i, u):
                    pe.wait_ge(s_xt, i * 2 + (NG * L + u + 1))
                    if not (isinstance(i, int) and i == 0):
                        pe.wait_ge(s_lgc, i * 2 + (NG * f + u - 1))
                    for j in range(GT):
                        mm = pe.matmul(bank(2 + u, E * j, E * j + E), XT[:, u, P * j:P * j + P], wr,
                                       start=True, stop=True)
                    mm.then_inc(s_lg, 1)

                def groups(i):
                    transpose_group(L, i + 1, 0)
                    logits(i, 1)
                    transpose_group(L, i + 1, 1)
                    logits(i + 1, 0)

                transpose_group(L, 0, 0)
                transpose_group(L, 0, 1)
                logits(0, 0)
                groups(0)
                with pe.Fori(1, NG // 2 - 1) as i:
                    groups(i)
                logits(NG // 2 - 1, 1)

                pe.wait_ge(s_mask, f + 1)
                Mv = MB.rearrange("p a b -> p (a b)")[:, 0:NT * E]
                pe.matmul(bank(4, 0, NT * E), before_bf[:, :], Mv, start=True, stop=True)
                pe.matmul(bank(5, 0, NT * E), ones_bf[:, :], Mv, start=True, stop=True).then_inc(s_rank, 1)
                pe.wait_ge(s_slot, 2 * f + 2)

                def turn(i, c):
                    tau, r = i * RING + c, c % RING
                    pe.wait_ge(s_xp[r], i * 16 + 16 * (rounds0(f, r) + c // RING + 1))
                    if not (isinstance(i, int) and i == 0 and c == 0):
                        pe.wait_ge(s_xpc, T0 + tau)
                    for s in range(S):
                        mm = pe.transpose(bank(4, P * s, P * s + P), XP[:, r, s, 0:D], ident)
                    mm.then_inc(s_xpt, 1)

                def hidden(i, c):
                    tau, r = i * RING + c, c % RING
                    pe.wait_ge(s_we[r], i * 16 + 16 * (rounds0(f, r) + c // RING + 1))
                    pe.wait_ge(s_xpc, T0 + tau + 1)
                    for q in range(FC):
                        if not (isinstance(i, int) and i == 0 and c == 0 and q < 2):
                            pe.wait_ge(s_g, tau * FC + (T0 * FC + q - 1))
                        for a in range(0, N, 512):
                            b = min(N, a + 512)
                            mm = pe.matmul(PS[:, 1024 * (q % 2) + a:1024 * (q % 2) + b],
                                           WE[:, r, q * P:q * P + P], XPT[:, c % PAIR, a:b], start=True, stop=True)
                        mm.then_inc(s_h, 1)

                def outputs(i, c):
                    tau, r = i * RING + c, c % RING
                    pe.wait_ge(s_g, tau * FC + (T0 * FC + FC))
                    if not (isinstance(i, int) and i == 0 and c == 0):
                        pe.wait_ge(s_yc, T0 + tau)
                    for s in range(S):
                        for q in range(FC):
                            mm = pe.matmul(PS[:, 3072 + P * s:3072 + P * s + P], HT[:, c % PAIR, q, P * s:P * s + P],
                                           WE[:, r, DFF + q * D:DFF + q * D + D], start=(q == 0), stop=(q == FC - 1))
                    mm.then_inc(s_y, 1)

                turn(0, 0)
                turn(0, 1)
                hidden(0, 0)
                whole = (tiles - 2) // RING

                def steps(i):
                    for c in range(1, RING + 1):
                        turn(i, c + 1)
                        hidden(i, c)
                        outputs(i, c - 1)

                steps(0)
                with pe.Fori(1, whole) as i:
                    steps(i)
                for c in range(RING * whole + 1, tiles + 1):
                    if c + 1 < tiles:
                        turn(0, c + 1)
                    if c < tiles:
                        hidden(0, c)
                    outputs(0, c - 1)

            def attention(L):
                def front(i, u):
                    pe.wait_ge(s_xt, i * 2 + (NG * L + u + 1))
                    first = isinstance(i, int) and i == 0 and u == 0
                    for n, w in enumerate(("wq", "wqr", "wk", "wkr")):
                        if not first:
                            pe.wait_ge(s_rope, i * 8 + (4 * u + n - 3))
                        pe.matmul(bank(2 + n), wt(w), XT[:, u, :], start=True, stop=True).then_inc(s_proj, 1)
                    if not first:
                        pe.wait_ge(s_va, i * 2 + u)
                    for j in range(GT):
                        mm = pe.matmul(bank(6, P * j, P * j + P), XT[:, u, P * j:P * j + P], wt("wv"),
                                       start=True, stop=True)
                    mm.then_inc(s_proj, 1)

                transpose_group(L, 0, 0)
                transpose_group(L, 0, 1)
                front(0, 0)
                with pe.Fori(0, NG // 2 - 1) as i:
                    transpose_group(L, i + 1, 0)
                    front(i, 1)
                    transpose_group(L, i + 1, 1)
                    front(i + 1, 0)
                front(NG // 2 - 1, 1)
                pe.wait_ge(s_va, NG + 1)

                def iteration(i, par, peeled):
                    has_m = not peeled or i + 1 < NG
                    has_e = not peeled or 0 <= i < NG
                    for s in range(HEADS):
                        g, j = s // 4, s % 4
                        if has_e and j == 0:
                            pe.wait_ge(s_nmi[g], i * 32 + 32)
                        if has_e:
                            scores(i, par, s, 0)
                        if has_m:
                            if j == 0:
                                pe.wait_ge(s_st[1 - par][g], half(i, 1, par) * LOADS)
                            maxima(i, par, s, 0)
                            maxima(i, par, s, 1)
                        if has_e:
                            scores(i, par, s, 1)
                        if has_m:
                            maxima(i, par, s, 2)
                            maxima(i, par, s, 3)
                        if not peeled or 0 <= 4 * i + g - 1 < 4 * NG:
                            weigh(i, par, g, j, peeled)
                        misc(i, par, s, peeled)

                def half(i, ahead, par):
                    if isinstance(i, int):
                        return (i + ahead) // 2 + 1
                    return HALF[0] + (1 if (par == 1 and ahead == 1) else 0)

                def scores(i, par, s, w):
                    if not (isinstance(i, int) and i == 0 and s == 0):
                        pe.wait_ge(s_exp, i * 32 + (2 * s + w - 1))
                    for k in range(2 * w, 2 * w + 2):
                        mm = pe.matmul(bank(k), KS[0:STACK, par, s, P * k:P * k + P], QS[0:STACK, par, s, :],
                                       start=True, stop=True)
                    mm.then_inc(s_e, 1)

                def maxima(i, par, s, a):
                    if not (isinstance(i, int) and i == -1 and s == 0 and a < 2):
                        pe.wait_ge(s_mr, i * 64 + (64 + 4 * s + a - 1))
                    pe.matmul(bank(4 + a % 2), QS[0:STACK, 1 - par, s, P * a:P * a + P], KS[0:STACK, 1 - par, s, :],
                              start=True, stop=True).then_inc(s_m, 1)

                def weigh(i, par, g, k, peeled):
                    gg = (g - 1) % 4
                    vpar = par if g else 1 - par
                    if k == 0:
                        pe.wait_ge(s_exp, i * 32 + 8 * g)
                        if not (peeled and 4 * i + g - 1 == 0):
                            pe.wait_ge(s_ot, i * 4 + g - 1)
                        if g == 1:
                            pe.wait_ge(s_vb, i + 1)
                    for j in range(4):
                        h = 4 * gg + j
                        mm = pe.matmul(bank(6)[32 * j:32 * j + HD + 1, :], VB[:, vpar, k, h, :],
                                       PT[:, gg % 2, j, k, :], start=(k == 0), stop=(k == GT - 1))
                    if k == GT - 1:
                        mm.then_inc(s_av, 1)

                def misc(i, par, s, peeled):
                    g, j = s // 4, s % 4

                    def earlier(what, n):
                        n_int = n if isinstance(n, int) else None
                        if n_int is None or n_int > 0:
                            pe.wait_ge(what, n)

                    def clamp(n, top):
                        return max(0, min(n, top)) if isinstance(n, int) else n

                    if j == 1:
                        if peeled and not 0 <= 4 * i + g - 2 < 4 * NG:
                            return
                        G = i * 4 + (g - 2)
                        earlier(s_nmt, clamp(i * 4 + g + 3, 4 * NG))
                        earlier(s_td, G)
                        if g == 2:
                            earlier(s_at, clamp(i, NG))
                        if g == 3:
                            earlier(s_od, clamp(i, NG))
                        pe.wait_ge(s_ot, G + 1)
                        for a in range(GT):
                            mm = pe.transpose(bank(7, P * a, P * a + P), OT[:, P * a:P * a + P], ident)
                        mm.then_inc(s_tp, 1)
                    if j == 2:
                        b, gg = (i, 3) if g == 0 else (i + 1, g - 1)
                        if peeled and not 0 <= b < NG:
                            return
                        earlier(s_td, clamp(i * 4 + (g - 1), 4 * NG))
                        earlier(s_nmt, b * 4 + gg)
                        pe.wait_ge(s_nmf, b * 4 + gg + 1)
                        pe.transpose(bank(7, 0, P)[0:32, :], NMF.rearrange("p a b -> p (a b)"), ident)\
                            .then_inc(s_nmp, 1)
                    if s in (7, 11) and (not peeled or 0 <= i - 1 < NG):
                        earlier(s_nmt, clamp(i * 4 + g + 4, 4 * NG))
                        earlier(s_td, clamp(i * 4 + (g - 1), 4 * NG))
                        if s == 7:
                            for a in range(GT):
                                mm = pe.transpose(bank(7, P * a, P * a + P), AO[:, a, :], ident)
                            mm.then_inc(s_ap, 1)
                        else:
                            pe.wait_ge(s_at, i)
                            for a in range(GT):
                                mm = pe.matmul(bank(7, P * a, P * a + P), AT[:, P * a:P * a + P], wt("wo"),
                                               start=True, stop=True)
                            mm.then_inc(s_op, 1)

                HALF = [0]
                iteration(-1, 1, True)
                iteration(0, 0, True)
                with pe.Fori(0, (LOOP_HI - 1) // 2) as i:
                    HALF[0] = i + 1
                    iteration(i * 2 + 1, 1, False)
                    HALF[0] = i + 2
                    iteration(i * 2 + 2, 0, False)
                for i in range(LOOP_HI, NG + 1):
                    iteration(i, i % 2, True)

            def linear(L):
                KVb = PS[:, 1024:2048].rearrange("p (a b) -> p a b", a=GT)

                def f1(i, u):
                    transpose_group(L, i, u)

                def f2(i, u):
                    n = i * 2 + (u + 1)
                    pe.wait_ge(s_xt, n + NG * L)
                    pe.matmul(bank(4), wt("lq"), XT[:, u, :], start=True, stop=True).then_inc(s_lq, 1)

                def f3(i, u):
                    n = i * 2 + (u + 1)
                    if not (isinstance(i, int) and i == 0 and u == 0):
                        pe.wait_ge(s_lv, n - 1)
                        pe.wait_ge(s_lkf, n - 1)
                    for j in range(GT):
                        mm = pe.matmul(KVb[:, j, :], XT[:, u, P * j:P * j + P], wt("lkv"), start=True, stop=True)
                    mm.then_inc(s_lk, 1)

                def b1(i, u):
                    n = i * 2 + (u + 1)
                    pe.wait_ge(s_lkf, n)
                    pe.wait_ge(s_lv, n)
                    pe.wait_ge(s_lqf, n)
                    for j in range(GT):
                        mm = pe.matmul(bank(4, 0, D + 1), LKF[:, u, j, :], LV[:, u, j, :],
                                       start=(j == 0), stop=(j == GT - 1))
                    mm.then_inc(s_kv, 1)

                def b2(i, u):
                    n = i * 2 + (u + 1)
                    pe.wait_ge(s_bd, n)
                    for j in range(GT):
                        mm = pe.matmul(PS[:, 2560 + 256 * j:2560 + 256 * j + D + HEADS],
                                       LQF[:, u, P * j:P * j + P], BD[:, u, :], start=True, stop=True)
                    mm.then_inc(s_ln, 1)

                def b3(i, u):
                    n = i * 2 + (u + 1)
                    pe.wait_ge(s_lao, n)
                    for j in range(GT):
                        mm = pe.transpose(bank(7, P * j, P * j + P), LAO[:, u, j, :], ident)
                    mm.then_inc(s_la, 1)

                def b4(i, u):
                    n = i * 2 + (u + 1)
                    pe.wait_ge(s_lat, n)
                    for j in range(GT):
                        mm = pe.matmul(bank(7, P * j, P * j + P), LAT[:, u, P * j:P * j + P], wt("lo"),
                                       start=True, stop=True)
                    mm.then_inc(s_lo2, 1)

                def both(i, u, i2, u2):
                    f1(i, u)
                    b1(i2, u2)
                    pe.wait_ge(s_bd, i2 * 2 + (u2 + 1))
                    f2(i, u)
                    b2(i2, u2)
                    f3(i, u)
                    if not (isinstance(i2, int) and i2 == 0 and u2 == 0):
                        pe.wait_ge(s_lres, i2 * 2 + u2)
                    b3(i2, u2)
                    b4(i2, u2)

                f1(0, 0)
                f2(0, 0)
                f3(0, 0)
                both(0, 1, 0, 0)
                with pe.Fori(0, NG // 2 - 1) as i:
                    both(i + 1, 0, i, 1)
                    both(i + 1, 1, i + 1, 0)
                i = NG // 2 - 1
                b1(i, 1)
                b2(i, 1)
                pe.wait_ge(s_lres, NG - 1)
                b3(i, 1)
                b4(i, 1)

            for L, kind in enumerate(SUBLAYERS):
                if kind in (FFN0, FFN1):
                    moe(L)
                elif kind == ATTN:
                    attention(L)
                else:
                    linear(L)

        @block.vector
        def _(dve):
            chain = Chain(dve, s_dve)

            def group_stats(t0):
                for j in range(GT):
                    ins = dve.bn_stats(BST[:, bass.ds(t0 + j, 1), :].rearrange("p a b -> p (a b)"),
                                       X[:, bass.ds(t0 + j, 1), :].rearrange("p a b -> p (a b)"))
                return ins

            def finish_stats(L):
                me, m2e, mo, m2o = BST[:, :, 1], BST[:, :, 2], BST[:, :, 4], BST[:, :, 5]
                a = [LN[:, k, :] for k in range(12)]
                dve.tensor_tensor(a[2], me, mo, ALU.add).then_inc(s_dve, 1)
                dve.tensor_tensor(a[3], me, mo, ALU.subtract).then_inc(s_dve, 1)
                dve.tensor_tensor(a[4], m2e, m2o, ALU.add).then_inc(s_dve, 1)
                chain.n += 3
                dve.wait_ge(s_dve, chain.n)
                chain(dve.tensor_scalar(a[0], a[2], 0.5, None, ALU.mult))
                chain(dve.tensor_tensor(a[5], a[3], a[3], ALU.mult))
                chain(dve.scalar_tensor_tensor(out=a[8], in0=a[5], scalar=D / 4.0, in1=a[4],
                                               op0=ALU.mult, op1=ALU.add))
                dve.tensor_scalar(a[6], a[8], 1.0 / D, LN_EPS, ALU.mult, ALU.add).then_inc(s_var, 1)
                dve.wait_ge(s_var, L + 1)
                dve.wait_ge(s_sd, L + 1)
                chain(dve.reciprocal(a[9], a[7]))
                chain(dve.tensor_tensor(a[10], a[9], a[9], ALU.mult))
                chain(dve.tensor_tensor(a[11], a[10], a[6], ALU.mult))
                chain(dve.tensor_scalar(a[10], a[11], -0.5, 1.5, ALU.mult, ALU.add))
                chain(dve.tensor_tensor(a[1], a[9], a[10], ALU.mult))

            def normalise(L, i, u, *waits):
                for s, n in waits:
                    dve.wait_ge(s, n)
                for j in range(GT):
                    t = i * (2 * GT) + (GT * u + j)
                    ins = dve.tensor_scalar(XS[:, u, j, :], X[:, bass.ds(t, 1), :].rearrange("p a b -> p (a b)"),
                                            MEAN[:, bass.ds(t, 1)], RSTD[:, bass.ds(t, 1)],
                                            ALU.subtract, ALU.mult)
                ins.then_inc(s_xs, 1)

            def moe(L):
                f = ffn_of(L)
                m, T0 = moe_of(f), TILES0[ffn_of(L)]
                E, S, tiles = m["E"], m["S"], m["tiles"]
                tag = TAG * (f + 1)
                rb = wt("rb0" if SUBLAYERS[L] == FFN0 else "rb1").rearrange("p (a b) -> p a b", a=GT)
                for k in range(2):
                    dve.tensor_scalar(XR[:, k, :, D], cst("tokid"), tag + k * TOKENS, None, ALU.add)\
                       .then_inc(s_dve, 1)
                    chain.n += 1

                def scores_in(i, u):
                    dve.wait_ge(s_lg, i * 2 + (NG * f + u + 1))
                    dve.tensor_tensor(LG[:, bass.ds(i * (2 * GT) + GT * u, GT), 0:E],
                                      bank(2 + u, 0, GT * E).rearrange("p (a b) -> p a b", a=GT), rb, ALU.add)\
                       .then_inc(s_lgc, 1)

                def norm(i, u):
                    if isinstance(i, int) and i == 0:
                        normalise(L, i, u)
                    else:
                        n = i * 2 + (u - 1)
                        normalise(L, i, u, (s_tr, n + NG * L), (s_row0, n + NG * f), (s_row1, n + NG * f))

                norm(0, 0)
                norm(0, 1)
                scores_in(0, 0)
                with dve.Fori(0, NG // 2 - 1) as i:
                    norm(i + 1, 0)
                    scores_in(i, 1)
                    norm(i + 1, 1)
                    scores_in(i + 1, 0)
                scores_in(NG // 2 - 1, 1)
                dve.wait_ge(s_lgc, NG * (f + 1))

                def bc(v):
                    return v.unsqueeze(2).to_broadcast((P, NT, E))

                lg = LG[:, :, 0:E]
                eoff = cst("eoff").rearrange("p (a b) -> p a b", a=NT)[:, :, 0:E]
                w = [RT[k][:, :, 0:E] for k in range(6)]
                r = [R1[:, k, :] for k in range(20)]
                oh = [w[0], w[1]]

                def best(k, scores, m_, i_):
                    chain(dve.tensor_reduce(m_, scores, AX_X, ALU.max))
                    chain(dve.tensor_tensor(w[2], scores, bc(m_), ALU.is_equal))
                    chain(dve.tensor_tensor(w[3], w[2], eoff, ALU.mult))
                    chain(dve.tensor_reduce(i_, w[3], AX_X, ALU.min))
                    chain(dve.tensor_tensor(oh[k], eoff, bc(i_), ALU.is_equal))

                best(0, lg, r[0], r[2])
                chain(dve.scalar_tensor_tensor(out=w[4], in0=oh[0], scalar=NEG, in1=lg,
                                               op0=ALU.mult, op1=ALU.add))
                best(1, w[4], r[1], r[3])
                Mv = MB.rearrange("p a b -> p (a b)")[:, 0:NT * E].rearrange("p (a b) -> p a b", a=NT)
                dve.tensor_tensor(Mv, oh[0], oh[1], ALU.add).then_inc(s_mask, 1)
                dve.tensor_tensor(r[4], r[1], r[0], ALU.subtract).then_inc(s_gap, 1)
                dve.wait_ge(s_ex, f + 1)
                chain(dve.tensor_scalar(r[6], r[5], 1.0, None, ALU.add))
                chain(dve.reciprocal(r[7], r[6]))
                chain(dve.tensor_tensor(r[8], r[5], r[7], ALU.mult))
                gates = [r[7], r[8]]

                dve.wait_ge(s_rank, f + 1)
                te = RT[2].rearrange("p a b -> p (a b)")[:, 0:E * NT]
                inc = RT[3].rearrange("p a b -> p (a b)")[:, 0:E * NT]
                exc = RT[4].rearrange("p a b -> p (a b)")[:, 0:E * NT]
                chain(dve.tensor_copy(te.rearrange("p (e t) -> p e t", e=E),
                                      bank(5, 0, NT * E).rearrange("p (t e) -> p e t", e=E)))
                chain(dve.tensor_tensor_scan(inc, cst("keep")[:, 0:E * NT], te, 0.0, ALU.mult, ALU.add))
                chain(dve.tensor_tensor(exc, inc, te, ALU.subtract))
                if E == E0:
                    n_e = inc.rearrange("p (e t) -> p e t", e=E)[:, :, NT - 1]
                    chain(dve.tensor_tensor(JT[:, :, :], n_e.unsqueeze(2).to_broadcast((P, E, 16)),
                                            cst("jtab").rearrange("p (a b) -> p a b", a=E), ALU.is_gt))
                    chain(dve.tensor_reduce(RE[:, 0, :], JT[:, :, :], AX_X, ALU.add))
                    chain(dve.tensor_tensor_scan(RE[:, 1, :], cst("ones")[:, 0:E], RE[:, 0, :], 0.0,
                                                 ALU.mult, ALU.add))
                    chain(dve.tensor_tensor(RE[:, 2, :], RE[:, 1, :], RE[:, 0, :], ALU.subtract))
                    chain(dve.tensor_scalar(RE[:, 3, :], RE[:, 2, :], float(S * P), None, ALU.mult))
                    chain(dve.tensor_tensor(exc.rearrange("p (e t) -> p e t", e=E),
                                            exc.rearrange("p (e t) -> p e t", e=E),
                                            RE[:, 3, :].unsqueeze(2).to_broadcast((P, E, NT)), ALU.add))
                    chain(dve.tensor_tensor(TT[:, :, :], cst("tiletab").rearrange("p (a b) -> p a b", b=E),
                                            RE[:, 1, :].unsqueeze(1).to_broadcast((P, tiles, E)), ALU.is_ge))
                    chain(dve.tensor_reduce(ETF[:, :], TT[:, :, :], AX_X, ALU.add))
                    dve.tensor_scalar(ET[:, :], ETF[:, :], float(E - 1), None, ALU.min).then_inc(s_slot, 1)
                else:
                    dve.tensor_copy(ET[:, 0:1], cst("ones")[:, 0:1]).then_inc(s_slot, 1)
                chain(dve.tensor_tensor(w[5], bank(4, 0, NT * E).rearrange("p (t e) -> p t e", e=E),
                                        exc.rearrange("p (e t) -> p t e", e=E), ALU.add))
                for k in range(2):
                    chain(dve.tensor_tensor(w[2 + k], oh[k], w[5], ALU.mult))
                    chain(dve.tensor_reduce(r[9 + k], w[2 + k], AX_X, ALU.add))
                if E == E0:
                    for k in range(2):
                        dve.tensor_scalar(GATE[:, k, :], gates[k], 0.5, None, ALU.mult).then_inc(s_dve, 1)
                        dve.tensor_copy(SLOT[:, k, :], r[9 + k]).then_inc(s_dve, 1)
                        chain.n += 2
                    dve.wait_ge(s_dve, chain.n)
                else:
                    for k in range(2):
                        chain(dve.tensor_scalar(r[11 + k], r[9 + k], float(CAPACITY), None, ALU.is_lt))
                        chain(dve.tensor_scalar(r[13], r[2 + k], 64.0, float(CAPACITY), ALU.add, ALU.mult))
                        chain(dve.tensor_tensor(r[14], r[13], r[9 + k], ALU.add))
                        chain(dve.tensor_scalar(r[15], cst("tokid"), float(SLOTS + k * TOKENS), None, ALU.add))
                        chain(dve.tensor_tensor(r[16], r[14], r[15], ALU.subtract))
                        chain(dve.tensor_tensor(r[13], r[16], r[11 + k], ALU.mult))
                        chain(dve.tensor_tensor(SLOT[:, k, :], r[13], r[15], ALU.add))
                        chain(dve.tensor_tensor(r[17 + k], gates[k], r[11 + k], ALU.mult))
                    chain(dve.tensor_tensor(r[13], r[17], r[18], ALU.add))
                    chain(dve.tensor_scalar(r[14], r[13], 1e-9, None, ALU.add))
                    chain(dve.reciprocal(r[15], r[14]))
                    for k in range(2):
                        chain(dve.scalar_tensor_tensor(out=GATE[:, k, :], in0=r[17 + k], scalar=0.5, in1=r[15],
                                                       op0=ALU.mult, op1=ALU.mult))
                dve.tensor_copy(RE[:, 7, 0:1], GATE[:, 0, 0:1]).then_inc(s_slot, 1)

                def tile_in(i, c):
                    tau = i * RING + c
                    dve.wait_ge(s_xpt, T0 + tau + 1)
                    if not (isinstance(i, int) and i == 0 and c < PAIR):
                        dve.wait_ge(s_h, (tau - (PAIR - 1)) * FC + T0 * FC)
                    dve.tensor_copy(XPT[:, c % PAIR, 0:S * P], PS[:, 2048:2048 + S * P]).then_inc(s_xpc, 1)

                def tile_out(i, c, steps):
                    tau, r_ = i * RING + c, c % RING
                    if not (isinstance(i, int) and i == 0 and c < RING):
                        dve.wait_ge(s_yo[r_], i * (16 * S) + 16 * S * (c // RING) + scattered0(f, r_))
                    idf = XP[:, r_, 0:S, D]
                    trash = cst("trash")[:, bass.ds(tau * S, S)]
                    a = [IDF[:, r_, k, 0:S] for k in range(3)]
                    dve.tensor_scalar(a[0], idf, tag, None, ALU.is_ge).then_inc(s_dve, 1)
                    steps.n += 1
                    steps(dve.scalar_tensor_tensor(out=a[1], in0=idf, scalar=tag, in1=trash,
                                                   op0=ALU.subtract, op1=ALU.subtract))
                    steps(dve.tensor_tensor(a[2], a[0], a[1], ALU.mult))
                    steps(dve.tensor_tensor(ID[:, r_, 0:S], a[2], trash, ALU.add))
                    dve.wait_ge(s_y, T0 + tau + 1)
                    dve.tensor_tensor(YS[:, r_, 0:S, :], PS[:, 3072:3072 + S * P].rearrange("p (a b) -> p a b", a=S),
                                      WE[:, r_, WROW - D:WROW].unsqueeze(1).to_broadcast((P, S, D)), ALU.add)\
                       .then_inc(s_yc, 1)

                tile_in(0, 0)
                tile_in(0, 1)
                whole = (tiles - 2) // RING
                for c in range(1, RING + 1):
                    tile_in(0, c + 1)
                    tile_out(0, c - 1, chain)
                with dve.Fori(1, whole) as i:
                    chain.loop(i, RING * 4, 1)
                    for c in range(1, RING + 1):
                        tile_in(i, c + 1)
                        tile_out(i, c - 1, chain)
                    chain.ended(whole - 1)
                for c in range(RING * whole + 1, tiles + 1):
                    if c + 1 < tiles:
                        tile_in(0, c + 1)
                    tile_out(0, c - 1, chain)

                last = L == len(SUBLAYERS) - 1
                with dve.Fori(0, NG // 2) as i:
                    chain.loop(i, 2 if last else 4)
                    for u in range(2):
                        dve.wait_ge(s_yin[u], i * 32 + 32 * (NG // 2 * f + 1))
                        t0 = i * (2 * GT) + GT * u
                        for k in range(2):
                            for j in range(GT):
                                xt = X[:, bass.ds(t0 + j, 1), :].rearrange("p a b -> p (a b)")
                                ins = dve.scalar_tensor_tensor(
                                    out=xt, in0=YC[:, u, k, j, :], scalar=GATE[:, k, bass.ds(t0 + j, 1)],
                                    in1=xt, op0=ALU.mult, op1=ALU.add)
                            if last and k == 1:
                                ins.then_inc(s_comb, 1)
                            else:
                                chain(ins)
                        if not last:
                            group_stats(t0).then_inc(s_comb, 1)
                    chain.ended(NG // 2)
                dve.wait_ge(s_comb, NG * (f + 1))

            def stats_loop():
                with dve.Fori(0, NG) as i:
                    chain.loop(i, 1)
                    chain(group_stats(i * GT))
                    chain.ended(NG)

            def attention(L):
                dve.memset(VA[:, :, :, HD:HD + 1], 1.0).then_inc(s_dve, 1)
                chain.n += 1
                rc, rs = cst("rope_c"), cst("rope_s")

                def norm(i, u):
                    if isinstance(i, int) and i == 0:
                        normalise(L, i, u)
                    else:
                        normalise(L, i, u, (s_tr, i * 2 + (NG * L + u - 1)))

                def rope(i, u):
                    n = i * 10 + 5 * u
                    if not (isinstance(i, int) and i == 0):
                        dve.wait_ge(s_lo, i * 2 + (u - 1))
                    for k, (b0, b1) in enumerate((("bq", "bqr"), ("bk", "bkr"))):
                        dve.wait_ge(s_proj, n + (2 * k + 1))
                        dve.scalar_tensor_tensor(out=QF[:, u, k, :], in0=bank(2 + 2 * k), scalar=wt(b0), in1=rc,
                                                 op0=ALU.add, op1=ALU.mult).then_inc(s_rope, 1)
                        dve.wait_ge(s_proj, n + (2 * k + 2))
                        dve.scalar_tensor_tensor(out=QT[:, k, :], in0=bank(3 + 2 * k), scalar=wt(b1), in1=rs,
                                                 op0=ALU.add, op1=ALU.mult).then_inc(s_rope, 1)
                    dve.wait_ge(s_rope, i * 8 + (4 * u + 4))
                    dve.tensor_tensor(QF[:, u], QF[:, u], QT[:, :, :], ALU.add).then_inc(s_rot, 1)
                    dve.wait_ge(s_proj, n + 5)
                    dve.tensor_tensor(VA[:, bass.ds(i * (2 * GT) + GT * u, GT), :, 0:HD],
                                      bank(6).rearrange("p (t h d) -> p t h d", t=GT, h=HEADS),
                                      wt("bv").rearrange("p (h d) -> p h d", h=HEADS).unsqueeze(1)
                                      .to_broadcast((P, GT, HEADS, HD)), ALU.add).then_inc(s_va, 1)

                norm(0, 0)
                norm(0, 1)
                rope(0, 0)

                def groups(i):
                    norm(i + 1, 0)
                    rope(i, 1)
                    norm(i + 1, 1)
                    rope(i + 1, 0)

                groups(0)
                with dve.Fori(1, NG // 2 - 1) as i:
                    groups(i)
                rope(NG // 2 - 1, 1)
                dve.wait_ge(s_va, NG)
                dve.memset(bank(6), 0.0).then_inc(s_va, 1)

                def iteration(i, par, peeled, steps):
                    has_m = not peeled or i + 1 < NG
                    for s in range(HEADS):
                        g, j = s // 4, s % 4
                        if j == 2 and (not peeled or 0 <= 4 * i + g - 2 < 4 * NG):
                            G = i * 4 + (g - 2)
                            gg = (g - 2) % 4
                            sums = bank(7).rearrange("p (a h r) -> p a h r", a=GT, h=4)
                            dve.wait_ge(s_tp, G + 1)
                            steps(dve.reciprocal(RD[:, :, :], sums[:, :, :, HD]))
                            if gg == 0 and not (peeled and 4 * i + g - 2 < 4):
                                dve.wait_ge(s_ap, i)
                            dve.tensor_tensor(AO.rearrange("p a (h d) -> p a h d", h=HEADS)[:, :, 4 * gg:4 * gg + 4, :],
                                              sums[:, :, :, 0:HD],
                                              RD.unsqueeze(3).to_broadcast((P, GT, 4, HD)), ALU.mult)\
                               .then_inc(s_td, 1)
                        if s == 12 and (not peeled or 0 <= i - 1 < NG):
                            dve.wait_ge(s_op, i)
                            xb = X[:, bass.ds(i * GT - GT, GT), :]
                            steps(dve.tensor_tensor(xb, bank(7).rearrange("p (a b) -> p a b", a=GT), xb, ALU.add))
                            dve.tensor_tensor(xb, xb, wt("bo").unsqueeze(1).to_broadcast((P, GT, D)), ALU.add)\
                               .then_inc(s_od, 1)
                        if has_m:
                            for a in range(GT):
                                dve.wait_ge(s_m, i * 64 + (64 + 4 * s + a + 1))
                                dve.tensor_reduce(MX[:, 0, s, a:a + 1], bank(4 + a % 2), AX_X, ALU.max)\
                                   .then_inc(s_mr, 1)
                            if j == 3:
                                mx = MX[:, 0, 4 * g:4 * g + 4, :].rearrange("p a b -> p (a b)")
                                dve.wait_ge(s_mr, i * 64 + (64 + 4 * s + 4))
                                if not (peeled and i == -1 and g == 0):
                                    dve.wait_ge(s_nmp, i * 4 + 4 + g)
                                steps(dve.tensor_scalar(NMB[:, :], mx, -1.0, None, ALU.mult))
                                steps(dve.tensor_copy(NMF[:, 0, :], NMB[:, :]))
                                dve.scalar_tensor_tensor(out=NMF[:, 1, :], in0=mx, scalar=-1.0, in1=NMB[:, :],
                                                         op0=ALU.mult, op1=ALU.subtract).then_inc(s_nmf, 1)

                iteration(-1, 1, True, chain)
                iteration(0, 0, True, chain)
                with dve.Fori(0, (LOOP_HI - 1) // 2) as i:
                    chain.loop(i, 2 * (4 + 1 + 8))
                    iteration(i * 2 + 1, 1, False, chain)
                    iteration(i * 2 + 2, 0, False, chain)
                    chain.ended((LOOP_HI - 1) // 2)
                for i in range(LOOP_HI, NG + 1):
                    iteration(i, i % 2, True, chain)
                dve.wait_ge(s_od, NG)

            def linear(L):
                KVb = PS[:, 1024:2048].rearrange("p (a b) -> p a b", a=GT)
                dve.memset(LV[:, :, :, D:D + 1], 1.0).then_inc(s_dve, 1)
                chain.n += 1

                def f1(i, u):
                    if isinstance(i, int) and i == 0:
                        normalise(L, i, u)
                    else:
                        normalise(L, i, u, (s_tr, i * 2 + (NG * L + u - 1)))

                def f2(i, u):
                    n = i * 2 + (u + 1)
                    dve.wait_ge(s_lq, n)
                    if not (isinstance(i, int) and i == 0):
                        dve.wait_ge(s_ln, n - 2)
                    dve.tensor_scalar(LQM[:, u], bank(4), 0.0, None, ALU.min).then_inc(s_lqm, 1)
                    dve.wait_ge(s_lqe, n)
                    dve.scalar_tensor_tensor(out=LQF[:, u], in0=bank(4), scalar=0.0, in1=LQE[:, u],
                                             op0=ALU.max, op1=ALU.add).then_inc(s_lqf, 1)

                def f3(i, u):
                    n = i * 2 + (u + 1)
                    dve.wait_ge(s_lk, n)
                    dve.wait_ge(s_lv, n)
                    dve.tensor_scalar(LKM[:, u], KVb[:, :, 0:D], 0.0, None, ALU.min).then_inc(s_lkm, 1)
                    dve.wait_ge(s_lke, n)
                    dve.scalar_tensor_tensor(out=LKF[:, u], in0=KVb[:, :, 0:D], scalar=0.0, in1=LKE[:, u],
                                             op0=ALU.max, op1=ALU.add).then_inc(s_lkf, 1)

                def b1(i, u):
                    n = i * 2 + (u + 1)
                    dve.wait_ge(s_kv, n)
                    dve.tensor_tensor(BD[:, u, 0:D], bank(4, 0, D), cst("blockmask"), ALU.mult)
                    dve.tensor_scalar(BD[:, u, D:D + HEADS], cst("headmask"), bank(4, D, D + 1), None, ALU.mult)\
                       .then_inc(s_bd, 1)

                def b2(i, u, steps):
                    n = i * 2 + (u + 1)
                    num = PS[:, 2560:2560 + 256 * GT].rearrange("p (a b) -> p a b", a=GT)
                    dve.wait_ge(s_ln, n)
                    steps(dve.tensor_scalar(LDN[:, u], num[:, :, D:D + HEADS], 1e-6, None, ALU.add))
                    steps(dve.reciprocal(LRD[:, u], LDN[:, u]))
                    dve.tensor_tensor(LAO[:, u].rearrange("p a (h d) -> p a h d", h=HEADS),
                                      num[:, :, 0:D].rearrange("p a (h d) -> p a h d", h=HEADS),
                                      LRD[:, u].unsqueeze(3).to_broadcast((P, GT, HEADS, HD)), ALU.mult)\
                       .then_inc(s_lao, 1)

                def b4(i, u, steps):
                    n = i * 2 + (u + 1)
                    dve.wait_ge(s_lo2, n)
                    t0 = i * (2 * GT) + GT * u
                    xb = X[:, bass.ds(t0, GT), :]
                    dve.tensor_tensor(xb, bank(7).rearrange("p (a b) -> p a b", a=GT), xb, ALU.add)\
                       .then_inc(s_lres, 1)
                    dve.wait_ge(s_lres, n)
                    steps(group_stats(t0))

                def both(i, u, i2, u2, steps):
                    f1(i, u)
                    b1(i2, u2)
                    f2(i, u)
                    b2(i2, u2, steps)
                    f3(i, u)
                    b4(i2, u2, steps)

                f1(0, 0)
                f2(0, 0)
                f3(0, 0)
                both(0, 1, 0, 0, chain)
                with dve.Fori(0, NG // 2 - 1) as i:
                    chain.loop(i, 6)
                    both(i + 1, 0, i, 1, chain)
                    both(i + 1, 1, i + 1, 0, chain)
                    chain.ended(NG // 2 - 1)
                i = NG // 2 - 1
                b1(i, 1)
                b2(i, 1, chain)
                b4(i, 1, chain)

            dve.wait_ge(s_x, 16)
            dve.wait_ge(s_cst, 16)
            dve.wait_ge(s_wt, 16)
            dve.wait_ge(s_cleared, CLEARED)
            dve.tensor_copy(before_bf[:, :], cst("before"))
            chain(dve.tensor_copy(ones_bf[:, :], cst("ones")))
            stats_loop()
            for L, kind in enumerate(SUBLAYERS):
                finish_stats(L)
                if kind in (FFN0, FFN1):
                    moe(L)
                elif kind == ATTN:
                    attention(L)
                    stats_loop()
                else:
                    linear(L)
            dve.tensor_copy(RE[:, 7, 0:1], cst("ones")[:, 0:1]).then_inc(s_final, NG)


CLEARED = 16 * (SLOTS // (P * 40) + PAIRS // (P * 32) + 1)
LOOP_HI = NG - 1
LOADS = 16 * (2 * PARTS * PARTS + 1)


def kernel(**inputs):
    import concourse.bacc as _bacc
    from concourse import mybir as _mybir
    from concourse.bass_utils import run_bass_kernel_spmd as _run

    a = {k: np.asarray(v) for k, v in inputs.items()}
    turned = (np.arange(D) // HD) * HD + (np.arange(D) + HD // 2) % HD

    def column(v):
        return v.reshape(P, 1)

    def every(v, n=1):
        return np.broadcast_to(np.tile(v.reshape(1, -1), (1, n)), (P, v.size * n))

    parts = {
        "wq": a["L0_attn_Wq"].T, "wqr": a["L0_attn_Wq"][turned].T,
        "wk": a["L0_attn_Wk"].T, "wkr": a["L0_attn_Wk"][turned].T,
        "wv": a["L0_attn_Wv"].T, "wo": a["L0_attn_Wo"].T,
        "lq": a["L1_attn_Wq"].T, "lkv": np.concatenate([a["L1_attn_Wk"].T, a["L1_attn_Wv"].T], 1),
        "lo": a["L1_attn_Wo"].T, "r0": a["L0_ffn_Wr"], "r1": a["L1_ffn_router_w"].T,
        "bq": column(a["L0_attn_bq"]), "bqr": column(a["L0_attn_bq"][turned]),
        "bk": column(a["L0_attn_bk"]), "bkr": column(a["L0_attn_bk"][turned]),
        "bv": every(a["L0_attn_bv"]), "bo": every(a["L0_attn_bo"]),
        "rb0": every(a["L0_ffn_br"], GT), "rb1": every(a["L1_ffn_router_b"], GT),
    }
    weights = np.ascontiguousarray(np.concatenate([parts[n] for n, _ in WEIGHTS], 1))

    def experts(w1, b1, w2, b2):
        e = w1.shape[0]
        return np.ascontiguousarray(np.concatenate([
            w1,
            w2.reshape(e, FC, P, D).transpose(0, 2, 1, 3).reshape(e, P, FC * D),
            b1.reshape(e, FC, P).transpose(0, 2, 1),
            np.broadcast_to(b2[:, None, :], (e, P, D))], 2))

    arrays = {
        "x": np.ascontiguousarray(a["L0_attn_x"].reshape(TOKENS, D)),
        "constants": constants(),
        "weights": weights,
        "experts0": experts(a["L0_ffn_W1"], a["L0_ffn_b1"], a["L0_ffn_W2"], a["L0_ffn_b2"]),
        "experts1": experts(a["L1_ffn_w1"], a["L1_ffn_b1"], a["L1_ffn_w2"], a["L1_ffn_b2"]),
    }
    nc = _bacc.Bacc("TRN2", target_bir_lowering=False, num_devices=1)
    args = [nc.dram_tensor(n, v.shape, _mybir.dt.from_np(v.dtype), kind="ExternalInput").ap()
            for n, v in arrays.items()]
    out = nc.dram_tensor("out", (TOKENS, D), F32, kind="ExternalOutput").ap()
    build(nc, *args, out)
    r = _run(nc, [arrays], core_ids=[0])
    return r.results[0]["out"].reshape(BATCHES, SEQ, D)
```

```python
from contextlib import ExitStack

import concourse.bass as bass
import numpy as np
from concourse import mybir

ALU = mybir.AluOpType
ACT = mybir.ActivationFunctionType
F32 = mybir.dt.float32
BF16 = mybir.dt.bfloat16
I32 = mybir.dt.int32
U32 = mybir.dt.uint32
AX_X = mybir.AxisListType.X

P = 128
D = 128
BATCHES, SEQ = 8, 512
TOKENS = BATCHES * SEQ
NT = TOKENS // P
GT = SEQ // P
NG = NT // GT
HEADS = 16
HD = D // HEADS
DFF = 512
FC = DFF // P
LN_EPS = 1e-5

CAPACITY = -(-5 * TOKENS * 2 // (4 * 16))
E0, S0 = 8, 2
E1, S1 = 16, CAPACITY // P
MOE = [dict(E=E0, S=S0, tiles=TOKENS * 2 // (S0 * P) + E0 - 1), dict(E=E1, S=S1, tiles=E1)]
assert CAPACITY == S1 * P
SLOTS = max(m["tiles"] * m["S"] * P for m in MOE)
PAIRS = 2 * TOKENS
REGION = TOKENS + S0 * P
SPARE = MOE[0]["tiles"] * S0 * P - PAIRS
ROW = D + 1
TAG = 65536.0
NEG = -3.0e38
WROW = FC * P + FC * D + FC + D

FFN0, ATTN, FFN1, LINATTN = range(4)
SUBLAYERS = [FFN0, ATTN, FFN0, FFN1, LINATTN, FFN1]

PARTS = 3
QK_ROWS = PARTS * PARTS * HD
STACK = 96
M_ROW = QK_ROWS

XCHUNKS = 4
RING = 4
PAIR = 2


def constant_layout():
    at, out = 0, {}
    for name, n in [("ident", P), ("before", P), ("ones", P), ("tokid", NT), ("eoff", E1),
                    ("region", E1), ("jtab", E0 * 16), ("tiletab", MOE[0]["tiles"] * E0),
                    ("tilerow", MOE[0]["tiles"]),
                    ("trash", SLOTS // P), ("blockmask", D), ("headmask", HEADS),
                    ("rope_c", SEQ), ("rope_s", SEQ)]:
        out[name] = (at, n)
        at += n
    return out, at


def constants():
    lay, n = constant_layout()
    c = np.zeros((P, n), np.float32)

    def put(name, v):
        a, w = lay[name]
        c[:, a:a + w] = np.broadcast_to(v, (P, w))

    p = np.arange(P)
    put("ident", np.eye(P))
    put("before", p[:, None] < p[None, :])
    put("ones", 1.0)
    put("tokid", np.arange(NT)[None, :] * P + p[:, None])
    put("eoff", np.arange(E1) - 64.0)
    put("region", np.arange(E1) * REGION)
    put("jtab", np.tile(np.arange(16) * S0 * P, E0)[None, :])
    put("tiletab", np.repeat(np.arange(MOE[0]["tiles"]), E0)[None, :])
    put("tilerow", np.arange(MOE[0]["tiles"]) * S0 * P)
    put("trash", PAIRS + np.arange(SLOTS // P)[None, :] * P + p[:, None])
    put("blockmask", (p[:, None] // HD) == (p[None, :] // HD))
    put("headmask", (p[:, None] // HD) == np.arange(HEADS)[None, :])
    inv = (1.0 / 10000.0 ** (np.arange(0, HD, 2) / HD)).astype(np.float32)
    ang = (np.arange(SEQ, dtype=np.float32)[:, None] * inv[None, :]).astype(np.float32).astype(np.float64)
    dim = p // HEADS
    ang = ang[:, dim % (HD // 2)].T
    put("rope_c", np.cos(ang))
    put("rope_s", np.sin(ang) * np.where(dim < HD // 2, -1.0, 1.0)[:, None])
    return c


WEIGHTS = [("wq", D), ("wqr", D), ("wk", D), ("wkr", D), ("wv", D), ("wo", D),
           ("lq", D), ("lkv", 2 * D), ("lo", D), ("r0", E0), ("r1", E1),
           ("bq", 1), ("bqr", 1), ("bk", 1), ("bkr", 1), ("bv", D), ("bo", D),
           ("rb0", GT * E0), ("rb1", GT * E1)]


def weight_layout():
    at, out = 0, {}
    for name, n in WEIGHTS:
        out[name] = (at, n)
        at += n
    return out, at


def build(nc, x_in, cst_in, w_in, ex0_in, ex1_in, out):
    CL, CN = constant_layout()
    WL, WN = weight_layout()
    ex_in = [ex0_in, ex1_in]

    ctx = ExitStack()
    with ctx:
        def sb(name, shape, dt=F32):
            return ctx.enter_context(nc.sbuf_tensor(name, shape, dt))

        def sem(name):
            return ctx.enter_context(nc.semaphore(name))

        X = sb("X", [P, NT, D])
        CST = sb("CST", [P, CN])
        WT = sb("WT", [P, WN])
        BST = sb("BST", [P, NT, 6])
        LN = sb("LN", [P, 12, NT])
        MEAN, RSTD = LN[:, 0, :], LN[:, 1, :]
        XS = sb("XS", [P, 2, GT, D])
        XT = sb("XT", [P, 2, SEQ])
        PS = ctx.enter_context(nc.psum_tensor("PS", [P, 8 * 512], F32))

        def bank(n, a=0, b=512):
            return PS[:, 512 * n + a:512 * n + b]

        def cst(name):
            a, n = CL[name]
            return CST[:, a:a + n]

        def wt(name):
            a, n = WL[name]
            return WT[:, a:a + n]

        ident = cst("ident")

        ARENA = 162 * 256
        arena = sb("arena", [P, ARENA])

        class Carver:
            def __init__(self):
                self.at = 0

            def __call__(self, shape, dt=F32, rows=P):
                n = int(np.prod(shape)) * (2 if dt == BF16 else 4)
                assert n % 4 == 0
                n //= 4
                assert self.at + n <= ARENA, (self.at, n)
                v = arena[0:rows, self.at:self.at + n]
                self.at += n
                if dt != F32:
                    v = v.bitcast(dt)
                names = "abcde"[:len(shape)]
                if len(shape) > 1:
                    v = v.rearrange(f"p ({' '.join(names)}) -> p {' '.join(names)}",
                                    **{k: s for k, s in zip(names[:-1], shape[:-1])})
                return v

        cv = Carver()
        XR = cv([2, NT, ROW])
        LG = cv([GT, E1])
        RT = [cv([GT, E1]) for _ in range(3)]
        OH = cv([2, GT, E1])
        PL = cv([2, GT, E1])
        MB = cv([2, GT, E1], BF16)
        SUM = cv([2, E1], BF16)
        SUMF = cv([E1])
        R1 = cv([20, NT])
        SLOT = cv([2, NT], U32)
        GATE = cv([2, NT])
        RE = cv([8, E0])
        ETF = cv([MOE[0]["tiles"]])
        ET = cv([MOE[0]["tiles"]], I32)
        TT = cv([MOE[0]["tiles"], E0])
        TW = cv([MOE[0]["tiles"], E0])
        TSF = cv([2, MOE[0]["tiles"]])
        TS = cv([MOE[0]["tiles"]], I32)
        CNT = cv([E0], I32)
        JT = cv([E0, 16])
        WE = cv([RING, WROW])
        XP = cv([RING, S1, ROW])
        XPT = cv([PAIR, S1 * P])
        HT = cv([PAIR, FC, S1 * P])
        YS = cv([RING, S1, D])
        IDF = cv([RING, 3, S1])
        ID = cv([RING, S1], U32)
        YC = cv([2, 2, GT, D])
        cv = Carver()
        QS = cv([2, HEADS, SEQ], BF16)
        KS = cv([2, HEADS, SEQ], BF16)
        at_weights = cv.at
        PT = cv([2, 4, GT, SEQ])
        at_main = cv.at
        VA = cv([NT, HEADS, HD + 1])
        VB = cv([2, GT, HEADS, HD + 1])
        MX = cv([2, HEADS, GT])
        NMB = cv([4 * GT], BF16)
        NMF = cv([2, 4 * GT])
        NMT = cv([P], BF16)
        OT = cv([SEQ])
        RD = cv([GT, 4])
        AO = cv([GT, D])
        AT = cv([SEQ])
        cv.at = at_weights
        QF = cv([2, 2, SEQ])
        QT = cv([2, SEQ])
        QR = cv([2, 2, SEQ])
        QP = cv([2, PARTS, 2, SEQ], BF16)
        assert cv.at <= at_main
        cv = Carver()
        LQM = cv([2, SEQ])
        LQE = cv([2, SEQ])
        LQF = cv([2, SEQ])
        LKM = cv([2, GT, D])
        LKE = cv([2, GT, D])
        LKF = cv([2, GT, D])
        LV = cv([2, GT, D + 1])
        BD = cv([2, D + HEADS])
        LRD = cv([2, GT, HEADS])
        LDN = cv([2, GT, HEADS])
        LAO = cv([2, GT, D])
        LAT = cv([2, SEQ])
        ZERO = sb("ZERO", [P, S1 * ROW])
        ones_bf = sb("ones_bf", [P, P], BF16)
        before_bf = sb("before_bf", [P, P], BF16)

        BUFS = [nc.dram_tensor("dispatched0", (E0 * REGION + SPARE, ROW), F32).ap(),
                nc.dram_tensor("dispatched1", (E1 * REGION, ROW), F32).ap()]
        YK = nc.dram_tensor("expert_out", (PAIRS + SLOTS, D), F32).ap()
        QKD = nc.dram_tensor("qk_parts", (BATCHES, 2, 2 * PARTS - 1, P, SEQ), BF16).ap()
        ZD = nc.dram_tensor("zero_rows", (2, 4 * SEQ), BF16).ap()

        s_x = [sem(f"x_loaded{c}") for c in range(XCHUNKS)]
        s_cst, s_wt = sem("cst_loaded"), sem("weights_loaded")
        s_zero, s_cleared = sem("zeros_made"), sem("scratch_cleared")
        s_dve, s_pool_chain = sem("dve_step"), sem("pool_step")
        s_var, s_sd = sem("variance_ready"), sem("deviation_ready")
        s_xs, s_tr, s_xt = sem("xs_ready"), sem("xs_transposed"), sem("xt_ready")
        s_row = sem("rows_copied")
        s_lg, s_lgc = sem("logits_done"), sem("logits_copied")
        s_gap, s_ex = sem("score_gap_ready"), sem("gap_exp_ready")
        s_sum = sem("choices_summed")
        s_mask, s_rank = sem("chosen_ready"), sem("ranks_done")
        s_counts, s_tiles, s_tails = sem("counts_done"), sem("tiles_ready"), sem("tails_cleared")
        s_slot, s_disp = sem("slots_ready"), sem("rows_dispatched")
        s_xp = [sem(f"tile_rows_in{r}") for r in range(RING)]
        s_we = [sem(f"expert_in{r}") for r in range(RING)]
        s_xpt, s_xpc = sem("tile_transposed"), sem("tile_copied")
        s_h, s_g = sem("hidden_done"), sem("gelu_done")
        s_y, s_yc = sem("y_done"), sem("y_copied")
        s_yo = [sem(f"y_scattered{r}") for r in range(RING)]
        s_yin = [sem(f"y_gathered{u}") for u in range(2)]
        s_comb = sem("group_combined")
        s_final, s_out = sem("x_final"), sem("out_stored")
        s_proj, s_rope, s_rot = sem("projected"), sem("rope_read"), sem("qk_roped")
        s_hi, s_r1, s_mid, s_lo = sem("hi_part"), sem("rest1"), sem("mid_part"), sem("lo_part")
        s_qd = [sem(f"qk_parts_stored{u}") for u in range(2)]
        s_va, s_fill = sem("v_copied"), sem("stack_filled")
        s_vb = sem("v_batch_copied")
        s_st = [[sem(f"stack_in{u}{g}") for g in range(4)] for u in range(2)]
        s_nmi = [sem(f"max_rows_in{g}") for g in range(4)]
        s_e, s_exp = sem("scores_done"), sem("exp_done")
        s_m, s_mr = sem("max_scores_done"), sem("max_done")
        s_nmf, s_nmp, s_nmt = sem("negmax_ready"), sem("negmax_transposed"), sem("negmax_copied")
        s_av, s_ot = sem("av_done"), sem("av_copied")
        s_tp, s_td = sem("av_transposed"), sem("av_normalised")
        s_ap, s_at, s_op, s_od = sem("ao_transposed"), sem("at_copied"), sem("wo_done"), sem("residual_done")
        s_lq, s_lqm, s_lqe, s_lqf = sem("lin_q_done"), sem("lin_q_min"), sem("lin_q_exp"), sem("lin_q_ready")
        s_lk, s_lkm, s_lke, s_lkf = sem("lin_kv_done"), sem("lin_k_min"), sem("lin_k_exp"), sem("lin_k_ready")
        s_lv, s_kv, s_bd = sem("lin_v_ready"), sem("kv_done"), sem("kv_masked")
        s_ln, s_lao, s_la, s_lat = sem("lin_num_done"), sem("lin_out_ready"), sem("lin_out_t"), sem("lin_at_copied")
        s_lo2, s_lres = sem("lin_wo_done"), sem("lin_residual_done")

        block = ctx.enter_context(nc.Block())

        def ffn_of(L):
            return sum(k in (FFN0, FFN1) for k in SUBLAYERS[:L])

        FFNS = [k for k in SUBLAYERS if k in (FFN0, FFN1)]

        def moe_of(f):
            return MOE[0 if FFNS[f] == FFN0 else 1]

        def first_kind(f):
            return sum(k == FFN0 for k in FFNS[:f])

        TILES0 = [sum(moe_of(j)["tiles"] for j in range(f)) for f in range(len(FFNS) + 1)]

        def rounds(f, r):
            return len(range(r, moe_of(f)["tiles"], RING))

        def rounds0(f, r):
            return sum(rounds(j, r) for j in range(f))

        def scattered0(f, r):
            return sum(rounds(j, r) * moe_of(j)["S"] * 16 for j in range(f))

        class Chain:

            def __init__(self, eng, s):
                self.eng, self.s, self.n, self.base = eng, s, 0, 0

            def __call__(self, ins):
                ins.then_inc(self.s, 1)
                self.n += 1
                self.eng.wait_ge(self.s, self.base + self.n)

            def loop(self, i, k, first=0):
                self.start, self.k = self.n, k
                self.base, self.n = i * k + (self.start - first * k), 0

            def ended(self, count):
                assert self.n == self.k, (self.n, self.k)
                self.base, self.n = 0, self.start + count * self.k

        @block.sync
        def _(sp):
            xs, n = x_in.rearrange("(t p) d -> p t d", p=P), NT // XCHUNKS
            for c in range(XCHUNKS):
                if c == 1:
                    sp.dma_start(CST[:, :], cst_in).then_inc(s_cst, 16)
                    sp.dma_start(WT[:, :], w_in).then_inc(s_wt, 16)
                sp.dma_start(X[:, n * c:n * c + n, :], xs[:, n * c:n * c + n, :]).then_inc(s_x[c], 16)
            sp.wait_ge(s_zero, 1)
            for e in range(E1):
                sp.dma_start(BUFS[1][e * REGION:e * REGION + CAPACITY, :].rearrange("(p r) c -> p (r c)", p=P),
                             ZERO[:, :]).then_inc(s_cleared, 16)
            for a in range(E0 * REGION, E0 * REGION + SPARE, S0 * P):
                sp.dma_start(BUFS[0][a:a + S0 * P, :].rearrange("(p r) c -> p (r c)", p=P),
                             ZERO[:, 0:S0 * ROW]).then_inc(s_cleared, 16)
            sp.dma_start(ZD.rearrange("a b -> (a b)").rearrange("(a b) -> a b", a=8),
                         ZERO[0:8, 0:256].bitcast(BF16)).then_inc(s_cleared, 16)

            def moe(L):
                f = ffn_of(L)
                m, T0 = moe_of(f), TILES0[ffn_of(L)]
                S, tiles, ex = m["S"], m["tiles"], ex_in[SUBLAYERS[L] == FFN1]
                buf = BUFS[0 if S == S0 else 1]
                if S == S0:
                    sp.wait_ge(s_tiles, first_kind(f) + 1)
                    for e in range(E0):
                        end = sp.value_load(CNT[0:1, e:e + 1], min_val=e * REGION, max_val=e * REGION + TOKENS)
                        sp.dma_start(buf[bass.ds(end, S0 * P), :].rearrange("(p r) c -> p (r c)", p=P),
                                     ZERO[:, 0:S0 * ROW]).then_inc(s_tails, 16)
                    sp.wait_ge(s_tails, 16 * E0 * (first_kind(f) + 1))
                sp.wait_ge(s_disp, 16 * 2 * NT * (f + 1))
                if f == 0:
                    sp.wait_ge(s_cleared, CLEARED)

                def load(i, c):
                    tau, r = i * RING + c, c % RING
                    if not (isinstance(i, int) and i == 0 and c < RING):
                        sp.wait_ge(s_yc, T0 + tau - (RING - 1))
                    if S == S0:
                        row = sp.value_load(TS[0:1, bass.ds(tau, 1)], min_val=0, max_val=E0 * REGION + SPARE - S0 * P)
                        e = sp.value_load(ET[0:1, bass.ds(tau, 1)], min_val=0, max_val=E0 - 1)
                    else:
                        row, e = tau * REGION, tau
                    sp.dma_start(XP[:, r, 0:S, :], buf[bass.ds(row, S * P), :]
                                 .rearrange("(j p) c -> p j c", p=P)).then_inc(s_xp[r], 16)
                    sp.dma_start(WE[:, r, :], ex[bass.ds(e, 1)].rearrange("o p n -> p (o n)"))\
                      .then_inc(s_we[r], 16)

                for c in range(RING):
                    load(0, c)
                whole = tiles // RING - 1
                with sp.Fori(0, whole) as i:
                    for c in range(RING):
                        load(i, RING + c)
                for c in range(RING * (whole + 1), tiles):
                    load(0, c)
                for r in range(RING):
                    sp.wait_ge(s_yo[r], scattered0(f + 1, r))
                src = YK[0:PAIRS, :].rearrange("(k t p) c -> p k t c", k=2, p=P)

                def fetch(i, u):
                    if not (isinstance(i, int) and i == 0):
                        sp.wait_ge(s_comb, i * 2 + (f * NG + u - 1))
                    for k in range(2):
                        sp.dma_start(YC[:, u, k], src[:, k, bass.ds(i * (2 * GT) + u * GT, GT), :])\
                          .then_inc(s_yin[u], 16)

                fetch(0, 0)
                fetch(0, 1)
                with sp.Fori(1, NG // 2) as i:
                    fetch(i, 0)
                    fetch(i, 1)

            def attention(L):
                def store(b, u):
                    sp.wait_ge(s_lo, b + 1)
                    for w, a, n in ((0, 0, PARTS), (1, 0, PARTS), (1, PARTS, PARTS - 1)):
                        sp.dma_start(QKD[bass.ds(b, 1), w, a:a + n].rearrange("o a r t -> r (o a) t"),
                                     QP[:, u, 0:n, w, :]).then_inc(s_qd[u], 16)

                def load(b, par, g):
                    hs = slice(4 * g, 4 * g + 4)
                    n = PARTS * HD
                    q, k = [QKD[bass.ds(b, 1), w].rearrange("o a (d h) t -> (o a d) (h t)", h=HEADS)
                            [:, 4 * g * SEQ:4 * (g + 1) * SEQ] for w in range(2)]
                    for turn in range(PARTS):
                        sp.dma_start(QS[turn * n:turn * n + n, par, hs, :].rearrange("r h t -> r (h t)"),
                                     q[0:n]).then_inc(s_st[par][g], 16)
                        sp.dma_start(KS[turn * n:turn * n + n, par, hs, :].rearrange("r h t -> r (h t)"),
                                     k[turn * HD:turn * HD + n]).then_inc(s_st[par][g], 16)
                    sp.dma_start(QS[M_ROW:M_ROW + 2, par, hs, :],
                                 ZD.rearrange("a (h t) -> a h t", h=4)).then_inc(s_st[par][g], 16)

                store(0, 0)
                store(1, 1)
                sp.wait_ge(s_fill, 2)
                for b in range(2):
                    sp.wait_ge(s_qd[b], STORES)
                    for g in range(4):
                        load(b, b, g)
                    store(2 + b, b)
                with sp.Fori(2, NG // 2) as i:
                    store(i * 2, 0)
                    store(i * 2 + 1, 1)
                sp.wait_ge(s_qd[0], STORES * NG // 2)
                sp.wait_ge(s_qd[1], STORES * NG // 2)

                def iteration(i, par, lo, hi):
                    for g in range(4):
                        gg = g - 1 if g else 3
                        has = (i >= 0 if g == 0 else i + 1 < NG) if lo else True
                        if has and not (lo and g == 0 and i >= NG):
                            bb = i if g == 0 else i + 1
                            pp = par if g == 0 else 1 - par
                            sp.wait_ge(s_nmt, bb * 4 + gg + 1)
                            for k in range(2):
                                sp.dma_start(
                                    QS[M_ROW + k:M_ROW + k + 1, pp, 4 * gg:4 * gg + 4, :]
                                    .rearrange("o h (a t) -> o (h a) t", t=P),
                                    NMT[16 * k:16 * k + 16, :]).then_inc(s_nmi[gg], 16)
                        if (not lo) or (0 <= i and i + 2 < NG):
                            sp.wait_ge(s_e, i * 32 + 8 * g + 8)
                            load(i + 2, par, g)

                iteration(-1, 1, True, True)
                iteration(0, 0, True, True)
                with sp.Fori(0, (LOOP_HI - 3) // 2) as i:
                    iteration(i * 2 + 1, 1, False, False)
                    iteration(i * 2 + 2, 0, False, False)
                for i in range(LOOP_HI - 2, NG + 1):
                    iteration(i, i % 2, True, True)

            for L, kind in enumerate(SUBLAYERS):
                if kind in (FFN0, FFN1):
                    moe(L)
                elif kind == ATTN:
                    attention(L)
            sp.wait_ge(s_final, NG)
            sp.dma_start(out.rearrange("(t p) d -> p t d", p=P), X[:, :, :]).then_inc(s_out, 16)
            sp.wait_ge(s_out, 16)

        @block.gpsimd
        def _(pool):
            nc.gpsimd.memset(ZERO[:, :], 0.0).then_inc(s_zero, 1)

            def moe(L):
                f = ffn_of(L)
                m, T0 = moe_of(f), TILES0[ffn_of(L)]
                S, tiles = m["S"], m["tiles"]
                buf = BUFS[0 if S == S0 else 1]
                if f == 0:
                    pool.wait_ge(s_cleared, CLEARED)
                for t in range(NT):
                    if t % GT == 0:
                        pool.wait_ge(s_row, NG * f + t // GT + 1)
                        pool.wait_ge(s_slot, NG * f + t // GT + 1)
                    for k in range(2):
                        pool.indirect_dma_start(buf, bass.IndirectOffsetOnAxis(ap=SLOT[:, k, t:t + 1], axis=0),
                                                XR[:, k, t, :], None).then_inc(s_disp, 16)

                def scatter(i, c):
                    tau, r = i * RING + c, c % RING
                    pool.wait_ge(s_yc, T0 + tau + 1)
                    pool.nop(nofuse=True)
                    for s in range(S):
                        pool.indirect_dma_start(YK, bass.IndirectOffsetOnAxis(ap=ID[:, r, s:s + 1], axis=0),
                                                YS[:, r, s, :], None).then_inc(s_yo[r], 16)

                whole = tiles // RING
                with pool.Fori(0, whole) as i:
                    for c in range(RING):
                        scatter(i, c)
                for c in range(RING * whole, tiles):
                    scatter(0, c)

            def attention(L):
                pool.wait_ge(s_comb, NG * ffn_of(L))
                pool.memset(QS[64:STACK], 0.0).then_inc(s_fill, 1)
                pool.memset(KS[64:STACK], 1.0).then_inc(s_fill, 1)
                pool.wait_ge(s_fill, 2)
                with pool.Fori(0, NG // 2) as i:
                    for u in range(2):
                        pool.wait_ge(s_hi, i * 2 + u + 1)
                        pool.tensor_tensor(QR[:, u], QF[:, u], QP[:, u, 0], ALU.subtract).then_inc(s_r1, 1)
                        pool.wait_ge(s_mid, i * 2 + u + 1)
                        pool.tensor_tensor(QP[:, u, 2], QR[:, u], QP[:, u, 1], ALU.subtract).then_inc(s_lo, 1)

                def values(i, par, wait):
                    if wait:
                        pool.wait_ge(s_av, i * 4)
                    pool.tensor_copy(VB[:, 1 - par], VA[:, bass.ds(i * GT + GT, GT)]).then_inc(s_vb, 1)

                pool.wait_ge(s_va, NG)
                values(-1, 1, False)
                values(0, 0, False)
                with pool.Fori(0, (LOOP_HI - 1) // 2) as i:
                    values(i * 2 + 1, 1, True)
                    values(i * 2 + 2, 0, True)

            for L, kind in enumerate(SUBLAYERS):
                if kind in (FFN0, FFN1):
                    moe(L)
                elif kind == ATTN:
                    attention(L)

        @block.scalar
        def _(act):
            def deviation(L):
                act.wait_ge(s_var, L + 1)
                act.activation(LN[:, 7, :], LN[:, 6, :], ACT.Sqrt).then_inc(s_sd, 1)

            def transposed_group(L, i, u):
                act.wait_ge(s_tr, i * 2 + (NG * L + u + 1))
                act.activation(XT[:, u, :], bank(u), ACT.Copy).then_inc(s_xt, 1)

            def moe(L):
                f = ffn_of(L)
                m, T0 = moe_of(f), TILES0[ffn_of(L)]
                S, tiles = m["S"], m["tiles"]
                func = ACT.Gelu_apprx_tanh if SUBLAYERS[L] == FFN0 else ACT.Gelu
                deviation(L)
                with act.Fori(0, NG // 2) as i:
                    for u in range(2):
                        transposed_group(L, i, u)
                        act.activation(XR[:, :, bass.ds(i * 2 * GT + u * GT, GT), 0:D],
                                       XS[:, u].unsqueeze(1).to_broadcast((P, 2, GT, D)), ACT.Copy)\
                           .then_inc(s_row, 1)
                act.wait_ge(s_gap, f + 1)
                act.activation(R1[:, 5, :], R1[:, 4, :], ACT.Exp).then_inc(s_ex, 1)

                def gelus(i, c):
                    tau, r = i * RING + c, c % RING
                    for q in range(FC):
                        act.wait_ge(s_h, tau * FC + (T0 * FC + q + 1))
                        if q == 0 and not (isinstance(i, int) and i == 0 and c < PAIR):
                            act.wait_ge(s_y, T0 + tau - (PAIR - 1))
                        act.activation(HT[:, c % PAIR, q, 0:S * P], PS[:, 1024 * (q % 2):1024 * (q % 2) + S * P],
                                       func, bias=WE[:, r, 2 * DFF + q:2 * DFF + q + 1]).then_inc(s_g, 1)

                for c in range(RING):
                    gelus(0, c)
                whole = tiles // RING - 1
                with act.Fori(0, whole) as i:
                    for c in range(RING):
                        gelus(i, RING + c)
                for c in range(RING * (whole + 1), tiles):
                    gelus(0, c)

            def attention(L):
                deviation(L)

                def split(i, u):
                    transposed_group(L, i, u)
                    act.wait_ge(s_rot, i * 2 + (u + 1))
                    if not (isinstance(i, int) and i == 0):
                        act.wait_ge(s_qd[u], i * STORES)
                    act.activation(QP[:, u, 0], QF[:, u], ACT.Copy).then_inc(s_hi, 1)
                    act.wait_ge(s_r1, i * 2 + (u + 1))
                    act.activation(QP[:, u, 1], QR[:, u], ACT.Copy).then_inc(s_mid, 1)

                split(0, 0)
                split(0, 1)
                with act.Fori(1, NG // 2) as i:
                    split(i, 0)
                    split(i, 1)

                def iteration(i, par, peeled):
                    has_m = not peeled or i + 1 < NG
                    has_e = not peeled or 0 <= i < NG
                    for s in range(HEADS):
                        g, j = s // 4, s % 4
                        if has_e:
                            exp(i, par, s, 0)
                        if j == 0 and (not peeled or 0 <= 4 * i + g - 2 < 4 * NG):
                            G = i * 4 + (g - 2)
                            act.wait_ge(s_av, G + 1)
                            if not (peeled and 4 * i + g - 2 == 0):
                                act.wait_ge(s_tp, G)
                            act.activation(OT[:, :], bank(6), ACT.Copy).then_inc(s_ot, 1)
                        if j == 3:
                            b, gg = (i, 3) if g == 0 else (i + 1, g - 1)
                            if not peeled or (0 <= b < NG):
                                act.wait_ge(s_nmp, b * 4 + gg + 1)
                                if not (peeled and b == 0 and gg == 0):
                                    bb, g2 = (b, gg - 1) if gg else (b - 1, 3)
                                    act.wait_ge(s_nmi[g2], bb * 32 + 32)
                                act.activation(NMT[0:32, :], bank(7, 0, P)[0:32, :], ACT.Copy).then_inc(s_nmt, 1)
                        if s == 8 and (not peeled or 0 <= i - 1 < NG):
                            act.wait_ge(s_ap, i)
                            act.activation(AT[:, :], bank(7), ACT.Copy).then_inc(s_at, 1)
                        if has_e:
                            exp(i, par, s, 1)

                def exp(i, par, s, w):
                    g, j = s // 4, s % 4
                    act.wait_ge(s_e, i * 32 + (2 * s + w + 1))
                    if w == 0 and j == 0 and not (isinstance(i, int) and 4 * i + g < 2):
                        act.wait_ge(s_av, i * 4 + g - 1)
                    act.activation(PT[:, g % 2, j, 2 * w:2 * w + 2, :],
                                   PS[:, 1024 * w:1024 * w + 1024].rearrange("p (a b) -> p a b", a=2),
                                   ACT.Exp, scale=float(1.0 / np.sqrt(HD))).then_inc(s_exp, 1)

                iteration(-1, 1, True)
                iteration(0, 0, True)
                with act.Fori(0, (LOOP_HI - 1) // 2) as i:
                    iteration(i * 2 + 1, 1, False)
                    iteration(i * 2 + 2, 0, False)
                for i in range(LOOP_HI, NG + 1):
                    iteration(i, i % 2, True)

            def linear(L):
                deviation(L)

                def front(i, u):
                    transposed_group(L, i, u)
                    n = i * 2 + (u + 1)
                    act.wait_ge(s_lqm, n)
                    act.activation(LQE[:, u], LQM[:, u], ACT.Exp).then_inc(s_lqe, 1)
                    act.wait_ge(s_lk, n)
                    if not (isinstance(i, int) and i == 0):
                        act.wait_ge(s_kv, n - 2)
                    act.activation(LV[:, u, :, 0:D],
                                   PS[:, 1024:2048].rearrange("p (a b) -> p a b", a=GT)[:, :, D:2 * D],
                                   ACT.Copy).then_inc(s_lv, 1)
                    act.wait_ge(s_lkm, n)
                    act.activation(LKE[:, u], LKM[:, u], ACT.Exp).then_inc(s_lke, 1)

                def back(i, u):
                    n = i * 2 + (u + 1)
                    act.wait_ge(s_la, n)
                    act.activation(LAT[:, u], bank(7), ACT.Copy).then_inc(s_lat, 1)

                front(0, 0)
                front(0, 1)
                back(0, 0)
                with act.Fori(0, NG // 2 - 1) as i:
                    front(i + 1, 0)
                    back(i, 1)
                    front(i + 1, 1)
                    back(i + 1, 0)
                back(NG // 2 - 1, 1)

            for L, kind in enumerate(SUBLAYERS):
                if kind in (FFN0, FFN1):
                    moe(L)
                elif kind == ATTN:
                    attention(L)
                else:
                    linear(L)

        @block.tensor
        def _(pe):
            pe.wait_ge(s_cst, 16)
            pe.wait_ge(s_wt, 16)

            def transpose_group(L, i, u):
                pe.wait_ge(s_xs, i * 2 + (NG * L + u + 1))
                for j in range(GT):
                    mm = pe.transpose(bank(u, P * j, P * j + P), XS[:, u, j, :], ident)
                mm.then_inc(s_tr, 1)

            def moe(L):
                f = ffn_of(L)
                m, T0 = moe_of(f), TILES0[ffn_of(L)]
                E, S, tiles = m["E"], m["S"], m["tiles"]
                wr = wt("r0" if SUBLAYERS[L] == FFN0 else "r1")
                N = S * P

                def logits(i, u):
                    pe.wait_ge(s_xt, i * 2 + (NG * L + u + 1))
                    if not (isinstance(i, int) and i == 0):
                        pe.wait_ge(s_lgc, i * 2 + (NG * f + u - 1))
                    for j in range(GT):
                        mm = pe.matmul(bank(2 + u, E * j, E * j + E), XT[:, u, P * j:P * j + P], wr,
                                       start=True, stop=True)
                    mm.then_inc(s_lg, 1)

                def ranks(i, u):
                    pe.wait_ge(s_mask, i * 2 + (NG * f + u + 1))
                    m_ = MB[:, u].rearrange("p a b -> p (a b)")[:, 0:GT * E]
                    pe.matmul(bank(4 + u, 0, GT * E), before_bf[:, :], m_, start=True, stop=False)
                    for j in range(GT - 1):
                        pe.matmul(bank(4 + u, E * (j + 1), E * GT).rearrange("p (a b) -> p a b", b=E), ones_bf[:, :],
                                  m_[:, E * j:E * j + E].unsqueeze(1).to_broadcast((P, GT - 1 - j, E)),
                                  start=False, stop=False)
                    pe.matmul(bank(4 + u, 0, GT * E).rearrange("p (a b) -> p a b", b=E), ones_bf[:, :],
                              SUM[:, u, 0:E].unsqueeze(1).to_broadcast((P, GT, E)), start=False, stop=True)\
                      .then_inc(s_rank, 1)

                def step(i, u):
                    ranks(i, u)
                    if not (isinstance(i, int) and i == NG // 2 - 1):
                        transpose_group(L, i + 1, u)
                    if not (isinstance(i, int) and i == NG // 2 - 1 and u == 1):
                        logits(i + u, 1 - u)

                transpose_group(L, 0, 0)
                transpose_group(L, 0, 1)
                logits(0, 0)
                step(0, 0)
                step(0, 1)
                with pe.Fori(1, NG // 2 - 1) as i:
                    step(i, 0)
                    step(i, 1)
                step(NG // 2 - 1, 0)
                step(NG // 2 - 1, 1)
                if S == S0:
                    pe.wait_ge(s_sum, first_kind(f) + 1)
                    pe.matmul(bank(6, 0, E), ones_bf[:, :], SUM[:, 0, 0:E], start=True, stop=True).then_inc(s_counts, 1)
                    pe.wait_ge(s_tiles, first_kind(f) + 1)
                pe.wait_ge(s_slot, NG * (f + 1))

                def turn(i, c):
                    tau, r = i * RING + c, c % RING
                    pe.wait_ge(s_xp[r], i * 16 + 16 * (rounds0(f, r) + c // RING + 1))
                    if not (isinstance(i, int) and i == 0 and c == 0):
                        pe.wait_ge(s_xpc, T0 + tau)
                    for s in range(S):
                        mm = pe.transpose(bank(4, P * s, P * s + P), XP[:, r, s, 0:D], ident)
                    mm.then_inc(s_xpt, 1)

                def hidden(i, c):
                    tau, r = i * RING + c, c % RING
                    pe.wait_ge(s_we[r], i * 16 + 16 * (rounds0(f, r) + c // RING + 1))
                    pe.wait_ge(s_xpc, T0 + tau + 1)
                    for q in range(FC):
                        if not (isinstance(i, int) and i == 0 and c == 0 and q < 2):
                            pe.wait_ge(s_g, tau * FC + (T0 * FC + q - 1))
                        for a in range(0, N, 512):
                            b = min(N, a + 512)
                            mm = pe.matmul(PS[:, 1024 * (q % 2) + a:1024 * (q % 2) + b],
                                           WE[:, r, q * P:q * P + P], XPT[:, c % PAIR, a:b], start=True, stop=True)
                        mm.then_inc(s_h, 1)

                def outputs(i, c):
                    tau, r = i * RING + c, c % RING
                    pe.wait_ge(s_g, tau * FC + (T0 * FC + FC))
                    if not (isinstance(i, int) and i == 0 and c == 0):
                        pe.wait_ge(s_yc, T0 + tau)
                    for s in range(S):
                        for q in range(FC):
                            mm = pe.matmul(PS[:, 3072 + P * s:3072 + P * s + P], HT[:, c % PAIR, q, P * s:P * s + P],
                                           WE[:, r, DFF + q * D:DFF + q * D + D], start=(q == 0), stop=(q == FC - 1))
                    mm.then_inc(s_y, 1)

                turn(0, 0)
                turn(0, 1)
                hidden(0, 0)
                whole = (tiles - 2) // RING

                def steps(i):
                    for c in range(1, RING + 1):
                        turn(i, c + 1)
                        hidden(i, c)
                        outputs(i, c - 1)

                steps(0)
                with pe.Fori(1, whole) as i:
                    steps(i)
                for c in range(RING * whole + 1, tiles + 1):
                    if c + 1 < tiles:
                        turn(0, c + 1)
                    if c < tiles:
                        hidden(0, c)
                    outputs(0, c - 1)

            def attention(L):
                def front(i, u):
                    pe.wait_ge(s_xt, i * 2 + (NG * L + u + 1))
                    first = isinstance(i, int) and i == 0 and u == 0
                    for n, w in enumerate(("wq", "wqr", "wk", "wkr")):
                        if not first:
                            pe.wait_ge(s_rope, i * 8 + (4 * u + n - 3))
                        pe.matmul(bank(2 + n), wt(w), XT[:, u, :], start=True, stop=True).then_inc(s_proj, 1)
                    if not first:
                        pe.wait_ge(s_va, i * 2 + u)
                    for j in range(GT):
                        mm = pe.matmul(bank(6, P * j, P * j + P), XT[:, u, P * j:P * j + P], wt("wv"),
                                       start=True, stop=True)
                    mm.then_inc(s_proj, 1)

                transpose_group(L, 0, 0)
                transpose_group(L, 0, 1)
                front(0, 0)
                with pe.Fori(0, NG // 2 - 1) as i:
                    transpose_group(L, i + 1, 0)
                    front(i, 1)
                    transpose_group(L, i + 1, 1)
                    front(i + 1, 0)
                front(NG // 2 - 1, 1)
                pe.wait_ge(s_va, NG + 1)

                def iteration(i, par, peeled):
                    has_m = not peeled or i + 1 < NG
                    has_e = not peeled or 0 <= i < NG
                    for s in range(HEADS):
                        g, j = s // 4, s % 4
                        if has_e and j == 0:
                            pe.wait_ge(s_nmi[g], i * 32 + 32)
                        if has_e:
                            scores(i, par, s, 0)
                        if has_m:
                            if j == 0:
                                pe.wait_ge(s_st[1 - par][g], half(i, 1, par) * LOADS)
                            maxima(i, par, s, 0)
                            maxima(i, par, s, 1)
                        if has_e:
                            scores(i, par, s, 1)
                        if has_m:
                            maxima(i, par, s, 2)
                            maxima(i, par, s, 3)
                        if not peeled or 0 <= 4 * i + g - 1 < 4 * NG:
                            weigh(i, par, g, j, peeled)
                        misc(i, par, s, peeled)

                def half(i, ahead, par):
                    if isinstance(i, int):
                        return (i + ahead) // 2 + 1
                    return HALF[0] + (1 if (par == 1 and ahead == 1) else 0)

                def scores(i, par, s, w):
                    if not (isinstance(i, int) and i == 0 and s == 0):
                        pe.wait_ge(s_exp, i * 32 + (2 * s + w - 1))
                    for k in range(2 * w, 2 * w + 2):
                        mm = pe.matmul(bank(k), KS[0:STACK, par, s, P * k:P * k + P], QS[0:STACK, par, s, :],
                                       start=True, stop=True)
                    mm.then_inc(s_e, 1)

                def maxima(i, par, s, a):
                    if not (isinstance(i, int) and i == -1 and s == 0 and a < 2):
                        pe.wait_ge(s_mr, i * 64 + (64 + 4 * s + a - 1))
                    pe.matmul(bank(4 + a % 2), QS[0:STACK, 1 - par, s, P * a:P * a + P], KS[0:STACK, 1 - par, s, :],
                              start=True, stop=True).then_inc(s_m, 1)

                def weigh(i, par, g, k, peeled):
                    gg = (g - 1) % 4
                    vpar = par if g else 1 - par
                    if k == 0:
                        pe.wait_ge(s_exp, i * 32 + 8 * g)
                        if not (peeled and 4 * i + g - 1 == 0):
                            pe.wait_ge(s_ot, i * 4 + g - 1)
                        if g == 1:
                            pe.wait_ge(s_vb, i + 1)
                    for j in range(4):
                        h = 4 * gg + j
                        mm = pe.matmul(bank(6)[32 * j:32 * j + HD + 1, :], VB[:, vpar, k, h, :],
                                       PT[:, gg % 2, j, k, :], start=(k == 0), stop=(k == GT - 1))
                    if k == GT - 1:
                        mm.then_inc(s_av, 1)

                def misc(i, par, s, peeled):
                    g, j = s // 4, s % 4

                    def earlier(what, n):
                        n_int = n if isinstance(n, int) else None
                        if n_int is None or n_int > 0:
                            pe.wait_ge(what, n)

                    def clamp(n, top):
                        return max(0, min(n, top)) if isinstance(n, int) else n

                    if j == 1:
                        if peeled and not 0 <= 4 * i + g - 2 < 4 * NG:
                            return
                        G = i * 4 + (g - 2)
                        earlier(s_nmt, clamp(i * 4 + g + 3, 4 * NG))
                        earlier(s_td, G)
                        if g == 2:
                            earlier(s_at, clamp(i, NG))
                        if g == 3:
                            earlier(s_od, clamp(i, NG))
                        pe.wait_ge(s_ot, G + 1)
                        for a in range(GT):
                            mm = pe.transpose(bank(7, P * a, P * a + P), OT[:, P * a:P * a + P], ident)
                        mm.then_inc(s_tp, 1)
                    if j == 2:
                        b, gg = (i, 3) if g == 0 else (i + 1, g - 1)
                        if peeled and not 0 <= b < NG:
                            return
                        earlier(s_td, clamp(i * 4 + (g - 1), 4 * NG))
                        earlier(s_nmt, b * 4 + gg)
                        pe.wait_ge(s_nmf, b * 4 + gg + 1)
                        pe.transpose(bank(7, 0, P)[0:32, :], NMF.rearrange("p a b -> p (a b)"), ident)\
                            .then_inc(s_nmp, 1)
                    if s in (7, 11) and (not peeled or 0 <= i - 1 < NG):
                        earlier(s_nmt, clamp(i * 4 + g + 4, 4 * NG))
                        earlier(s_td, clamp(i * 4 + (g - 1), 4 * NG))
                        if s == 7:
                            for a in range(GT):
                                mm = pe.transpose(bank(7, P * a, P * a + P), AO[:, a, :], ident)
                            mm.then_inc(s_ap, 1)
                        else:
                            pe.wait_ge(s_at, i)
                            for a in range(GT):
                                mm = pe.matmul(bank(7, P * a, P * a + P), AT[:, P * a:P * a + P], wt("wo"),
                                               start=True, stop=True)
                            mm.then_inc(s_op, 1)

                HALF = [0]
                iteration(-1, 1, True)
                iteration(0, 0, True)
                with pe.Fori(0, (LOOP_HI - 1) // 2) as i:
                    HALF[0] = i + 1
                    iteration(i * 2 + 1, 1, False)
                    HALF[0] = i + 2
                    iteration(i * 2 + 2, 0, False)
                for i in range(LOOP_HI, NG + 1):
                    iteration(i, i % 2, True)

            def linear(L):
                KVb = PS[:, 1024:2048].rearrange("p (a b) -> p a b", a=GT)

                def f1(i, u):
                    transpose_group(L, i, u)

                def f2(i, u):
                    n = i * 2 + (u + 1)
                    pe.wait_ge(s_xt, n + NG * L)
                    pe.matmul(bank(4), wt("lq"), XT[:, u, :], start=True, stop=True).then_inc(s_lq, 1)

                def f3(i, u):
                    n = i * 2 + (u + 1)
                    if not (isinstance(i, int) and i == 0 and u == 0):
                        pe.wait_ge(s_lv, n - 1)
                        pe.wait_ge(s_lkf, n - 1)
                    for j in range(GT):
                        mm = pe.matmul(KVb[:, j, :], XT[:, u, P * j:P * j + P], wt("lkv"), start=True, stop=True)
                    mm.then_inc(s_lk, 1)

                def b1(i, u):
                    n = i * 2 + (u + 1)
                    pe.wait_ge(s_lkf, n)
                    pe.wait_ge(s_lv, n)
                    pe.wait_ge(s_lqf, n)
                    for j in range(GT):
                        mm = pe.matmul(bank(4, 0, D + 1), LKF[:, u, j, :], LV[:, u, j, :],
                                       start=(j == 0), stop=(j == GT - 1))
                    mm.then_inc(s_kv, 1)

                def b2(i, u):
                    n = i * 2 + (u + 1)
                    pe.wait_ge(s_bd, n)
                    for j in range(GT):
                        mm = pe.matmul(PS[:, 2560 + 256 * j:2560 + 256 * j + D + HEADS],
                                       LQF[:, u, P * j:P * j + P], BD[:, u, :], start=True, stop=True)
                    mm.then_inc(s_ln, 1)

                def b3(i, u):
                    n = i * 2 + (u + 1)
                    pe.wait_ge(s_lao, n)
                    for j in range(GT):
                        mm = pe.transpose(bank(7, P * j, P * j + P), LAO[:, u, j, :], ident)
                    mm.then_inc(s_la, 1)

                def b4(i, u):
                    n = i * 2 + (u + 1)
                    pe.wait_ge(s_lat, n)
                    for j in range(GT):
                        mm = pe.matmul(bank(7, P * j, P * j + P), LAT[:, u, P * j:P * j + P], wt("lo"),
                                       start=True, stop=True)
                    mm.then_inc(s_lo2, 1)

                def both(i, u, i2, u2):
                    f1(i, u)
                    b1(i2, u2)
                    pe.wait_ge(s_bd, i2 * 2 + (u2 + 1))
                    f2(i, u)
                    b2(i2, u2)
                    f3(i, u)
                    if not (isinstance(i2, int) and i2 == 0 and u2 == 0):
                        pe.wait_ge(s_lres, i2 * 2 + u2)
                    b3(i2, u2)
                    b4(i2, u2)

                f1(0, 0)
                f2(0, 0)
                f3(0, 0)
                both(0, 1, 0, 0)
                with pe.Fori(0, NG // 2 - 1) as i:
                    both(i + 1, 0, i, 1)
                    both(i + 1, 1, i + 1, 0)
                i = NG // 2 - 1
                b1(i, 1)
                b2(i, 1)
                pe.wait_ge(s_lres, NG - 1)
                b3(i, 1)
                b4(i, 1)

            for L, kind in enumerate(SUBLAYERS):
                if kind in (FFN0, FFN1):
                    moe(L)
                elif kind == ATTN:
                    attention(L)
                else:
                    linear(L)

        @block.vector
        def _(dve):
            chain = Chain(dve, s_dve)

            def group_stats(t0):
                for j in range(GT):
                    ins = dve.bn_stats(BST[:, bass.ds(t0 + j, 1), :].rearrange("p a b -> p (a b)"),
                                       X[:, bass.ds(t0 + j, 1), :].rearrange("p a b -> p (a b)"))
                return ins

            def finish_stats(L):
                me, m2e, mo, m2o = BST[:, :, 1], BST[:, :, 2], BST[:, :, 4], BST[:, :, 5]
                a = [LN[:, k, :] for k in range(12)]
                dve.tensor_tensor(a[2], me, mo, ALU.add).then_inc(s_dve, 1)
                dve.tensor_tensor(a[3], me, mo, ALU.subtract).then_inc(s_dve, 1)
                dve.tensor_tensor(a[4], m2e, m2o, ALU.add).then_inc(s_dve, 1)
                chain.n += 3
                dve.wait_ge(s_dve, chain.n)
                chain(dve.tensor_scalar(a[0], a[2], 0.5, None, ALU.mult))
                chain(dve.tensor_tensor(a[5], a[3], a[3], ALU.mult))
                chain(dve.scalar_tensor_tensor(out=a[8], in0=a[5], scalar=D / 4.0, in1=a[4],
                                               op0=ALU.mult, op1=ALU.add))
                dve.tensor_scalar(a[6], a[8], 1.0 / D, LN_EPS, ALU.mult, ALU.add).then_inc(s_var, 1)
                dve.wait_ge(s_var, L + 1)
                dve.wait_ge(s_sd, L + 1)
                chain(dve.reciprocal(a[9], a[7]))
                chain(dve.tensor_tensor(a[10], a[9], a[9], ALU.mult))
                chain(dve.tensor_tensor(a[11], a[10], a[6], ALU.mult))
                chain(dve.tensor_scalar(a[10], a[11], -0.5, 1.5, ALU.mult, ALU.add))
                chain(dve.tensor_tensor(a[1], a[9], a[10], ALU.mult))

            def normalise(L, i, u, *waits):
                for s, n in waits:
                    dve.wait_ge(s, n)
                for j in range(GT):
                    t = i * (2 * GT) + (GT * u + j)
                    ins = dve.tensor_scalar(XS[:, u, j, :], X[:, bass.ds(t, 1), :].rearrange("p a b -> p (a b)"),
                                            MEAN[:, bass.ds(t, 1)], RSTD[:, bass.ds(t, 1)],
                                            ALU.subtract, ALU.mult)
                ins.then_inc(s_xs, 1)

            def moe(L):
                f = ffn_of(L)
                m, T0 = moe_of(f), TILES0[ffn_of(L)]
                E, S, tiles = m["E"], m["S"], m["tiles"]
                tag = TAG * (f + 1)
                rb = wt("rb0" if SUBLAYERS[L] == FFN0 else "rb1").rearrange("p (a b) -> p a b", a=GT)
                for k in range(2):
                    dve.tensor_scalar(XR[:, k, :, D], cst("tokid"), tag + k * TOKENS, None, ALU.add)\
                       .then_inc(s_dve, 1)
                    chain.n += 1

                def norm(i, u):
                    if isinstance(i, int) and i == 0:
                        normalise(L, i, u)
                    else:
                        n = i * 2 + (u - 1)
                        normalise(L, i, u, (s_tr, n + NG * L), (s_row, n + NG * f))

                lg = LG[:, :, 0:E]
                w = [RT[k][:, :, 0:E] for k in range(3)]
                oh = [OH[:, k, :, 0:E] for k in range(2)]
                r = [R1[:, k, :] for k in range(20)]

                def every(name):
                    return cst(name)[:, 0:E].unsqueeze(1).to_broadcast((P, GT, E))

                def choose(i, u, steps):
                    t0 = i * (2 * GT) + GT * u

                    def best(k, scores):
                        m_, i_ = r[k][:, bass.ds(t0, GT)], r[2 + k][:, bass.ds(t0, GT)]
                        steps(dve.tensor_reduce(m_, scores, AX_X, ALU.max))
                        steps(dve.tensor_tensor(w[0], scores, m_.unsqueeze(2).to_broadcast((P, GT, E)), ALU.is_equal))
                        steps(dve.tensor_tensor(w[1], w[0], every("eoff"), ALU.mult))
                        steps(dve.tensor_reduce(i_, w[1], AX_X, ALU.min))
                        steps(dve.tensor_tensor(oh[k], every("eoff"), i_.unsqueeze(2).to_broadcast((P, GT, E)),
                                                ALU.is_equal))

                    n = i * 2 + (NG * f + u + 1)
                    dve.wait_ge(s_lg, n)
                    dve.tensor_tensor(lg, bank(2 + u, 0, GT * E).rearrange("p (a b) -> p a b", a=GT), rb, ALU.add)\
                       .then_inc(s_lgc, 1)
                    dve.wait_ge(s_lgc, n)
                    best(0, lg)
                    steps(dve.scalar_tensor_tensor(out=w[2], in0=oh[0], scalar=NEG, in1=lg,
                                                   op0=ALU.mult, op1=ALU.add))
                    best(1, w[2])
                    m_ = MB[:, u].rearrange("p a b -> p (a b)")[:, 0:GT * E].rearrange("p (a b) -> p a b", a=GT)
                    dve.tensor_tensor(m_, oh[0], oh[1], ALU.add).then_inc(s_mask, 1)
                    dve.wait_ge(s_mask, n)
                    steps(dve.tensor_reduce(SUMF[:, 0:E], m_.rearrange("p a b -> p b a"), AX_X, ALU.add))
                    steps(dve.tensor_tensor(SUM[:, 1 - u, 0:E], SUM[:, u, 0:E], SUMF[:, 0:E], ALU.add))

                def place(i, u, steps):
                    t0 = i * (2 * GT) + GT * u
                    dve.wait_ge(s_rank, i * 2 + (NG * f + u + 1))
                    steps(dve.tensor_tensor(w[0], bank(4 + u, 0, GT * E).rearrange("p (a b) -> p a b", a=GT),
                                            every("region"), ALU.add))
                    steps(dve.tensor_tensor(PL[:, :, :, 0:E], OH[:, :, :, 0:E],
                                            w[0].unsqueeze(1).to_broadcast((P, 2, GT, E)), ALU.mult))
                    steps(dve.tensor_reduce(R1[:, 9:11, bass.ds(t0, GT)], PL[:, :, :, 0:E], AX_X, ALU.add))
                    dve.tensor_copy(SLOT[:, :, bass.ds(t0, GT)], R1[:, 9:11, bass.ds(t0, GT)]).then_inc(s_slot, 1)

                chain(dve.memset(SUM[:, 0], 0.0))
                norm(0, 0)
                norm(0, 1)
                with dve.Fori(0, NG // 2 - 1) as i:
                    chain.loop(i, 2 * (5 + 1 + 5 + 2 + 3))
                    for u in range(2):
                        choose(i, u, chain)
                        norm(i + 1, u)
                        place(i, u, chain)
                    chain.ended(NG // 2 - 1)
                for u in range(2):
                    choose(NG // 2 - 1, u, chain)
                    place(NG // 2 - 1, u, chain)

                if E == E0:
                    dve.tensor_copy(RE[:, 7, 0:1], cst("ones")[:, 0:1]).then_inc(s_sum, 1)
                    dve.wait_ge(s_counts, first_kind(f) + 1)
                    n_e = bank(6, 0, E)
                    chain(dve.tensor_tensor(JT[:, :, :], n_e.unsqueeze(2).to_broadcast((P, E, 16)),
                                            cst("jtab").rearrange("p (a b) -> p a b", a=E), ALU.is_gt))
                    dve.tensor_tensor(CNT[:, :], n_e, cst("region")[:, 0:E], ALU.add).then_inc(s_dve, 1)
                    chain.n += 1
                    chain(dve.tensor_reduce(RE[:, 0, :], JT[:, :, :], AX_X, ALU.add))
                    chain(dve.tensor_tensor_scan(RE[:, 1, :], cst("ones")[:, 0:E], RE[:, 0, :], 0.0,
                                                 ALU.mult, ALU.add))
                    chain(dve.tensor_scalar(RE[:, 2, :], RE[:, 0, :], -float(S * P), float(REGION),
                                            ALU.mult, ALU.add))
                    chain(dve.tensor_tensor(TT[:, :, :], cst("tiletab").rearrange("p (a b) -> p a b", b=E),
                                            RE[:, 1, :].unsqueeze(1).to_broadcast((P, tiles, E)), ALU.is_ge))
                    chain(dve.tensor_tensor(TW[:, :, :], TT[:, :, :],
                                            RE[:, 2, :].unsqueeze(1).to_broadcast((P, tiles, E)), ALU.mult))
                    chain(dve.tensor_reduce(ETF[:, :], TT[:, :, :], AX_X, ALU.add))
                    chain(dve.tensor_scalar(ET[:, :], ETF[:, :], float(E - 1), None, ALU.min))
                    chain(dve.tensor_reduce(TSF[:, 0, :], TW[:, :, :], AX_X, ALU.add))
                    dve.tensor_tensor(TS[:, :], TSF[:, 0, :], cst("tilerow"), ALU.add).then_inc(s_tiles, 1)

                dve.tensor_tensor(r[4], r[1], r[0], ALU.subtract).then_inc(s_gap, 1)
                dve.wait_ge(s_ex, f + 1)
                chain(dve.tensor_scalar(r[6], r[5], 1.0, None, ALU.add))
                chain(dve.reciprocal(r[7], r[6]))
                chain(dve.tensor_tensor(r[8], r[5], r[7], ALU.mult))
                gates = [r[7], r[8]]
                if E == E0:
                    for k in range(2):
                        chain(dve.tensor_scalar(GATE[:, k, :], gates[k], 0.5, None, ALU.mult))
                else:
                    for k in range(2):
                        chain(dve.tensor_scalar(r[13], r[2 + k], 64.0, float(REGION), ALU.add, ALU.mult))
                        chain(dve.tensor_tensor(r[14], r[9 + k], r[13], ALU.subtract))
                        chain(dve.tensor_scalar(r[11 + k], r[14], float(CAPACITY), None, ALU.is_lt))
                        chain(dve.tensor_tensor(r[17 + k], gates[k], r[11 + k], ALU.mult))
                    chain(dve.tensor_tensor(r[13], r[17], r[18], ALU.add))
                    chain(dve.tensor_scalar(r[14], r[13], 1e-9, None, ALU.add))
                    chain(dve.reciprocal(r[15], r[14]))
                    for k in range(2):
                        chain(dve.scalar_tensor_tensor(out=GATE[:, k, :], in0=r[17 + k], scalar=0.5, in1=r[15],
                                                       op0=ALU.mult, op1=ALU.mult))

                def tile_in(i, c):
                    tau = i * RING + c
                    dve.wait_ge(s_xpt, T0 + tau + 1)
                    if not (isinstance(i, int) and i == 0 and c < PAIR):
                        dve.wait_ge(s_h, (tau - (PAIR - 1)) * FC + T0 * FC)
                    dve.tensor_copy(XPT[:, c % PAIR, 0:S * P], PS[:, 2048:2048 + S * P]).then_inc(s_xpc, 1)

                def tile_out(i, c, steps):
                    tau, r_ = i * RING + c, c % RING
                    if not (isinstance(i, int) and i == 0 and c < RING):
                        dve.wait_ge(s_yo[r_], i * (16 * S) + 16 * S * (c // RING) + scattered0(f, r_))
                    idf = XP[:, r_, 0:S, D]
                    trash = cst("trash")[:, bass.ds(tau * S, S)]
                    a = [IDF[:, r_, k, 0:S] for k in range(3)]
                    dve.tensor_scalar(a[0], idf, tag, None, ALU.is_ge).then_inc(s_dve, 1)
                    steps.n += 1
                    steps(dve.scalar_tensor_tensor(out=a[1], in0=idf, scalar=tag, in1=trash,
                                                   op0=ALU.subtract, op1=ALU.subtract))
                    steps(dve.tensor_tensor(a[2], a[0], a[1], ALU.mult))
                    steps(dve.tensor_tensor(ID[:, r_, 0:S], a[2], trash, ALU.add))
                    dve.wait_ge(s_y, T0 + tau + 1)
                    dve.tensor_tensor(YS[:, r_, 0:S, :], PS[:, 3072:3072 + S * P].rearrange("p (a b) -> p a b", a=S),
                                      WE[:, r_, WROW - D:WROW].unsqueeze(1).to_broadcast((P, S, D)), ALU.add)\
                       .then_inc(s_yc, 1)

                tile_in(0, 0)
                tile_in(0, 1)
                whole = (tiles - 2) // RING
                for c in range(1, RING + 1):
                    tile_in(0, c + 1)
                    tile_out(0, c - 1, chain)
                with dve.Fori(1, whole) as i:
                    chain.loop(i, RING * 4, 1)
                    for c in range(1, RING + 1):
                        tile_in(i, c + 1)
                        tile_out(i, c - 1, chain)
                    chain.ended(whole - 1)
                for c in range(RING * whole + 1, tiles + 1):
                    if c + 1 < tiles:
                        tile_in(0, c + 1)
                    tile_out(0, c - 1, chain)

                last = L == len(SUBLAYERS) - 1
                with dve.Fori(0, NG // 2) as i:
                    chain.loop(i, 2 if last else 4)
                    for u in range(2):
                        dve.wait_ge(s_yin[u], i * 32 + 32 * (NG // 2 * f + 1))
                        t0 = i * (2 * GT) + GT * u
                        for k in range(2):
                            for j in range(GT):
                                xt = X[:, bass.ds(t0 + j, 1), :].rearrange("p a b -> p (a b)")
                                ins = dve.scalar_tensor_tensor(
                                    out=xt, in0=YC[:, u, k, j, :], scalar=GATE[:, k, bass.ds(t0 + j, 1)],
                                    in1=xt, op0=ALU.mult, op1=ALU.add)
                            if last and k == 1:
                                ins.then_inc(s_comb, 1)
                            else:
                                chain(ins)
                        if not last:
                            group_stats(t0).then_inc(s_comb, 1)
                    chain.ended(NG // 2)
                dve.wait_ge(s_comb, NG * (f + 1))

            def stats_loop():
                with dve.Fori(0, NG) as i:
                    chain.loop(i, 1)
                    chain(group_stats(i * GT))
                    chain.ended(NG)

            def attention(L):
                dve.memset(VA[:, :, :, HD:HD + 1], 1.0).then_inc(s_dve, 1)
                chain.n += 1
                rc, rs = cst("rope_c"), cst("rope_s")

                def norm(i, u):
                    if isinstance(i, int) and i == 0:
                        normalise(L, i, u)
                    else:
                        normalise(L, i, u, (s_tr, i * 2 + (NG * L + u - 1)))

                def rope(i, u):
                    n = i * 10 + 5 * u
                    if not (isinstance(i, int) and i == 0):
                        dve.wait_ge(s_lo, i * 2 + (u - 1))
                    for k, (b0, b1) in enumerate((("bq", "bqr"), ("bk", "bkr"))):
                        dve.wait_ge(s_proj, n + (2 * k + 1))
                        dve.scalar_tensor_tensor(out=QF[:, u, k, :], in0=bank(2 + 2 * k), scalar=wt(b0), in1=rc,
                                                 op0=ALU.add, op1=ALU.mult).then_inc(s_rope, 1)
                        dve.wait_ge(s_proj, n + (2 * k + 2))
                        dve.scalar_tensor_tensor(out=QT[:, k, :], in0=bank(3 + 2 * k), scalar=wt(b1), in1=rs,
                                                 op0=ALU.add, op1=ALU.mult).then_inc(s_rope, 1)
                    dve.wait_ge(s_rope, i * 8 + (4 * u + 4))
                    dve.tensor_tensor(QF[:, u], QF[:, u], QT[:, :, :], ALU.add).then_inc(s_rot, 1)
                    dve.wait_ge(s_proj, n + 5)
                    dve.tensor_tensor(VA[:, bass.ds(i * (2 * GT) + GT * u, GT), :, 0:HD],
                                      bank(6).rearrange("p (t h d) -> p t h d", t=GT, h=HEADS),
                                      wt("bv").rearrange("p (h d) -> p h d", h=HEADS).unsqueeze(1)
                                      .to_broadcast((P, GT, HEADS, HD)), ALU.add).then_inc(s_va, 1)

                norm(0, 0)
                norm(0, 1)
                rope(0, 0)

                def groups(i):
                    norm(i + 1, 0)
                    rope(i, 1)
                    norm(i + 1, 1)
                    rope(i + 1, 0)

                groups(0)
                with dve.Fori(1, NG // 2 - 1) as i:
                    groups(i)
                rope(NG // 2 - 1, 1)
                dve.wait_ge(s_va, NG)
                dve.memset(bank(6), 0.0).then_inc(s_va, 1)

                def iteration(i, par, peeled, steps):
                    has_m = not peeled or i + 1 < NG
                    for s in range(HEADS):
                        g, j = s // 4, s % 4
                        if j == 2 and (not peeled or 0 <= 4 * i + g - 2 < 4 * NG):
                            G = i * 4 + (g - 2)
                            gg = (g - 2) % 4
                            sums = bank(7).rearrange("p (a h r) -> p a h r", a=GT, h=4)
                            dve.wait_ge(s_tp, G + 1)
                            steps(dve.reciprocal(RD[:, :, :], sums[:, :, :, HD]))
                            if gg == 0 and not (peeled and 4 * i + g - 2 < 4):
                                dve.wait_ge(s_ap, i)
                            dve.tensor_tensor(AO.rearrange("p a (h d) -> p a h d", h=HEADS)[:, :, 4 * gg:4 * gg + 4, :],
                                              sums[:, :, :, 0:HD],
                                              RD.unsqueeze(3).to_broadcast((P, GT, 4, HD)), ALU.mult)\
                               .then_inc(s_td, 1)
                        if s == 12 and (not peeled or 0 <= i - 1 < NG):
                            dve.wait_ge(s_op, i)
                            xb = X[:, bass.ds(i * GT - GT, GT), :]
                            steps(dve.tensor_tensor(xb, bank(7).rearrange("p (a b) -> p a b", a=GT), xb, ALU.add))
                            dve.tensor_tensor(xb, xb, wt("bo").unsqueeze(1).to_broadcast((P, GT, D)), ALU.add)\
                               .then_inc(s_od, 1)
                        if has_m:
                            for a in range(GT):
                                dve.wait_ge(s_m, i * 64 + (64 + 4 * s + a + 1))
                                dve.tensor_reduce(MX[:, 0, s, a:a + 1], bank(4 + a % 2), AX_X, ALU.max)\
                                   .then_inc(s_mr, 1)
                            if j == 3:
                                mx = MX[:, 0, 4 * g:4 * g + 4, :].rearrange("p a b -> p (a b)")
                                dve.wait_ge(s_mr, i * 64 + (64 + 4 * s + 4))
                                if not (peeled and i == -1 and g == 0):
                                    dve.wait_ge(s_nmp, i * 4 + 4 + g)
                                steps(dve.tensor_scalar(NMB[:, :], mx, -1.0, None, ALU.mult))
                                steps(dve.tensor_copy(NMF[:, 0, :], NMB[:, :]))
                                dve.scalar_tensor_tensor(out=NMF[:, 1, :], in0=mx, scalar=-1.0, in1=NMB[:, :],
                                                         op0=ALU.mult, op1=ALU.subtract).then_inc(s_nmf, 1)

                iteration(-1, 1, True, chain)
                iteration(0, 0, True, chain)
                with dve.Fori(0, (LOOP_HI - 1) // 2) as i:
                    chain.loop(i, 2 * (4 + 1 + 8))
                    iteration(i * 2 + 1, 1, False, chain)
                    iteration(i * 2 + 2, 0, False, chain)
                    chain.ended((LOOP_HI - 1) // 2)
                for i in range(LOOP_HI, NG + 1):
                    iteration(i, i % 2, True, chain)
                dve.wait_ge(s_od, NG)

            def linear(L):
                KVb = PS[:, 1024:2048].rearrange("p (a b) -> p a b", a=GT)
                dve.memset(LV[:, :, :, D:D + 1], 1.0).then_inc(s_dve, 1)
                chain.n += 1

                def f1(i, u):
                    if isinstance(i, int) and i == 0:
                        normalise(L, i, u)
                    else:
                        normalise(L, i, u, (s_tr, i * 2 + (NG * L + u - 1)))

                def f2(i, u):
                    n = i * 2 + (u + 1)
                    dve.wait_ge(s_lq, n)
                    if not (isinstance(i, int) and i == 0):
                        dve.wait_ge(s_ln, n - 2)
                    dve.tensor_scalar(LQM[:, u], bank(4), 0.0, None, ALU.min).then_inc(s_lqm, 1)
                    dve.wait_ge(s_lqe, n)
                    dve.scalar_tensor_tensor(out=LQF[:, u], in0=bank(4), scalar=0.0, in1=LQE[:, u],
                                             op0=ALU.max, op1=ALU.add).then_inc(s_lqf, 1)

                def f3(i, u):
                    n = i * 2 + (u + 1)
                    dve.wait_ge(s_lk, n)
                    dve.wait_ge(s_lv, n)
                    dve.tensor_scalar(LKM[:, u], KVb[:, :, 0:D], 0.0, None, ALU.min).then_inc(s_lkm, 1)
                    dve.wait_ge(s_lke, n)
                    dve.scalar_tensor_tensor(out=LKF[:, u], in0=KVb[:, :, 0:D], scalar=0.0, in1=LKE[:, u],
                                             op0=ALU.max, op1=ALU.add).then_inc(s_lkf, 1)

                def b1(i, u):
                    n = i * 2 + (u + 1)
                    dve.wait_ge(s_kv, n)
                    dve.tensor_tensor(BD[:, u, 0:D], bank(4, 0, D), cst("blockmask"), ALU.mult)
                    dve.tensor_scalar(BD[:, u, D:D + HEADS], cst("headmask"), bank(4, D, D + 1), None, ALU.mult)\
                       .then_inc(s_bd, 1)

                def b2(i, u, steps):
                    n = i * 2 + (u + 1)
                    num = PS[:, 2560:2560 + 256 * GT].rearrange("p (a b) -> p a b", a=GT)
                    dve.wait_ge(s_ln, n)
                    steps(dve.tensor_scalar(LDN[:, u], num[:, :, D:D + HEADS], 1e-6, None, ALU.add))
                    steps(dve.reciprocal(LRD[:, u], LDN[:, u]))
                    dve.tensor_tensor(LAO[:, u].rearrange("p a (h d) -> p a h d", h=HEADS),
                                      num[:, :, 0:D].rearrange("p a (h d) -> p a h d", h=HEADS),
                                      LRD[:, u].unsqueeze(3).to_broadcast((P, GT, HEADS, HD)), ALU.mult)\
                       .then_inc(s_lao, 1)

                def b4(i, u, steps):
                    n = i * 2 + (u + 1)
                    dve.wait_ge(s_lo2, n)
                    t0 = i * (2 * GT) + GT * u
                    xb = X[:, bass.ds(t0, GT), :]
                    dve.tensor_tensor(xb, bank(7).rearrange("p (a b) -> p a b", a=GT), xb, ALU.add)\
                       .then_inc(s_lres, 1)
                    dve.wait_ge(s_lres, n)
                    steps(group_stats(t0))

                def both(i, u, i2, u2, steps):
                    f1(i, u)
                    b1(i2, u2)
                    f2(i, u)
                    b2(i2, u2, steps)
                    f3(i, u)
                    b4(i2, u2, steps)

                f1(0, 0)
                f2(0, 0)
                f3(0, 0)
                both(0, 1, 0, 0, chain)
                with dve.Fori(0, NG // 2 - 1) as i:
                    chain.loop(i, 6)
                    both(i + 1, 0, i, 1, chain)
                    both(i + 1, 1, i + 1, 0, chain)
                    chain.ended(NG // 2 - 1)
                i = NG // 2 - 1
                b1(i, 1)
                b2(i, 1, chain)
                b4(i, 1, chain)

            dve.wait_ge(s_cst, 16)
            dve.tensor_copy(before_bf[:, :], cst("before"))
            chain(dve.tensor_copy(ones_bf[:, :], cst("ones")))
            n = NT // XCHUNKS
            for c in range(XCHUNKS):
                dve.wait_ge(s_x[c], 16)
                with dve.Fori(0, n // GT) as i:
                    chain.loop(i, 1)
                    chain(group_stats(i * GT + n * c))
                    chain.ended(n // GT)
            dve.wait_ge(s_wt, 16)
            for L, kind in enumerate(SUBLAYERS):
                finish_stats(L)
                if kind in (FFN0, FFN1):
                    moe(L)
                elif kind == ATTN:
                    attention(L)
                    stats_loop()
                else:
                    linear(L)
            dve.tensor_copy(RE[:, 7, 0:1], cst("ones")[:, 0:1]).then_inc(s_final, NG)


CLEARED = 16 * (E1 + SPARE // (S0 * P) + 1)
LOOP_HI = NG - 1
STORES = 16 * 3
LOADS = 16 * (2 * PARTS + 1)


def kernel(**inputs):
    import concourse.bacc as _bacc
    from concourse import mybir as _mybir
    from concourse.bass_utils import run_bass_kernel_spmd as _run

    a = {k: np.asarray(v) for k, v in inputs.items()}
    turned = (np.arange(D) // HD) * HD + (np.arange(D) + HD // 2) % HD

    def column(v):
        return v.reshape(P, 1)

    def every(v, n=1):
        return np.broadcast_to(np.tile(v.reshape(1, -1), (1, n)), (P, v.size * n))

    by_dim = np.arange(D).reshape(HEADS, HD).T.reshape(-1)
    rotated = turned[by_dim]

    parts = {
        "wq": a["L0_attn_Wq"][by_dim].T, "wqr": a["L0_attn_Wq"][rotated].T,
        "wk": a["L0_attn_Wk"][by_dim].T, "wkr": a["L0_attn_Wk"][rotated].T,
        "wv": a["L0_attn_Wv"].T, "wo": a["L0_attn_Wo"].T,
        "lq": a["L1_attn_Wq"].T, "lkv": np.concatenate([a["L1_attn_Wk"].T, a["L1_attn_Wv"].T], 1),
        "lo": a["L1_attn_Wo"].T, "r0": a["L0_ffn_Wr"], "r1": a["L1_ffn_router_w"].T,
        "bq": column(a["L0_attn_bq"][by_dim]), "bqr": column(a["L0_attn_bq"][rotated]),
        "bk": column(a["L0_attn_bk"][by_dim]), "bkr": column(a["L0_attn_bk"][rotated]),
        "bv": every(a["L0_attn_bv"]), "bo": every(a["L0_attn_bo"]),
        "rb0": every(a["L0_ffn_br"], GT), "rb1": every(a["L1_ffn_router_b"], GT),
    }
    weights = np.ascontiguousarray(np.concatenate([parts[n] for n, _ in WEIGHTS], 1))

    def experts(w1, b1, w2, b2):
        e = w1.shape[0]
        return np.ascontiguousarray(np.concatenate([
            w1,
            w2.reshape(e, FC, P, D).transpose(0, 2, 1, 3).reshape(e, P, FC * D),
            b1.reshape(e, FC, P).transpose(0, 2, 1),
            np.broadcast_to(b2[:, None, :], (e, P, D))], 2))

    arrays = {
        "x": np.ascontiguousarray(a["L0_attn_x"].reshape(TOKENS, D)),
        "constants": constants(),
        "weights": weights,
        "experts0": experts(a["L0_ffn_W1"], a["L0_ffn_b1"], a["L0_ffn_W2"], a["L0_ffn_b2"]),
        "experts1": experts(a["L1_ffn_w1"], a["L1_ffn_b1"], a["L1_ffn_w2"], a["L1_ffn_b2"]),
    }
    nc = _bacc.Bacc("TRN2", target_bir_lowering=False, num_devices=1)
    args = [nc.dram_tensor(n, v.shape, _mybir.dt.from_np(v.dtype), kind="ExternalInput").ap()
            for n, v in arrays.items()]
    out = nc.dram_tensor("out", (TOKENS, D), F32, kind="ExternalOutput").ap()
    build(nc, *args, out)
    r = _run(nc, [arrays], core_ids=[0])
    return r.results[0]["out"].reshape(BATCHES, SEQ, D)
```

```python
from contextlib import ExitStack

import concourse.bass as bass
import numpy as np
from concourse import mybir

ALU = mybir.AluOpType
ACT = mybir.ActivationFunctionType
F32 = mybir.dt.float32
BF16 = mybir.dt.bfloat16
I32 = mybir.dt.int32
U32 = mybir.dt.uint32
AX_X = mybir.AxisListType.X

P = 128
D = 128
BATCHES, SEQ = 8, 512
TOKENS = BATCHES * SEQ
NT = TOKENS // P
GT = SEQ // P
NG = NT // GT
HEADS = 16
HD = D // HEADS
DFF = 512
FC = DFF // P
LN_EPS = 1e-5

CAPACITY = -(-5 * TOKENS * 2 // (4 * 16))
E0, S0 = 8, 2
E1, S1 = 16, CAPACITY // P
MOE = [dict(E=E0, S=S0, tiles=TOKENS * 2 // (S0 * P) + E0 - 1), dict(E=E1, S=S1, tiles=E1)]
assert CAPACITY == S1 * P
SLOTS = max(m["tiles"] * m["S"] * P for m in MOE)
PAIRS = 2 * TOKENS
REGION = TOKENS + S0 * P
SPARE = MOE[0]["tiles"] * S0 * P - PAIRS
ROW = D + 1
TAG = 65536.0
NEG = -3.0e38
WROW = FC * P + FC * D + FC + D

FFN0, ATTN, FFN1, LINATTN = range(4)
SUBLAYERS = [FFN0, ATTN, FFN0, FFN1, LINATTN, FFN1]

PARTS = 3
QK_ROWS = PARTS * PARTS * HD
STACK = 96
M_ROW = QK_ROWS

XCHUNKS = 4
RING = 4
PAIR = 2


def constant_layout():
    at, out = 0, {}
    for name, n in [("ident", P), ("before", P), ("ones", P), ("tokid", NT), ("eoff", E1),
                    ("region", E1), ("jtab", 16), ("tile", MOE[0]["tiles"]),
                    ("tilerow", MOE[0]["tiles"]),
                    ("trash", SLOTS // P), ("blockmask", D), ("headmask", HEADS),
                    ("rope_c", SEQ), ("rope_s", SEQ)]:
        out[name] = (at, n)
        at += n
    return out, at


def constants():
    lay, n = constant_layout()
    c = np.zeros((P, n), np.float32)

    def put(name, v):
        a, w = lay[name]
        c[:, a:a + w] = np.broadcast_to(v, (P, w))

    p = np.arange(P)
    put("ident", np.eye(P))
    put("before", p[:, None] < p[None, :])
    put("ones", 1.0)
    put("tokid", np.arange(NT)[None, :] * P + p[:, None])
    put("eoff", np.arange(E1) - 64.0)
    put("region", np.arange(E1) * REGION)
    put("jtab", np.arange(16) * S0 * P)
    put("tile", np.arange(MOE[0]["tiles"]))
    put("tilerow", np.arange(MOE[0]["tiles"]) * S0 * P)
    put("trash", PAIRS + np.arange(SLOTS // P)[None, :] * P + p[:, None])
    put("blockmask", (p[:, None] // HD) == (p[None, :] // HD))
    put("headmask", (p[:, None] // HD) == np.arange(HEADS)[None, :])
    inv = (1.0 / 10000.0 ** (np.arange(0, HD, 2) / HD)).astype(np.float32)
    ang = (np.arange(SEQ, dtype=np.float32)[:, None] * inv[None, :]).astype(np.float32).astype(np.float64)
    dim = p // HEADS
    ang = ang[:, dim % (HD // 2)].T
    put("rope_c", np.cos(ang))
    put("rope_s", np.sin(ang) * np.where(dim < HD // 2, -1.0, 1.0)[:, None])
    return c


WEIGHTS = [("wq", D), ("wqr", D), ("wk", D), ("wkr", D), ("wv", D), ("wo", D),
           ("lq", D), ("lkv", 2 * D), ("lo", D), ("r0", E0), ("r1", E1),
           ("bq", 1), ("bqr", 1), ("bk", 1), ("bkr", 1), ("bv", D), ("bo", D),
           ("rb0", GT * E0), ("rb1", GT * E1)]


def weight_layout():
    at, out = 0, {}
    for name, n in WEIGHTS:
        out[name] = (at, n)
        at += n
    return out, at


def build(nc, x_in, cst_in, w_in, ex0_in, ex1_in, out):
    CL, CN = constant_layout()
    WL, WN = weight_layout()
    ex_in = [ex0_in, ex1_in]

    ctx = ExitStack()
    with ctx:
        def sb(name, shape, dt=F32):
            return ctx.enter_context(nc.sbuf_tensor(name, shape, dt))

        def sem(name):
            return ctx.enter_context(nc.semaphore(name))

        X = sb("X", [P, NT, D])
        CST = sb("CST", [P, CN])
        WT = sb("WT", [P, WN])
        BST = sb("BST", [P, NT, 6])
        LN = sb("LN", [P, 12, NT])
        MEAN, RSTD = LN[:, 0, :], LN[:, 1, :]
        YC = sb("YC", [P, 2, 2, GT, D])
        GATE = sb("GATE", [P, 2, NT])
        XS = sb("XS", [P, 2, GT, D])
        XT = sb("XT", [P, 2, SEQ])
        PS = ctx.enter_context(nc.psum_tensor("PS", [P, 8 * 512], F32))

        def bank(n, a=0, b=512):
            return PS[:, 512 * n + a:512 * n + b]

        def cst(name):
            a, n = CL[name]
            return CST[:, a:a + n]

        def wt(name):
            a, n = WL[name]
            return WT[:, a:a + n]

        ident = cst("ident")

        ARENA = 157 * 256 + 128
        arena = sb("arena", [P, ARENA])

        class Carver:
            def __init__(self):
                self.at = 0

            def __call__(self, shape, dt=F32, rows=P):
                n = int(np.prod(shape)) * (2 if dt == BF16 else 4)
                assert n % 4 == 0
                n //= 4
                assert self.at + n <= ARENA, (self.at, n)
                v = arena[0:rows, self.at:self.at + n]
                self.at += n
                if dt != F32:
                    v = v.bitcast(dt)
                names = "abcde"[:len(shape)]
                if len(shape) > 1:
                    v = v.rearrange(f"p ({' '.join(names)}) -> p {' '.join(names)}",
                                    **{k: s for k, s in zip(names[:-1], shape[:-1])})
                return v

        cv = Carver()
        XR = cv([2, NT, ROW])
        LG = cv([GT, E1])
        RT = [cv([GT, E1]) for _ in range(3)]
        OH = cv([2, GT, E1])
        PL = cv([2, GT, E1])
        MB = cv([2, GT, E1], BF16)
        SUM = cv([2, E1], BF16)
        SUMF = cv([E1])
        R1 = cv([20, NT])
        SLOT = cv([2, NT], U32)
        RE = cv([8, E0])
        ETF = cv([MOE[0]["tiles"]])
        ET = cv([MOE[0]["tiles"]], I32)
        TT = cv([MOE[0]["tiles"], E0])
        TW = cv([MOE[0]["tiles"], E0])
        TSF = cv([MOE[0]["tiles"]])
        TS = cv([MOE[0]["tiles"]], I32)
        CNT = cv([E0], I32)
        JT = cv([E0, 16])
        WE = cv([RING, WROW])
        XP = cv([RING, S1, ROW])
        XPT = cv([PAIR, S1 * P])
        HT = cv([PAIR, FC, S1 * P])
        YS = cv([RING, S1, D])
        IDF = cv([RING, 3, S1])
        ID = cv([RING, S1], U32)
        cv = Carver()
        QS = cv([2, HEADS, SEQ], BF16)
        KS = cv([2, HEADS, SEQ], BF16)
        at_weights = cv.at
        PT = cv([2, 4, GT, SEQ])
        at_main = cv.at
        VA = cv([NT, HEADS, HD + 1])
        VB = cv([2, GT, HEADS, HD + 1])
        MX = cv([HEADS, GT])
        NMB = cv([4 * GT], BF16)
        NMF = cv([2, 4 * GT])
        NMT = cv([P], BF16)
        OT = cv([SEQ])
        RD = cv([GT, 4])
        AO = cv([GT, D])
        AT = cv([SEQ])
        cv.at = at_weights
        QF = cv([2, 2, SEQ])
        QT = cv([2, SEQ])
        QR = cv([2, 2, SEQ])
        QP = cv([2, PARTS, 2, SEQ], BF16)
        assert cv.at <= at_main
        cv = Carver()
        LQM = cv([2, SEQ])
        LQE = cv([2, SEQ])
        LQF = cv([2, SEQ])
        LKM = cv([2, GT, D])
        LKE = cv([2, GT, D])
        LKF = cv([2, GT, D])
        LV = cv([2, GT, D + 1])
        BD = cv([2, D + HEADS])
        LRD = cv([2, GT, HEADS])
        LDN = cv([2, GT, HEADS])
        LAO = cv([2, GT, D])
        LAT = cv([2, SEQ])
        ZERO = sb("ZERO", [P, S0, ROW])
        ones_bf = sb("ones_bf", [P, P], BF16)
        before_bf = sb("before_bf", [P, P], BF16)

        BUFS = [nc.dram_tensor("dispatched0", (E0 * REGION + SPARE, ROW), F32).ap(),
                nc.dram_tensor("dispatched1", (E1 * REGION, ROW), F32).ap()]
        YK = nc.dram_tensor("expert_out", (PAIRS + SLOTS, D), F32).ap()
        QKD = nc.dram_tensor("qk_parts", (BATCHES, 2, 2 * PARTS - 1, P, SEQ), BF16).ap()
        ZD = nc.dram_tensor("zero_rows", (2, 4 * SEQ), BF16).ap()

        s_x = [sem(f"x_loaded{c}") for c in range(XCHUNKS)]
        s_cst, s_wt = sem("cst_loaded"), sem("weights_loaded")
        s_zero, s_cleared = sem("zeros_made"), sem("scratch_cleared")
        s_dve, s_pool_chain = sem("dve_step"), sem("pool_step")
        s_var, s_sd = sem("variance_ready"), sem("deviation_ready")
        s_xs, s_tr, s_xt = sem("xs_ready"), sem("xs_transposed"), sem("xt_ready")
        s_row = sem("rows_copied")
        s_lg, s_lgc = sem("logits_done"), sem("logits_copied")
        s_gap, s_ex = sem("score_gap_ready"), sem("gap_exp_ready")
        s_sum = sem("choices_summed")
        s_mask, s_rank = sem("chosen_ready"), sem("ranks_done")
        s_counts, s_tiles, s_tails = sem("counts_done"), sem("tiles_ready"), sem("tails_cleared")
        s_slot, s_disp = sem("slots_ready"), sem("rows_dispatched")
        s_xp = [sem(f"tile_rows_in{r}") for r in range(RING)]
        s_we = [sem(f"expert_in{r}") for r in range(RING)]
        s_xpt, s_xpc = sem("tile_transposed"), sem("tile_copied")
        s_h, s_g = sem("hidden_done"), sem("gelu_done")
        s_y, s_yc = sem("y_done"), sem("y_copied")
        s_yo = [sem(f"y_scattered{r}") for r in range(RING)]
        s_yin = [sem(f"y_gathered{u}") for u in range(2)]
        s_comb = sem("group_combined")
        s_out = sem("out_stored")
        s_proj, s_rope, s_rot = sem("projected"), sem("rope_read"), sem("qk_roped")
        s_hi, s_r1, s_mid, s_lo = sem("hi_part"), sem("rest1"), sem("mid_part"), sem("lo_part")
        s_qd = [sem(f"qk_parts_stored{u}") for u in range(2)]
        s_va, s_fill = sem("v_copied"), sem("stack_filled")
        s_vb = sem("v_batch_copied")
        s_st = [[sem(f"stack_in{u}{g}") for g in range(4)] for u in range(2)]
        s_nmi = [sem(f"max_rows_in{g}") for g in range(4)]
        s_e, s_exp = sem("scores_done"), sem("exp_done")
        s_m, s_mr = sem("max_scores_done"), sem("max_done")
        s_nmf, s_nmp, s_nmt = sem("negmax_ready"), sem("negmax_transposed"), sem("negmax_copied")
        s_av, s_ot = sem("av_done"), sem("av_copied")
        s_tp, s_td = sem("av_transposed"), sem("av_normalised")
        s_ap, s_at, s_op, s_od = sem("ao_transposed"), sem("at_copied"), sem("wo_done"), sem("residual_done")
        s_lq, s_lqe, s_lqf = sem("lin_q_done"), sem("lin_q_exp"), sem("lin_q_ready")
        s_lk, s_lke, s_lkf = sem("lin_kv_done"), sem("lin_k_exp"), sem("lin_k_ready")
        s_lv, s_kv, s_bd = sem("lin_v_ready"), sem("kv_done"), sem("kv_masked")
        s_ln, s_lao, s_la, s_lat = sem("lin_num_done"), sem("lin_out_ready"), sem("lin_out_t"), sem("lin_at_copied")
        s_lo2, s_lres = sem("lin_wo_done"), sem("lin_residual_done")

        block = ctx.enter_context(nc.Block())

        def ffn_of(L):
            return sum(k in (FFN0, FFN1) for k in SUBLAYERS[:L])

        FFNS = [k for k in SUBLAYERS if k in (FFN0, FFN1)]

        def moe_of(f):
            return MOE[0 if FFNS[f] == FFN0 else 1]

        def first_kind(f):
            return sum(k == FFN0 for k in FFNS[:f])

        TILES0 = [sum(moe_of(j)["tiles"] for j in range(f)) for f in range(len(FFNS) + 1)]

        def rounds(f, r):
            return len(range(r, moe_of(f)["tiles"], RING))

        def rounds0(f, r):
            return sum(rounds(j, r) for j in range(f))

        def scattered0(f, r):
            return sum(rounds(j, r) * moe_of(j)["S"] * 16 for j in range(f))

        def chunks_held(S):
            return 4 if S * P <= 512 else 2

        def hidden_chunk(S, q):
            n = chunks_held(S)
            at = 2048 // n * (q % n)
            return PS[:, at:at + S * P]

        def fused(L):
            return L == 0 or SUBLAYERS[L - 1] in (FFN0, FFN1) and SUBLAYERS[L] in FUSED

        def dev0(L):
            return sum(NG if fused(j) else 1 for j in range(L))

        class Chain:

            def __init__(self, eng, s):
                self.eng, self.s, self.n, self.base = eng, s, 0, 0

            def __call__(self, ins):
                ins.then_inc(self.s, 1)
                self.n += 1
                self.eng.wait_ge(self.s, self.base + self.n)

            def many(self, *all_ins):
                for ins in all_ins:
                    ins.then_inc(self.s, 1)
                self.n += len(all_ins)
                self.eng.wait_ge(self.s, self.base + self.n)

            def loop(self, i, k, first=0):
                self.start, self.k = self.n, k
                self.base, self.n = i * k + (self.start - first * k), 0

            def ended(self, count):
                assert self.n == self.k, (self.n, self.k)
                self.base, self.n = 0, self.start + count * self.k

        @block.sync
        def _(sp):
            xs, n = x_in.rearrange("(t p) d -> p t d", p=P), NT // XCHUNKS
            for c in range(XCHUNKS):
                if c == 1:
                    sp.dma_start(CST[:, :], cst_in).then_inc(s_cst, 16)
                    sp.dma_start(WT[:, :], w_in).then_inc(s_wt, 16)
                sp.dma_start(X[:, n * c:n * c + n, :], xs[:, n * c:n * c + n, :]).then_inc(s_x[c], 16)
            sp.wait_ge(s_zero, 1)
            for e in range(E1):
                sp.dma_start(BUFS[1][e * REGION:e * REGION + CAPACITY, :].rearrange("(p r) c -> p r c", p=P),
                             ZERO[:, 0:1, :].to_broadcast((P, S1, ROW))).then_inc(s_cleared, 16)
            for a in range(E0 * REGION, E0 * REGION + SPARE, S0 * P):
                sp.dma_start(BUFS[0][a:a + S0 * P, :].rearrange("(p r) c -> p r c", p=P),
                             ZERO[:, :, :]).then_inc(s_cleared, 16)
            sp.dma_start(ZD.rearrange("a b -> (a b)").rearrange("(a b) -> a b", a=8),
                         ZERO.rearrange("p a b -> p (a b)")[0:8, 0:256].bitcast(BF16)).then_inc(s_cleared, 16)

            def fetch(L, i, u):
                f = ffn_of(L)
                src = YK[0:PAIRS, :].rearrange("(k t p) c -> p k t c", k=2, p=P)
                if not (isinstance(i, int) and i == 0):
                    sp.wait_ge(s_comb, i * 2 + (f * NG + u - 1))
                for k in range(2):
                    sp.dma_start(YC[:, u, k], src[:, k, bass.ds(i * (2 * GT) + u * GT, GT), :])\
                      .then_inc(s_yin[u], 16)

            def fetches(L):
                with sp.Fori(1, NG // 2) as i:
                    fetch(L, i, 0)
                    fetch(L, i, 1)

            def moe(L):
                if L and fused(L):
                    fetches(L - 1)
                f = ffn_of(L)
                m, T0 = moe_of(f), TILES0[ffn_of(L)]
                S, tiles, ex = m["S"], m["tiles"], ex_in[SUBLAYERS[L] == FFN1]
                buf = BUFS[0 if S == S0 else 1]
                if S == S0:
                    sp.wait_ge(s_tiles, first_kind(f) + 1)
                    for e in range(E0):
                        end = sp.value_load(CNT[0:1, e:e + 1], min_val=e * REGION, max_val=e * REGION + TOKENS)
                        sp.dma_start(buf[bass.ds(end, S0 * P), :].rearrange("(p r) c -> p r c", p=P),
                                     ZERO[:, :, :]).then_inc(s_tails, 16)
                    sp.wait_ge(s_tails, 16 * E0 * (first_kind(f) + 1))
                sp.wait_ge(s_disp, 16 * 2 * NT * (f + 1))
                if f == 0:
                    sp.wait_ge(s_cleared, CLEARED)

                def load(i, c):
                    tau, r = i * RING + c, c % RING
                    if S == S0:
                        row = sp.value_load(TS[0:1, bass.ds(tau, 1)], min_val=0, max_val=E0 * REGION + SPARE - S0 * P)
                        e = sp.value_load(ET[0:1, bass.ds(tau, 1)], min_val=0, max_val=E0 - 1)
                    else:
                        row, e = tau * REGION, tau
                    if not (isinstance(i, int) and i == 0 and c < RING):
                        sp.wait_ge(s_yc, T0 + tau - (RING - 1))
                    sp.dma_start(XP[:, r, 0:S, :], buf[bass.ds(row, S * P), :]
                                 .rearrange("(j p) c -> p j c", p=P)).then_inc(s_xp[r], 16)
                    sp.dma_start(WE[:, r, :], ex[bass.ds(e, 1)].rearrange("o p n -> p (o n)"))\
                      .then_inc(s_we[r], 16)

                for c in range(RING):
                    load(0, c)
                whole = tiles // RING - 1
                with sp.Fori(0, whole) as i:
                    for c in range(RING):
                        load(i, RING + c)
                for c in range(RING * (whole + 1), tiles):
                    load(0, c)
                for r in range(RING):
                    sp.wait_ge(s_yo[r], scattered0(f + 1, r))
                fetch(L, 0, 0)
                fetch(L, 0, 1)
                if L + 1 < len(SUBLAYERS) and not fused(L + 1):
                    fetches(L)

            def attention(L):
                def store(b, u):
                    sp.wait_ge(s_lo, b + 1)
                    for w, a, n in ((0, 0, PARTS), (1, 0, PARTS), (1, PARTS, PARTS - 1)):
                        sp.dma_start(QKD[bass.ds(b, 1), w, a:a + n].rearrange("o a r t -> r (o a) t"),
                                     QP[:, u, 0:n, w, :]).then_inc(s_qd[u], 16)

                def load(b, par, g):
                    hs = slice(4 * g, 4 * g + 4)
                    n = PARTS * HD
                    q, k = [QKD[bass.ds(b, 1), w].rearrange("o a (d h) t -> (o a d) (h t)", h=HEADS)
                            [:, 4 * g * SEQ:4 * (g + 1) * SEQ] for w in range(2)]
                    for turn in range(PARTS):
                        sp.dma_start(QS[turn * n:turn * n + n, par, hs, :].rearrange("r h t -> r (h t)"),
                                     q[0:n]).then_inc(s_st[par][g], 16)
                        sp.dma_start(KS[turn * n:turn * n + n, par, hs, :].rearrange("r h t -> r (h t)"),
                                     k[turn * HD:turn * HD + n]).then_inc(s_st[par][g], 16)
                    sp.dma_start(QS[M_ROW:M_ROW + 2, par, hs, :],
                                 ZD.rearrange("a (h t) -> a h t", h=4)).then_inc(s_st[par][g], 16)

                pieces = [(b, g) for b in range(2) for g in range(4)]
                sp.wait_ge(s_fill, 2)
                for n in range(NG):
                    if n + 2 < NG:
                        fetch(L - 1, n // 2 + 1, n % 2)
                    store(n, n % 2)
                    for b, g in pieces[:0 if n < 2 else 2]:
                        if g == 0:
                            sp.wait_ge(s_qd[b], STORES * (n // 2 + (n % 2 >= b)))
                        load(b, b, g)
                        pieces.remove((b, g))
                sp.wait_ge(s_qd[0], STORES * NG // 2)
                sp.wait_ge(s_qd[1], STORES * NG // 2)

                def iteration(i, par, peeled):
                    for g in range(4):
                        gg = g - 1 if g else 3
                        if not peeled or (0 <= i < NG if g == 0 else i + 1 < NG):
                            bb = i if g == 0 else i + 1
                            pp = par if g == 0 else 1 - par
                            sp.wait_ge(s_nmt, bb * 4 + gg + 1)
                            for k in range(2):
                                sp.dma_start(
                                    QS[M_ROW + k:M_ROW + k + 1, pp, 4 * gg:4 * gg + 4, :]
                                    .rearrange("o h (a t) -> o (h a) t", t=P),
                                    NMT[16 * k:16 * k + 16, :]).then_inc(s_nmi[gg], 16)
                        if not peeled or 0 <= i < NG - 2:
                            sp.wait_ge(s_e, i * 32 + 8 * g + 8)
                            load(i + 2, par, g)

                iteration(-1, 1, True)
                iteration(0, 0, True)
                with sp.Fori(0, (LOOP_HI - 3) // 2) as i:
                    iteration(i * 2 + 1, 1, False)
                    iteration(i * 2 + 2, 0, False)
                for i in range(LOOP_HI - 2, NG + 1):
                    iteration(i, i % 2, True)

            for L, kind in enumerate(SUBLAYERS):
                if kind in (FFN0, FFN1):
                    moe(L)
                elif kind == ATTN:
                    attention(L)
            L = len(SUBLAYERS) - 1
            res = out.rearrange("(t p) d -> p t d", p=P)

            def deliver(i, u):
                t0 = i * (2 * GT) + u * GT
                sp.wait_ge(s_comb, i * 2 + (NG * ffn_of(L) + u + 1))
                sp.dma_start(res[:, bass.ds(t0, GT), :], X[:, bass.ds(t0, GT), :]).then_inc(s_out, 16)

            with sp.Fori(1, NG // 2) as i:
                for u in range(2):
                    fetch(L, i, u)
                    deliver(i - 1, u)
            deliver(NG // 2 - 1, 0)
            deliver(NG // 2 - 1, 1)
            sp.wait_ge(s_out, 16 * NG)

        @block.gpsimd
        def _(pool):
            nc.gpsimd.memset(ZERO[:, :, :], 0.0).then_inc(s_zero, 1)

            def moe(L):
                f = ffn_of(L)
                m, T0 = moe_of(f), TILES0[ffn_of(L)]
                S, tiles = m["S"], m["tiles"]
                buf = BUFS[0 if S == S0 else 1]
                if S == S1:
                    pool.wait_ge(s_cleared, CLEARED)
                for t in range(NT):
                    if t % GT == 0:
                        pool.wait_ge(s_row, NG * f + t // GT + 1)
                        pool.wait_ge(s_slot, NG * f + t // GT + 1)
                    for k in range(2):
                        pool.indirect_dma_start(buf, bass.IndirectOffsetOnAxis(ap=SLOT[:, k, t:t + 1], axis=0),
                                                XR[:, k, t, :], None).then_inc(s_disp, 16)

                def scatter(i, c):
                    tau, r = i * RING + c, c % RING
                    pool.wait_ge(s_yc, T0 + tau + 1)
                    pool.nop(nofuse=True)
                    for s in range(S):
                        pool.indirect_dma_start(YK, bass.IndirectOffsetOnAxis(ap=ID[:, r, s:s + 1], axis=0),
                                                YS[:, r, s, :], None).then_inc(s_yo[r], 16)

                whole = tiles // RING
                with pool.Fori(0, whole) as i:
                    for c in range(RING):
                        scatter(i, c)
                for c in range(RING * whole, tiles):
                    scatter(0, c)

            def attention(L):
                pool.wait_ge(s_comb, NG * (ffn_of(L) - 1) + 1)
                pool.memset(QS[64:STACK], 0.0).then_inc(s_fill, 1)
                pool.memset(KS[64:STACK], 1.0).then_inc(s_fill, 1)
                pool.wait_ge(s_fill, 2)
                with pool.Fori(0, NG // 2) as i:
                    for u in range(2):
                        pool.wait_ge(s_rope, i * 8 + (4 * u + 4))
                        pool.tensor_tensor(QF[:, u], QF[:, u], QT[:, :, :], ALU.add).then_inc(s_rot, 1)
                        pool.wait_ge(s_hi, i * 2 + u + 1)
                        pool.tensor_tensor(QR[:, u], QF[:, u], QP[:, u, 0], ALU.subtract).then_inc(s_r1, 1)
                        pool.wait_ge(s_mid, i * 2 + u + 1)
                        pool.tensor_tensor(QP[:, u, 2], QR[:, u], QP[:, u, 1], ALU.subtract).then_inc(s_lo, 1)

                def values(i, par, wait):
                    if wait:
                        pool.wait_ge(s_av, i * 4)
                    pool.tensor_copy(VB[:, 1 - par], VA[:, bass.ds(i * GT + GT, GT)]).then_inc(s_vb, 1)

                pool.wait_ge(s_va, NG)
                values(-1, 1, False)
                values(0, 0, False)
                with pool.Fori(0, (LOOP_HI - 1) // 2) as i:
                    values(i * 2 + 1, 1, True)
                    values(i * 2 + 2, 0, True)

            for L, kind in enumerate(SUBLAYERS):
                if kind in (FFN0, FFN1):
                    moe(L)
                elif kind == ATTN:
                    attention(L)

        @block.scalar
        def _(act):
            def deviation(L, i=None, u=0):
                if i is None and not fused(L):
                    act.wait_ge(s_var, dev0(L) + 1)
                    act.activation(LN[:, 7, :], LN[:, 6, :], ACT.Sqrt).then_inc(s_sd, 1)
                elif i is not None and fused(L):
                    act.wait_ge(s_var, i * 2 + (dev0(L) + u + 1))
                    cols = bass.ds(i * (2 * GT) + u * GT, GT)
                    act.activation(LN[:, 7, cols], LN[:, 6, cols], ACT.Sqrt).then_inc(s_sd, 1)

            def transposed_group(L, i, u):
                act.wait_ge(s_tr, i * 2 + (NG * L + u + 1))
                act.activation(XT[:, u, :], bank(u), ACT.Copy).then_inc(s_xt, 1)

            def moe(L):
                f = ffn_of(L)
                m, T0 = moe_of(f), TILES0[ffn_of(L)]
                S, tiles = m["S"], m["tiles"]
                func = ACT.Gelu_apprx_tanh if SUBLAYERS[L] == FFN0 else ACT.Gelu
                deviation(L)
                deviation(L, 0, 0)
                deviation(L, 0, 1)

                def rows(i, u, more=True):
                    transposed_group(L, i, u)
                    act.activation(XR[:, :, bass.ds(i * 2 * GT + u * GT, GT), 0:D],
                                   XS[:, u].unsqueeze(1).to_broadcast((P, 2, GT, D)), ACT.Copy)\
                       .then_inc(s_row, 1)
                    if more:
                        deviation(L, i + 1, u)

                with act.Fori(0, NG // 2 - 1) as i:
                    rows(i, 0)
                    rows(i, 1)
                rows(NG // 2 - 1, 0, False)
                rows(NG // 2 - 1, 1, False)
                act.wait_ge(s_gap, f + 1)
                act.activation(R1[:, 5, :], R1[:, 4, :], ACT.Exp).then_inc(s_ex, 1)

                def gelus(i, c):
                    tau, r = i * RING + c, c % RING
                    for q in range(FC):
                        act.wait_ge(s_h, tau * FC + (T0 * FC + q + 1))
                        if q == 0 and not (isinstance(i, int) and i == 0 and c < PAIR):
                            act.wait_ge(s_y, T0 + tau - (PAIR - 1))
                        act.activation(HT[:, c % PAIR, q, 0:S * P], hidden_chunk(S, q),
                                       func, bias=WE[:, r, 2 * DFF + q:2 * DFF + q + 1]).then_inc(s_g, 1)

                for c in range(RING):
                    gelus(0, c)
                whole = tiles // RING - 1
                with act.Fori(0, whole) as i:
                    for c in range(RING):
                        gelus(i, RING + c)
                for c in range(RING * (whole + 1), tiles):
                    gelus(0, c)

            def attention(L):
                deviation(L)

                def ahead(i, u):
                    deviation(L, i, u)
                    transposed_group(L, i, u)

                def split(i, u):
                    act.wait_ge(s_rot, i * 2 + (u + 1))
                    if not (isinstance(i, int) and i == 0):
                        act.wait_ge(s_qd[u], i * STORES)
                    act.activation(QP[:, u, 0], QF[:, u], ACT.Copy).then_inc(s_hi, 1)
                    act.wait_ge(s_r1, i * 2 + (u + 1))
                    act.activation(QP[:, u, 1], QR[:, u], ACT.Copy).then_inc(s_mid, 1)

                def step(i):
                    ahead(i, 1)
                    split(i, 0)
                    ahead(i + 1, 0)
                    split(i, 1)

                ahead(0, 0)
                step(0)
                with act.Fori(1, NG // 2 - 1) as i:
                    step(i)
                ahead(NG // 2 - 1, 1)
                split(NG // 2 - 1, 0)
                split(NG // 2 - 1, 1)

                def iteration(i, par, peeled):
                    has_m = not peeled or i + 1 < NG
                    has_e = not peeled or 0 <= i < NG
                    for s in range(HEADS):
                        g, j = s // 4, s % 4
                        if has_e:
                            exp(i, par, s, 0)
                        if j == 0 and (not peeled or 0 <= 4 * i + g - 2 < 4 * NG):
                            G = i * 4 + (g - 2)
                            act.wait_ge(s_av, G + 1)
                            if not (peeled and 4 * i + g - 2 == 0):
                                act.wait_ge(s_tp, G)
                            act.activation(OT[:, :], bank(6), ACT.Copy).then_inc(s_ot, 1)
                        if j == 3:
                            b, gg = (i, 3) if g == 0 else (i + 1, g - 1)
                            if not peeled or (0 <= b < NG):
                                act.wait_ge(s_nmp, b * 4 + gg + 1)
                                if not (peeled and b == 0 and gg == 0):
                                    bb, g2 = (b, gg - 1) if gg else (b - 1, 3)
                                    act.wait_ge(s_nmi[g2], bb * 32 + 32)
                                act.activation(NMT[0:32, :], bank(7, 0, P)[0:32, :], ACT.Copy).then_inc(s_nmt, 1)
                        if s == 8 and (not peeled or 0 <= i - 1 < NG):
                            act.wait_ge(s_ap, i)
                            act.activation(AT[:, :], bank(7), ACT.Copy).then_inc(s_at, 1)
                        if has_e:
                            exp(i, par, s, 1)

                def exp(i, par, s, w):
                    g, j = s // 4, s % 4
                    act.wait_ge(s_e, i * 32 + (2 * s + w + 1))
                    if w == 0 and j == 0 and not (isinstance(i, int) and 4 * i + g < 2):
                        act.wait_ge(s_av, i * 4 + g - 1)
                    act.activation(PT[:, g % 2, j, 2 * w:2 * w + 2, :],
                                   PS[:, 1024 * w:1024 * w + 1024].rearrange("p (a b) -> p a b", a=2),
                                   ACT.Exp, scale=float(1.0 / np.sqrt(HD))).then_inc(s_exp, 1)

                iteration(-1, 1, True)
                iteration(0, 0, True)
                with act.Fori(0, (LOOP_HI - 1) // 2) as i:
                    iteration(i * 2 + 1, 1, False)
                    iteration(i * 2 + 2, 0, False)
                for i in range(LOOP_HI, NG + 1):
                    iteration(i, i % 2, True)

            def linear(L):
                deviation(L)

                def front(i, u):
                    n = i * 2 + (u + 1)
                    act.wait_ge(s_lq, n)
                    act.activation(LQE[:, u], bank(4), ACT.Exp).then_inc(s_lqe, 1)
                    act.wait_ge(s_lk, n)
                    if not (isinstance(i, int) and i == 0):
                        act.wait_ge(s_kv, n - 2)
                    act.activation(LV[:, u, :, 0:D],
                                   PS[:, 1024:2048].rearrange("p (a b) -> p a b", a=GT)[:, :, D:2 * D],
                                   ACT.Copy).then_inc(s_lv, 1)
                    act.activation(LKE[:, u],
                                   PS[:, 1024:2048].rearrange("p (a b) -> p a b", a=GT)[:, :, 0:D],
                                   ACT.Exp).then_inc(s_lke, 1)

                def back(i, u):
                    n = i * 2 + (u + 1)
                    act.wait_ge(s_la, n)
                    act.activation(LAT[:, u], bank(7), ACT.Copy).then_inc(s_lat, 1)

                def both(i, u, i2, u2, more=True):
                    front(i, u)
                    if more:
                        transposed_group(L, i + u, 1 - u)
                    back(i2, u2)

                transposed_group(L, 0, 0)
                transposed_group(L, 0, 1)
                front(0, 0)
                both(0, 1, 0, 0)
                with act.Fori(1, NG // 2 - 1) as i:
                    both(i, 0, i - 1, 1)
                    both(i, 1, i, 0)
                i = NG // 2 - 1
                both(i, 0, i - 1, 1)
                both(i, 1, i, 0, False)
                back(i, 1)

            for L, kind in enumerate(SUBLAYERS):
                if kind in (FFN0, FFN1):
                    moe(L)
                elif kind == ATTN:
                    attention(L)
                else:
                    linear(L)

        @block.tensor
        def _(pe):
            pe.wait_ge(s_cst, 16)
            pe.wait_ge(s_wt, 16)

            def transpose_group(L, i, u):
                pe.wait_ge(s_xs, i * 2 + (NG * L + u + 1))
                for j in range(GT):
                    mm = pe.transpose(bank(u, P * j, P * j + P), XS[:, u, j, :], ident)
                mm.then_inc(s_tr, 1)

            def moe(L):
                f = ffn_of(L)
                m, T0 = moe_of(f), TILES0[ffn_of(L)]
                E, S, tiles = m["E"], m["S"], m["tiles"]
                wr = wt("r0" if SUBLAYERS[L] == FFN0 else "r1")
                N = S * P

                def logits(i, u):
                    pe.wait_ge(s_xt, i * 2 + (NG * L + u + 1))
                    if not (isinstance(i, int) and i == 0):
                        pe.wait_ge(s_lgc, i * 2 + (NG * f + u - 1))
                    for j in range(GT):
                        mm = pe.matmul(bank(2 + u, E * j, E * j + E), XT[:, u, P * j:P * j + P], wr,
                                       start=True, stop=True)
                    mm.then_inc(s_lg, 1)

                def ranks(i, u):
                    pe.wait_ge(s_mask, i * 2 + (NG * f + u + 1))
                    m_ = MB[:, u].rearrange("p a b -> p (a b)")[:, 0:GT * E]
                    pe.matmul(bank(4 + u, 0, GT * E), before_bf[:, :], m_, start=True, stop=False)
                    for j in range(GT - 1):
                        pe.matmul(bank(4 + u, E * (j + 1), E * GT).rearrange("p (a b) -> p a b", b=E), ones_bf[:, :],
                                  m_[:, E * j:E * j + E].unsqueeze(1).to_broadcast((P, GT - 1 - j, E)),
                                  start=False, stop=False)
                    pe.matmul(bank(4 + u, 0, GT * E).rearrange("p (a b) -> p a b", b=E), ones_bf[:, :],
                              SUM[:, u, 0:E].unsqueeze(1).to_broadcast((P, GT, E)), start=False, stop=True)\
                      .then_inc(s_rank, 1)

                def step(i, u):
                    ranks(i, u)
                    if not (isinstance(i, int) and i == NG // 2 - 1 and u == 1):
                        logits(i + u, 1 - u)
                    if not (isinstance(i, int) and i == NG // 2 - 1):
                        transpose_group(L, i + 1, u)

                transpose_group(L, 0, 0)
                transpose_group(L, 0, 1)
                logits(0, 0)
                step(0, 0)
                step(0, 1)
                with pe.Fori(1, NG // 2 - 1) as i:
                    step(i, 0)
                    step(i, 1)
                step(NG // 2 - 1, 0)
                step(NG // 2 - 1, 1)
                if S == S0:
                    pe.wait_ge(s_sum, first_kind(f) + 1)
                    pe.matmul(bank(6, 0, E), ones_bf[:, :], SUM[:, 0, 0:E], start=True, stop=True).then_inc(s_counts, 1)
                    pe.wait_ge(s_tiles, first_kind(f) + 1)
                pe.wait_ge(s_slot, NG * (f + 1))

                def turn(i, c):
                    tau, r = i * RING + c, c % RING
                    pe.wait_ge(s_xp[r], i * 16 + 16 * (rounds0(f, r) + c // RING + 1))
                    if not (isinstance(i, int) and i == 0 and c == 0):
                        pe.wait_ge(s_xpc, T0 + tau)
                    for s in range(S):
                        mm = pe.transpose(bank(4, P * s, P * s + P), XP[:, r, s, 0:D], ident)
                    mm.then_inc(s_xpt, 1)

                def hidden(i, c):
                    tau, r = i * RING + c, c % RING
                    pe.wait_ge(s_we[r], i * 16 + 16 * (rounds0(f, r) + c // RING + 1))
                    pe.wait_ge(s_xpc, T0 + tau + 1)
                    for q in range(FC):
                        if not (isinstance(i, int) and i == 0 and c == 0 and q < chunks_held(S)):
                            pe.wait_ge(s_g, tau * FC + (T0 * FC + q + 1 - chunks_held(S)))
                        for a in range(0, N, 512):
                            b = min(N, a + 512)
                            mm = pe.matmul(hidden_chunk(S, q)[:, a:b],
                                           WE[:, r, q * P:q * P + P], XPT[:, c % PAIR, a:b], start=True, stop=True)
                        mm.then_inc(s_h, 1)

                def outputs(i, c):
                    tau, r = i * RING + c, c % RING
                    pe.wait_ge(s_g, tau * FC + (T0 * FC + FC))
                    if not (isinstance(i, int) and i == 0 and c == 0):
                        pe.wait_ge(s_yc, T0 + tau)
                    for s in range(S):
                        for q in range(FC):
                            mm = pe.matmul(PS[:, 3072 + P * s:3072 + P * s + P], HT[:, c % PAIR, q, P * s:P * s + P],
                                           WE[:, r, DFF + q * D:DFF + q * D + D], start=(q == 0), stop=(q == FC - 1))
                    mm.then_inc(s_y, 1)

                turn(0, 0)
                turn(0, 1)
                hidden(0, 0)
                whole = (tiles - 2) // RING

                def steps(i):
                    for c in range(1, RING + 1):
                        turn(i, c + 1)
                        hidden(i, c)
                        outputs(i, c - 1)

                steps(0)
                with pe.Fori(1, whole) as i:
                    steps(i)
                for c in range(RING * whole + 1, tiles + 1):
                    if c + 1 < tiles:
                        turn(0, c + 1)
                    if c < tiles:
                        hidden(0, c)
                    outputs(0, c - 1)

            def attention(L):
                def front(i, u):
                    pe.wait_ge(s_xt, i * 2 + (NG * L + u + 1))
                    first = isinstance(i, int) and i == 0 and u == 0
                    for n, w in enumerate(("wq", "wqr", "wk", "wkr")):
                        if not first:
                            pe.wait_ge(s_rope, i * 8 + (4 * u + n - 3))
                        pe.matmul(bank(2 + n), wt(w), XT[:, u, :], start=True, stop=True).then_inc(s_proj, 1)
                    if not first:
                        pe.wait_ge(s_va, i * 2 + u)
                    for j in range(GT):
                        mm = pe.matmul(bank(6, P * j, P * j + P), XT[:, u, P * j:P * j + P], wt("wv"),
                                       start=True, stop=True)
                    mm.then_inc(s_proj, 1)

                def step(i):
                    front(i, 0)
                    transpose_group(L, i, 1)
                    front(i, 1)
                    transpose_group(L, i + 1, 0)

                transpose_group(L, 0, 0)
                step(0)
                with pe.Fori(1, NG // 2 - 1) as i:
                    step(i)
                front(NG // 2 - 1, 0)
                transpose_group(L, NG // 2 - 1, 1)
                front(NG // 2 - 1, 1)
                pe.wait_ge(s_va, NG + 1)

                def iteration(i, par, peeled):
                    has_m = not peeled or i + 1 < NG
                    has_e = not peeled or 0 <= i < NG
                    for s in range(HEADS):
                        g, j = s // 4, s % 4
                        if has_e and j == 0:
                            pe.wait_ge(s_nmi[g], i * 32 + 32)
                        if has_e:
                            scores(i, par, s, 0)
                        if has_m:
                            if j == 0:
                                pe.wait_ge(s_st[1 - par][g], half(i, 1, par) * LOADS)
                            maxima(i, par, s, 0)
                        has_w = not peeled or 0 <= 4 * i + g - 1 < 4 * NG
                        if has_w:
                            weigh(i, par, g, j, 0, peeled)
                        if has_m:
                            maxima(i, par, s, 1)
                        if has_e:
                            scores(i, par, s, 1)
                        if has_m:
                            maxima(i, par, s, 2)
                        if has_w:
                            weigh(i, par, g, j, 1, peeled)
                        if has_m:
                            maxima(i, par, s, 3)
                        misc(i, par, s, peeled)

                def half(i, ahead, par):
                    if isinstance(i, int):
                        return (i + ahead) // 2 + 1
                    return HALF[0] + (1 if (par == 1 and ahead == 1) else 0)

                def scores(i, par, s, w):
                    if not (isinstance(i, int) and i == 0 and s == 0):
                        pe.wait_ge(s_exp, i * 32 + (2 * s + w - 1))
                    for k in range(2 * w, 2 * w + 2):
                        mm = pe.matmul(bank(k), KS[0:STACK, par, s, P * k:P * k + P], QS[0:STACK, par, s, :],
                                       start=True, stop=True)
                    mm.then_inc(s_e, 1)

                def maxima(i, par, s, a):
                    if not (isinstance(i, int) and i == -1 and s == 0 and a < 2):
                        pe.wait_ge(s_mr, i * 64 + (64 + 4 * s + a - 1))
                    pe.matmul(bank(4 + a % 2), QS[0:STACK, 1 - par, s, P * a:P * a + P], KS[0:STACK, 1 - par, s, :],
                              start=True, stop=True).then_inc(s_m, 1)

                def weigh(i, par, g, k, half_, peeled):
                    gg = (g - 1) % 4
                    vpar = par if g else 1 - par
                    if k == 0 and half_ == 0:
                        pe.wait_ge(s_exp, i * 32 + 8 * g)
                        if not (peeled and 4 * i + g - 1 == 0):
                            pe.wait_ge(s_ot, i * 4 + g - 1)
                        if g == 1:
                            pe.wait_ge(s_vb, i + 1)
                    for j in range(2 * half_, 2 * half_ + 2):
                        h = 4 * gg + j
                        mm = pe.matmul(bank(6)[32 * j:32 * j + HD + 1, :], VB[:, vpar, k, h, :],
                                       PT[:, gg % 2, j, k, :], start=(k == 0), stop=(k == GT - 1))
                    if k == GT - 1 and half_ == 1:
                        mm.then_inc(s_av, 1)

                def misc(i, par, s, peeled):
                    g, j = s // 4, s % 4

                    def earlier(what, n):
                        n_int = n if isinstance(n, int) else None
                        if n_int is None or n_int > 0:
                            pe.wait_ge(what, n)

                    def clamp(n, top):
                        return max(0, min(n, top)) if isinstance(n, int) else n

                    if j == 1:
                        if peeled and not 0 <= 4 * i + g - 2 < 4 * NG:
                            return
                        G = i * 4 + (g - 2)
                        earlier(s_nmt, clamp(i * 4 + g + 3, 4 * NG))
                        earlier(s_td, G)
                        if g == 2:
                            earlier(s_at, clamp(i, NG))
                        if g == 3:
                            earlier(s_od, clamp(i, NG))
                        pe.wait_ge(s_ot, G + 1)
                        for a in range(GT):
                            mm = pe.transpose(bank(7, P * a, P * a + P), OT[:, P * a:P * a + P], ident)
                        mm.then_inc(s_tp, 1)
                    if j == 2:
                        b, gg = (i, 3) if g == 0 else (i + 1, g - 1)
                        if peeled and not 0 <= b < NG:
                            return
                        earlier(s_td, clamp(i * 4 + (g - 1), 4 * NG))
                        earlier(s_nmt, b * 4 + gg)
                        pe.wait_ge(s_nmf, b * 4 + gg + 1)
                        pe.transpose(bank(7, 0, P)[0:32, :], NMF.rearrange("p a b -> p (a b)"), ident)\
                            .then_inc(s_nmp, 1)
                    if s in (7, 11) and (not peeled or 0 <= i - 1 < NG):
                        earlier(s_nmt, clamp(i * 4 + g + 4, 4 * NG))
                        earlier(s_td, clamp(i * 4 + (g - 1), 4 * NG))
                        if s == 7:
                            for a in range(GT):
                                mm = pe.transpose(bank(7, P * a, P * a + P), AO[:, a, :], ident)
                            mm.then_inc(s_ap, 1)
                        else:
                            pe.wait_ge(s_at, i)
                            for a in range(GT):
                                mm = pe.matmul(bank(7, P * a, P * a + P), AT[:, P * a:P * a + P], wt("wo"),
                                               start=True, stop=True)
                            mm.then_inc(s_op, 1)

                HALF = [0]
                iteration(-1, 1, True)
                iteration(0, 0, True)
                with pe.Fori(0, (LOOP_HI - 1) // 2) as i:
                    HALF[0] = i + 1
                    iteration(i * 2 + 1, 1, False)
                    HALF[0] = i + 2
                    iteration(i * 2 + 2, 0, False)
                for i in range(LOOP_HI, NG + 1):
                    iteration(i, i % 2, True)

            def linear(L):
                KVb = PS[:, 1024:2048].rearrange("p (a b) -> p a b", a=GT)

                def f1(i, u):
                    transpose_group(L, i, u)

                def f2(i, u):
                    n = i * 2 + (u + 1)
                    pe.wait_ge(s_xt, n + NG * L)
                    pe.matmul(bank(4), wt("lq"), XT[:, u, :], start=True, stop=True).then_inc(s_lq, 1)

                def f3(i, u):
                    n = i * 2 + (u + 1)
                    if not (isinstance(i, int) and i == 0 and u == 0):
                        pe.wait_ge(s_lv, n - 1)
                        pe.wait_ge(s_lkf, n - 1)
                    for j in range(GT):
                        mm = pe.matmul(KVb[:, j, :], XT[:, u, P * j:P * j + P], wt("lkv"), start=True, stop=True)
                    mm.then_inc(s_lk, 1)

                def b1(i, u):
                    n = i * 2 + (u + 1)
                    pe.wait_ge(s_lkf, n)
                    pe.wait_ge(s_lv, n)
                    pe.wait_ge(s_lqf, n)
                    for j in range(GT):
                        mm = pe.matmul(bank(4, 0, D + 1), LKF[:, u, j, :], LV[:, u, j, :],
                                       start=(j == 0), stop=(j == GT - 1))
                    mm.then_inc(s_kv, 1)

                def b2(i, u):
                    n = i * 2 + (u + 1)
                    pe.wait_ge(s_bd, n)
                    for j in range(GT):
                        mm = pe.matmul(PS[:, 2560 + 256 * j:2560 + 256 * j + D + HEADS],
                                       LQF[:, u, P * j:P * j + P], BD[:, u, :], start=True, stop=True)
                    mm.then_inc(s_ln, 1)

                def b3(i, u):
                    n = i * 2 + (u + 1)
                    pe.wait_ge(s_lao, n)
                    for j in range(GT):
                        mm = pe.transpose(bank(7, P * j, P * j + P), LAO[:, u, j, :], ident)
                    mm.then_inc(s_la, 1)

                def b4(i, u):
                    n = i * 2 + (u + 1)
                    pe.wait_ge(s_lat, n)
                    for j in range(GT):
                        mm = pe.matmul(bank(7, P * j, P * j + P), LAT[:, u, P * j:P * j + P], wt("lo"),
                                       start=True, stop=True)
                    mm.then_inc(s_lo2, 1)

                def both(i, u, i2, u2, more=True):
                    b1(i2, u2)
                    pe.wait_ge(s_bd, i2 * 2 + (u2 + 1))
                    f2(i, u)
                    b2(i2, u2)
                    f3(i, u)
                    if more:
                        f1(i + u, 1 - u)
                    if not (isinstance(i2, int) and i2 == 0 and u2 == 0):
                        pe.wait_ge(s_lres, i2 * 2 + u2)
                    b3(i2, u2)
                    b4(i2, u2)

                f1(0, 0)
                f1(0, 1)
                f2(0, 0)
                f3(0, 0)
                both(0, 1, 0, 0)
                with pe.Fori(1, NG // 2 - 1) as i:
                    both(i, 0, i - 1, 1)
                    both(i, 1, i, 0)
                i = NG // 2 - 1
                both(i, 0, i - 1, 1)
                both(i, 1, i, 0, False)
                b1(i, 1)
                b2(i, 1)
                pe.wait_ge(s_lres, NG - 1)
                b3(i, 1)
                b4(i, 1)

            for L, kind in enumerate(SUBLAYERS):
                if kind in (FFN0, FFN1):
                    moe(L)
                elif kind == ATTN:
                    attention(L)
                else:
                    linear(L)

        @block.vector
        def _(dve):
            chain = Chain(dve, s_dve)

            def group_stats(t0):
                for j in range(GT):
                    ins = dve.bn_stats(BST[:, bass.ds(t0 + j, 1), :].rearrange("p a b -> p (a b)"),
                                       X[:, bass.ds(t0 + j, 1), :].rearrange("p a b -> p (a b)"))
                return ins

            def variance(L, cols, steps):
                me, m2e, mo, m2o = [BST[:, cols, k] for k in (1, 2, 4, 5)]
                a = [LN[:, k, cols] for k in range(12)]
                steps.many(dve.tensor_tensor(a[2], me, mo, ALU.add),
                           dve.tensor_tensor(a[3], me, mo, ALU.subtract),
                           dve.tensor_tensor(a[4], m2e, m2o, ALU.add))
                steps.many(dve.tensor_scalar(a[0], a[2], 0.5, None, ALU.mult),
                           dve.tensor_tensor(a[5], a[3], a[3], ALU.mult))
                steps(dve.scalar_tensor_tensor(out=a[8], in0=a[5], scalar=D / 4.0, in1=a[4],
                                               op0=ALU.mult, op1=ALU.add))
                dve.tensor_scalar(a[6], a[8], 1.0 / D, LN_EPS, ALU.mult, ALU.add).then_inc(s_var, 1)

            def scaling(L, cols, n, steps):
                a = [LN[:, k, cols] for k in range(12)]
                dve.wait_ge(s_sd, n + (dev0(L) + 1))
                steps(dve.reciprocal(a[9], a[7]))
                steps(dve.tensor_tensor(a[10], a[9], a[9], ALU.mult))
                steps(dve.tensor_tensor(a[11], a[10], a[6], ALU.mult))
                steps(dve.tensor_scalar(a[10], a[11], -0.5, 1.5, ALU.mult, ALU.add))
                steps(dve.tensor_tensor(a[1], a[9], a[10], ALU.mult))

            def finish_stats(L):
                if not fused(L):
                    variance(L, slice(0, NT), chain)
                    scaling(L, slice(0, NT), 0, chain)

            def combine(L, i, u, steps):
                f = ffn_of(L)
                dve.wait_ge(s_yin[u], i * 32 + 32 * (NG // 2 * f + 1))
                t0 = i * (2 * GT) + GT * u
                for k in range(2):
                    for j in range(GT):
                        xt = X[:, bass.ds(t0 + j, 1), :].rearrange("p a b -> p (a b)")
                        ins = dve.scalar_tensor_tensor(
                            out=xt, in0=YC[:, u, k, j, :], scalar=GATE[:, k, bass.ds(t0 + j, 1)],
                            in1=xt, op0=ALU.mult, op1=ALU.add)
                    if k == 0:
                        steps(ins)
                    else:
                        ins.then_inc(s_comb, 1)

            def arrive(L, i, u, steps):
                if fused(L):
                    t0 = i * (2 * GT) + GT * u
                    if L:
                        combine(L - 1, i, u, steps)
                        dve.wait_ge(s_comb, i * 2 + (NG * ffn_of(L - 1) + u + 1))
                    steps(group_stats(t0))
                    variance(L, bass.ds(t0, GT), steps)

            def scale(L, i, u, steps):
                if fused(L):
                    scaling(L, bass.ds(i * (2 * GT) + GT * u, GT), i * 2 + u, steps)

            def front_steps(L):
                return (7 if L == 0 else 8) + 5 if fused(L) else 0

            def normalise(L, i, u, *waits):
                for s, n in waits:
                    dve.wait_ge(s, n)
                for j in range(GT):
                    t = i * (2 * GT) + (GT * u + j)
                    ins = dve.tensor_scalar(XS[:, u, j, :], X[:, bass.ds(t, 1), :].rearrange("p a b -> p (a b)"),
                                            MEAN[:, bass.ds(t, 1)], RSTD[:, bass.ds(t, 1)],
                                            ALU.subtract, ALU.mult)
                ins.then_inc(s_xs, 1)

            def moe(L):
                f = ffn_of(L)
                m, T0 = moe_of(f), TILES0[ffn_of(L)]
                E, S, tiles = m["E"], m["S"], m["tiles"]
                tag = TAG * (f + 1)
                rb = wt("rb0" if SUBLAYERS[L] == FFN0 else "rb1").rearrange("p (a b) -> p a b", a=GT)
                for k in range(2):
                    dve.tensor_scalar(XR[:, k, :, D], cst("tokid"), tag + k * TOKENS, None, ALU.add)\
                       .then_inc(s_dve, 1)
                    chain.n += 1

                def norm(i, u):
                    if isinstance(i, int) and i == 0:
                        normalise(L, i, u)
                    else:
                        n = i * 2 + (u - 1)
                        normalise(L, i, u, (s_tr, n + NG * L), (s_row, n + NG * f))

                lg = LG[:, :, 0:E]
                w = [RT[k][:, :, 0:E] for k in range(3)]
                oh = [OH[:, k, :, 0:E] for k in range(2)]
                r = [R1[:, k, :] for k in range(20)]

                def every(name):
                    return cst(name)[:, 0:E].unsqueeze(1).to_broadcast((P, GT, E))

                def choose(i, u, steps):
                    t0 = i * (2 * GT) + GT * u

                    def best(k, scores):
                        m_, i_ = r[k][:, bass.ds(t0, GT)], r[2 + k][:, bass.ds(t0, GT)]
                        steps(dve.tensor_reduce(m_, scores, AX_X, ALU.max))
                        steps(dve.tensor_tensor(w[0], scores, m_.unsqueeze(2).to_broadcast((P, GT, E)), ALU.is_equal))
                        steps(dve.tensor_tensor(w[1], w[0], every("eoff"), ALU.mult))
                        steps(dve.tensor_reduce(i_, w[1], AX_X, ALU.min))
                        steps(dve.tensor_tensor(oh[k], every("eoff"), i_.unsqueeze(2).to_broadcast((P, GT, E)),
                                                ALU.is_equal))

                    n = i * 2 + (NG * f + u + 1)
                    dve.wait_ge(s_lg, n)
                    dve.tensor_tensor(lg, bank(2 + u, 0, GT * E).rearrange("p (a b) -> p a b", a=GT), rb, ALU.add)\
                       .then_inc(s_lgc, 1)
                    dve.wait_ge(s_lgc, n)
                    best(0, lg)
                    steps(dve.scalar_tensor_tensor(out=w[2], in0=oh[0], scalar=NEG, in1=lg,
                                                   op0=ALU.mult, op1=ALU.add))
                    best(1, w[2])
                    m_ = MB[:, u].rearrange("p a b -> p (a b)")[:, 0:GT * E].rearrange("p (a b) -> p a b", a=GT)
                    dve.tensor_tensor(m_, oh[0], oh[1], ALU.add).then_inc(s_mask, 1)
                    dve.wait_ge(s_mask, n)
                    steps(dve.tensor_reduce(SUMF[:, 0:E], m_.rearrange("p a b -> p b a"), AX_X, ALU.add))
                    steps(dve.tensor_tensor(SUM[:, 1 - u, 0:E], SUM[:, u, 0:E], SUMF[:, 0:E], ALU.add))

                def place(i, u, steps):
                    t0 = i * (2 * GT) + GT * u
                    dve.wait_ge(s_rank, i * 2 + (NG * f + u + 1))
                    steps(dve.tensor_tensor(w[0], bank(4 + u, 0, GT * E).rearrange("p (a b) -> p a b", a=GT),
                                            every("region"), ALU.add))
                    steps(dve.tensor_tensor(PL[:, :, :, 0:E], OH[:, :, :, 0:E],
                                            w[0].unsqueeze(1).to_broadcast((P, 2, GT, E)), ALU.mult))
                    steps(dve.tensor_reduce(R1[:, 9:11, bass.ds(t0, GT)], PL[:, :, :, 0:E], AX_X, ALU.add))
                    dve.tensor_copy(SLOT[:, :, bass.ds(t0, GT)], R1[:, 9:11, bass.ds(t0, GT)]).then_inc(s_slot, 1)

                for u in range(2):
                    arrive(L, 0, u, chain)
                    scale(L, 0, u, chain)
                    norm(0, u)
                chain(dve.memset(SUM[:, 0], 0.0))
                if L == 0:
                    for c in range(1, XCHUNKS):
                        dve.wait_ge(s_x[c], 16)
                with dve.Fori(0, NG // 2 - 1) as i:
                    chain.loop(i, 2 * (5 + 1 + 5 + 2 + 3 + front_steps(L)))
                    for u in range(2):
                        choose(i, u, chain)
                        arrive(L, i + 1, u, chain)
                        if fused(L):
                            place(i, u, chain)
                            scale(L, i + 1, u, chain)
                            norm(i + 1, u)
                        else:
                            norm(i + 1, u)
                            place(i, u, chain)
                    chain.ended(NG // 2 - 1)
                for u in range(2):
                    choose(NG // 2 - 1, u, chain)
                    place(NG // 2 - 1, u, chain)

                if E == E0:
                    dve.tensor_copy(RE[:, 7, 0:1], cst("ones")[:, 0:1]).then_inc(s_sum, 1)
                    dve.wait_ge(s_counts, first_kind(f) + 1)
                    n_e = bank(6, 0, E)
                    chain(dve.tensor_tensor(JT[:, :, :], n_e.unsqueeze(2).to_broadcast((P, E, 16)),
                                            cst("jtab").unsqueeze(1).to_broadcast((P, E, 16)), ALU.is_gt))
                    dve.tensor_tensor(CNT[:, :], n_e, cst("region")[:, 0:E], ALU.add).then_inc(s_dve, 1)
                    chain.n += 1
                    chain(dve.tensor_reduce(RE[:, 0, :], JT[:, :, :], AX_X, ALU.add))
                    chain(dve.tensor_tensor_scan(RE[:, 1, :], cst("ones")[:, 0:E], RE[:, 0, :], 0.0,
                                                 ALU.mult, ALU.add))
                    chain(dve.tensor_scalar(RE[:, 2, :], RE[:, 0, :], -float(S * P), float(REGION),
                                            ALU.mult, ALU.add))
                    chain(dve.tensor_tensor(TT[:, :, :], cst("tile").unsqueeze(2).to_broadcast((P, tiles, E)),
                                            RE[:, 1, :].unsqueeze(1).to_broadcast((P, tiles, E)), ALU.is_ge))
                    chain(dve.tensor_tensor(TW[:, :, :], TT[:, :, :],
                                            RE[:, 2, :].unsqueeze(1).to_broadcast((P, tiles, E)), ALU.mult))
                    chain(dve.tensor_reduce(ETF[:, :], TT[:, :, :], AX_X, ALU.add))
                    chain(dve.tensor_scalar(ET[:, :], ETF[:, :], float(E - 1), None, ALU.min))
                    chain(dve.tensor_reduce(TSF[:, :], TW[:, :, :], AX_X, ALU.add))
                    dve.tensor_tensor(TS[:, :], TSF[:, :], cst("tilerow"), ALU.add).then_inc(s_tiles, 1)

                dve.tensor_tensor(r[4], r[1], r[0], ALU.subtract).then_inc(s_gap, 1)
                dve.wait_ge(s_ex, f + 1)
                chain(dve.tensor_scalar(r[6], r[5], 1.0, None, ALU.add))
                chain(dve.reciprocal(r[7], r[6]))
                chain(dve.tensor_tensor(r[8], r[5], r[7], ALU.mult))
                gates = [r[7], r[8]]
                if E == E0:
                    for k in range(2):
                        chain(dve.tensor_scalar(GATE[:, k, :], gates[k], 0.5, None, ALU.mult))
                else:
                    for k in range(2):
                        chain(dve.tensor_scalar(r[13], r[2 + k], 64.0, float(REGION), ALU.add, ALU.mult))
                        chain(dve.tensor_tensor(r[14], r[9 + k], r[13], ALU.subtract))
                        chain(dve.tensor_scalar(r[11 + k], r[14], float(CAPACITY), None, ALU.is_lt))
                        chain(dve.tensor_tensor(r[17 + k], gates[k], r[11 + k], ALU.mult))
                    chain(dve.tensor_tensor(r[13], r[17], r[18], ALU.add))
                    chain(dve.tensor_scalar(r[14], r[13], 1e-9, None, ALU.add))
                    chain(dve.reciprocal(r[15], r[14]))
                    for k in range(2):
                        chain(dve.scalar_tensor_tensor(out=GATE[:, k, :], in0=r[17 + k], scalar=0.5, in1=r[15],
                                                       op0=ALU.mult, op1=ALU.mult))

                def tile_in(i, c):
                    tau = i * RING + c
                    dve.wait_ge(s_xpt, T0 + tau + 1)
                    if not (isinstance(i, int) and i == 0 and c < PAIR):
                        dve.wait_ge(s_h, (tau - (PAIR - 1)) * FC + T0 * FC)
                    dve.tensor_copy(XPT[:, c % PAIR, 0:S * P], PS[:, 2048:2048 + S * P]).then_inc(s_xpc, 1)

                def tile_out(i, c, steps):
                    tau, r_ = i * RING + c, c % RING
                    if not (isinstance(i, int) and i == 0 and c < RING):
                        dve.wait_ge(s_yo[r_], i * (16 * S) + 16 * S * (c // RING) + scattered0(f, r_))
                    idf = XP[:, r_, 0:S, D]
                    trash = cst("trash")[:, bass.ds(tau * S, S)]
                    a = [IDF[:, r_, k, 0:S] for k in range(3)]
                    dve.tensor_scalar(a[0], idf, tag, None, ALU.is_ge).then_inc(s_dve, 1)
                    steps.n += 1
                    steps(dve.scalar_tensor_tensor(out=a[1], in0=idf, scalar=tag, in1=trash,
                                                   op0=ALU.subtract, op1=ALU.subtract))
                    steps(dve.tensor_tensor(a[2], a[0], a[1], ALU.mult))
                    steps(dve.tensor_tensor(ID[:, r_, 0:S], a[2], trash, ALU.add))
                    dve.wait_ge(s_y, T0 + tau + 1)
                    dve.tensor_tensor(YS[:, r_, 0:S, :], PS[:, 3072:3072 + S * P].rearrange("p (a b) -> p a b", a=S),
                                      WE[:, r_, WROW - D:WROW].unsqueeze(1).to_broadcast((P, S, D)), ALU.add)\
                       .then_inc(s_yc, 1)

                tile_in(0, 0)
                tile_in(0, 1)
                whole = (tiles - 2) // RING
                for c in range(1, RING + 1):
                    tile_in(0, c + 1)
                    tile_out(0, c - 1, chain)
                with dve.Fori(1, whole) as i:
                    chain.loop(i, RING * 4, 1)
                    for c in range(1, RING + 1):
                        tile_in(i, c + 1)
                        tile_out(i, c - 1, chain)
                    chain.ended(whole - 1)
                for c in range(RING * whole + 1, tiles + 1):
                    if c + 1 < tiles:
                        tile_in(0, c + 1)
                    tile_out(0, c - 1, chain)

                last = L == len(SUBLAYERS) - 1
                if last or not fused(L + 1):
                    with dve.Fori(0, NG // 2) as i:
                        chain.loop(i, 2 if last else 4)
                        for u in range(2):
                            combine(L, i, u, chain)
                            if not last:
                                dve.wait_ge(s_comb, i * 2 + (NG * f + u + 1))
                                chain(group_stats(i * (2 * GT) + GT * u))
                        chain.ended(NG // 2)

            def attention(L):
                rc, rs = cst("rope_c"), cst("rope_s")

                def norm(i, u):
                    if isinstance(i, int) and i == 0:
                        normalise(L, i, u)
                    else:
                        normalise(L, i, u, (s_tr, i * 2 + (NG * L + u - 1)))

                def rope(i, u):
                    n = i * 10 + 5 * u
                    if not (isinstance(i, int) and i == 0):
                        dve.wait_ge(s_lo, i * 2 + (u - 1))
                    for k, (b0, b1) in enumerate((("bq", "bqr"), ("bk", "bkr"))):
                        dve.wait_ge(s_proj, n + (2 * k + 1))
                        dve.scalar_tensor_tensor(out=QF[:, u, k, :], in0=bank(2 + 2 * k), scalar=wt(b0), in1=rc,
                                                 op0=ALU.add, op1=ALU.mult).then_inc(s_rope, 1)
                        dve.wait_ge(s_proj, n + (2 * k + 2))
                        if k == 0 and not (isinstance(i, int) and i == 0 and u == 0):
                            dve.wait_ge(s_rot, i * 2 + u)
                        dve.scalar_tensor_tensor(out=QT[:, k, :], in0=bank(3 + 2 * k), scalar=wt(b1), in1=rs,
                                                 op0=ALU.add, op1=ALU.mult).then_inc(s_rope, 1)
                    dve.wait_ge(s_proj, n + 5)
                    dve.tensor_tensor(VA[:, bass.ds(i * (2 * GT) + GT * u, GT), :, 0:HD],
                                      bank(6).rearrange("p (t h d) -> p t h d", t=GT, h=HEADS),
                                      wt("bv").rearrange("p (h d) -> p h d", h=HEADS).unsqueeze(1)
                                      .to_broadcast((P, GT, HEADS, HD)), ALU.add).then_inc(s_va, 1)

                def step(i, u, i2, u2):
                    arrive(L, i2, u2, chain)
                    rope(i, u)
                    scale(L, i2, u2, chain)
                    norm(i2, u2)

                last = NG // 2 - 1
                arrive(L, 0, 0, chain)
                scale(L, 0, 0, chain)
                norm(0, 0)
                chain(dve.memset(VA[:, :, :, HD:HD + 1], 1.0))
                step(0, 0, 0, 1)
                step(0, 1, 1, 0)
                with dve.Fori(1, last) as i:
                    chain.loop(i, 2 * front_steps(L), 1)
                    step(i, 0, i, 1)
                    step(i, 1, i + 1, 0)
                    chain.ended(last - 1)
                step(last, 0, last, 1)
                rope(last, 1)
                dve.wait_ge(s_va, NG)
                dve.memset(bank(6), 0.0).then_inc(s_va, 1)

                def iteration(i, par, peeled, steps):
                    has_m = not peeled or i + 1 < NG
                    for s in range(HEADS):
                        g, j = s // 4, s % 4
                        if j == 2 and (not peeled or 0 <= 4 * i + g - 2 < 4 * NG):
                            G = i * 4 + (g - 2)
                            gg = (g - 2) % 4
                            sums = bank(7).rearrange("p (a h r) -> p a h r", a=GT, h=4)
                            dve.wait_ge(s_tp, G + 1)
                            steps(dve.reciprocal(RD[:, :, :], sums[:, :, :, HD]))
                            if gg == 0 and not (peeled and 4 * i + g - 2 < 4):
                                dve.wait_ge(s_ap, i)
                            dve.tensor_tensor(AO.rearrange("p a (h d) -> p a h d", h=HEADS)[:, :, 4 * gg:4 * gg + 4, :],
                                              sums[:, :, :, 0:HD],
                                              RD.unsqueeze(3).to_broadcast((P, GT, 4, HD)), ALU.mult)\
                               .then_inc(s_td, 1)
                        if s == 12 and (not peeled or 0 <= i - 1 < NG):
                            dve.wait_ge(s_op, i)
                            xb = X[:, bass.ds(i * GT - GT, GT), :]
                            steps(dve.tensor_tensor(xb, bank(7).rearrange("p (a b) -> p a b", a=GT), xb, ALU.add))
                            dve.tensor_tensor(xb, xb, wt("bo").unsqueeze(1).to_broadcast((P, GT, D)), ALU.add)\
                               .then_inc(s_od, 1)
                            dve.wait_ge(s_od, i)
                            steps(group_stats(i * GT - GT))
                        if has_m:
                            for a in range(GT):
                                dve.wait_ge(s_m, i * 64 + (64 + 4 * s + a + 1))
                                dve.tensor_reduce(MX[:, s, a:a + 1], bank(4 + a % 2), AX_X, ALU.max)\
                                   .then_inc(s_mr, 1)
                            if j == 3:
                                mx = MX[:, 4 * g:4 * g + 4, :].rearrange("p a b -> p (a b)")
                                dve.wait_ge(s_mr, i * 64 + (64 + 4 * s + 4))
                                if not (peeled and i == -1 and g == 0):
                                    dve.wait_ge(s_nmp, i * 4 + 4 + g)
                                steps(dve.tensor_scalar(NMB[:, :], mx, -1.0, None, ALU.mult))
                                steps(dve.tensor_copy(NMF[:, 0, :], NMB[:, :]))
                                dve.scalar_tensor_tensor(out=NMF[:, 1, :], in0=mx, scalar=-1.0, in1=NMB[:, :],
                                                         op0=ALU.mult, op1=ALU.subtract).then_inc(s_nmf, 1)

                iteration(-1, 1, True, chain)
                iteration(0, 0, True, chain)
                with dve.Fori(0, (LOOP_HI - 1) // 2) as i:
                    chain.loop(i, 2 * (4 + 2 + 8))
                    iteration(i * 2 + 1, 1, False, chain)
                    iteration(i * 2 + 2, 0, False, chain)
                    chain.ended((LOOP_HI - 1) // 2)
                for i in range(LOOP_HI, NG + 1):
                    iteration(i, i % 2, True, chain)
                dve.wait_ge(s_od, NG)

            def linear(L):
                KVb = PS[:, 1024:2048].rearrange("p (a b) -> p a b", a=GT)

                def f1(i, u):
                    if isinstance(i, int) and i == 0:
                        normalise(L, i, u)
                    else:
                        normalise(L, i, u, (s_tr, i * 2 + (NG * L + u - 1)))

                def f2(i, u, steps):
                    n = i * 2 + (u + 1)
                    dve.wait_ge(s_lqe, n)
                    steps(dve.tensor_scalar(LQM[:, u], LQE[:, u], 1.0, None, ALU.min))
                    if not (isinstance(i, int) and i == 0):
                        dve.wait_ge(s_ln, n - 2)
                    dve.scalar_tensor_tensor(out=LQF[:, u], in0=bank(4), scalar=0.0, in1=LQM[:, u],
                                             op0=ALU.max, op1=ALU.add).then_inc(s_lqf, 1)

                def f3(i, u, steps):
                    n = i * 2 + (u + 1)
                    dve.wait_ge(s_lke, n)
                    steps(dve.tensor_scalar(LKM[:, u], LKE[:, u], 1.0, None, ALU.min))
                    dve.scalar_tensor_tensor(out=LKF[:, u], in0=KVb[:, :, 0:D], scalar=0.0, in1=LKM[:, u],
                                             op0=ALU.max, op1=ALU.add).then_inc(s_lkf, 1)

                def b1(i, u):
                    n = i * 2 + (u + 1)
                    dve.wait_ge(s_kv, n)
                    dve.tensor_tensor(BD[:, u, 0:D], bank(4, 0, D), cst("blockmask"), ALU.mult)
                    dve.tensor_scalar(BD[:, u, D:D + HEADS], cst("headmask"), bank(4, D, D + 1), None, ALU.mult)\
                       .then_inc(s_bd, 1)

                def b2(i, u, steps):
                    n = i * 2 + (u + 1)
                    num = PS[:, 2560:2560 + 256 * GT].rearrange("p (a b) -> p a b", a=GT)
                    dve.wait_ge(s_ln, n)
                    steps(dve.tensor_scalar(LDN[:, u], num[:, :, D:D + HEADS], 1e-6, None, ALU.add))
                    steps(dve.reciprocal(LRD[:, u], LDN[:, u]))
                    dve.tensor_tensor(LAO[:, u].rearrange("p a (h d) -> p a h d", h=HEADS),
                                      num[:, :, 0:D].rearrange("p a (h d) -> p a h d", h=HEADS),
                                      LRD[:, u].unsqueeze(3).to_broadcast((P, GT, HEADS, HD)), ALU.mult)\
                       .then_inc(s_lao, 1)

                def b4(i, u, steps):
                    n = i * 2 + (u + 1)
                    dve.wait_ge(s_lo2, n)
                    t0 = i * (2 * GT) + GT * u
                    xb = X[:, bass.ds(t0, GT), :]
                    dve.tensor_tensor(xb, bank(7).rearrange("p (a b) -> p a b", a=GT), xb, ALU.add)\
                       .then_inc(s_lres, 1)
                    dve.wait_ge(s_lres, n)
                    steps(group_stats(t0))

                def both(i, u, i2, u2, steps, more=True):
                    b1(i2, u2)
                    f2(i, u, steps)
                    b2(i2, u2, steps)
                    if more:
                        f1(i + u, 1 - u)
                    f3(i, u, steps)
                    b4(i2, u2, steps)

                f1(0, 0)
                f1(0, 1)
                chain(dve.memset(LV[:, :, :, D:D + 1], 1.0))
                f2(0, 0, chain)
                f3(0, 0, chain)
                both(0, 1, 0, 0, chain)
                with dve.Fori(1, NG // 2 - 1) as i:
                    chain.loop(i, 2 * (3 + 2), 1)
                    both(i, 0, i - 1, 1, chain)
                    both(i, 1, i, 0, chain)
                    chain.ended(NG // 2 - 2)
                i = NG // 2 - 1
                both(i, 0, i - 1, 1, chain)
                both(i, 1, i, 0, chain, False)
                b1(i, 1)
                b2(i, 1, chain)
                b4(i, 1, chain)

            dve.wait_ge(s_x[0], 16)
            dve.wait_ge(s_cst, 16)
            dve.wait_ge(s_wt, 16)
            dve.tensor_copy(before_bf[:, :], cst("before"))
            chain(dve.tensor_copy(ones_bf[:, :], cst("ones")))
            for L, kind in enumerate(SUBLAYERS):
                finish_stats(L)
                if kind in (FFN0, FFN1):
                    moe(L)
                elif kind == ATTN:
                    attention(L)
                else:
                    linear(L)


CLEARED = 16 * (E1 + SPARE // (S0 * P) + 1)
LOOP_HI = NG - 1
STORES = 16 * 3
FUSED = (ATTN, FFN1)
LOADS = 16 * (2 * PARTS + 1)


def kernel(**inputs):
    import concourse.bacc as _bacc
    from concourse import mybir as _mybir
    from concourse.bass_utils import run_bass_kernel_spmd as _run

    a = {k: np.asarray(v) for k, v in inputs.items()}
    turned = (np.arange(D) // HD) * HD + (np.arange(D) + HD // 2) % HD

    def column(v):
        return v.reshape(P, 1)

    def every(v, n=1):
        return np.broadcast_to(np.tile(v.reshape(1, -1), (1, n)), (P, v.size * n))

    by_dim = np.arange(D).reshape(HEADS, HD).T.reshape(-1)
    rotated = turned[by_dim]

    parts = {
        "wq": a["L0_attn_Wq"][by_dim].T, "wqr": a["L0_attn_Wq"][rotated].T,
        "wk": a["L0_attn_Wk"][by_dim].T, "wkr": a["L0_attn_Wk"][rotated].T,
        "wv": a["L0_attn_Wv"].T, "wo": a["L0_attn_Wo"].T,
        "lq": a["L1_attn_Wq"].T, "lkv": np.concatenate([a["L1_attn_Wk"].T, a["L1_attn_Wv"].T], 1),
        "lo": a["L1_attn_Wo"].T, "r0": a["L0_ffn_Wr"], "r1": a["L1_ffn_router_w"].T,
        "bq": column(a["L0_attn_bq"][by_dim]), "bqr": column(a["L0_attn_bq"][rotated]),
        "bk": column(a["L0_attn_bk"][by_dim]), "bkr": column(a["L0_attn_bk"][rotated]),
        "bv": every(a["L0_attn_bv"]), "bo": every(a["L0_attn_bo"]),
        "rb0": every(a["L0_ffn_br"], GT), "rb1": every(a["L1_ffn_router_b"], GT),
    }
    weights = np.ascontiguousarray(np.concatenate([parts[n] for n, _ in WEIGHTS], 1))

    def experts(w1, b1, w2, b2):
        e = w1.shape[0]
        return np.ascontiguousarray(np.concatenate([
            w1,
            w2.reshape(e, FC, P, D).transpose(0, 2, 1, 3).reshape(e, P, FC * D),
            b1.reshape(e, FC, P).transpose(0, 2, 1),
            np.broadcast_to(b2[:, None, :], (e, P, D))], 2))

    arrays = {
        "x": np.ascontiguousarray(a["L0_attn_x"].reshape(TOKENS, D)),
        "constants": constants(),
        "weights": weights,
        "experts0": experts(a["L0_ffn_W1"], a["L0_ffn_b1"], a["L0_ffn_W2"], a["L0_ffn_b2"]),
        "experts1": experts(a["L1_ffn_w1"], a["L1_ffn_b1"], a["L1_ffn_w2"], a["L1_ffn_b2"]),
    }
    nc = _bacc.Bacc("TRN2", target_bir_lowering=False, num_devices=1)
    args = [nc.dram_tensor(n, v.shape, _mybir.dt.from_np(v.dtype), kind="ExternalInput").ap()
            for n, v in arrays.items()]
    out = nc.dram_tensor("out", (TOKENS, D), F32, kind="ExternalOutput").ap()
    build(nc, *args, out)
    r = _run(nc, [arrays], core_ids=[0])
    return r.results[0]["out"].reshape(BATCHES, SEQ, D)
```
